# Optimizing a Trainium2 kernel written in Bass

```python
import numpy as np
import jax
import jax.numpy as jnp

def _softmax(x, axis=-1):
    return jax.nn.softmax(x, axis=axis)

def _gelu(x):
    return jax.nn.gelu(x, approximate=True)

def _silu(x):
    return jax.nn.silu(x)

def _sigmoid(x):
    return jax.nn.sigmoid(x)

def _layernorm(x, axis=-1, eps=1e-05):
    m = jnp.mean(x, axis=axis, keepdims=True)
    v = jnp.var(x, axis=axis, keepdims=True)
    return (x - m) / jnp.sqrt(v + eps)

def _scatter_add(tgt, idx, src, axis=0):
    return tgt.at[idx].add(src)

def _segment_sum(src, seg, n):
    return jax.ops.segment_sum(src, seg, n)
kernel_name = 'mk_lm_tower_d1_tok_ids2048_r4_06c1e6'

def setup_inputs(seed: int=0):
    np.random.seed(seed)
    _w = jnp.asarray

    def _rec_inputs():
        import jax
        import jax.numpy as jnp
        _rk = jax.random.key(seed)
        x = jax.random.randint(jax.random.fold_in(_rk, 1), (16, 512), 0, 127990, jnp.int32)
        return x
    x = _rec_inputs()

    def _L0_tok_setup():
        import jax, jax.numpy as jnp
        import numpy as np
        VOCAB = 32000
        EMBED = 512
        N_TRAIN = 64
        BATCH, SEQ = (4, 1024)
        key = jax.random.key(seed)
        k1, k2, k3, k4 = jax.random.split(key, 4)
        x = jax.random.randint(k1, (BATCH, SEQ), 0, VOCAB, dtype=jnp.int64 if jax.config.jax_enable_x64 else jnp.int32)
        W = jax.random.normal(k2, (VOCAB, EMBED), dtype=jnp.float32)
        delta_values = jax.random.normal(k3, (N_TRAIN * EMBED,), dtype=jnp.float32)
        token_indices = jnp.sort(jax.random.randint(k4, (N_TRAIN,), 0, VOCAB, dtype=jnp.int32))
        return {'x': x, 'W': W, 'delta_values': delta_values, 'token_indices': token_indices}
    _L0_tok_all = _L0_tok_setup()
    _L0_tok_in = {k: v for k, v in _L0_tok_all.items() if k in ('W', 'delta_values', 'token_indices')}
    del _L0_tok_all

    def _L0_attn_setup():
        import jax, jax.numpy as jnp
        import numpy as np
        import math
        HIDDEN = 512
        NUM_HEADS = 16
        NUM_KV_HEADS = 8
        HEAD_DIM = HIDDEN // NUM_HEADS
        ROPE_THETA = 1000000.0
        SPARSITY_RATIO = 0.5
        VISION_SPARSITY_RATIO = 0.4
        BATCH = 2
        SEQ = 512

        def rotate_half(x):
            h = x.shape[-1] // 2
            return jnp.concatenate([-x[..., h:], x[..., :h]], axis=-1)
        key = jax.random.key(seed)
        ks = jax.random.split(key, 12)
        s = 1.0 / math.sqrt(HIDDEN)
        return {'hidden_states': jax.random.normal(ks[0], (BATCH, SEQ, HIDDEN), jnp.float32), 'Wq': jax.random.normal(ks[1], (HIDDEN, NUM_HEADS * HEAD_DIM), jnp.float32) * s, 'bq': jax.random.normal(ks[2], (NUM_HEADS * HEAD_DIM,), jnp.float32) * 0.01, 'Wk': jax.random.normal(ks[3], (HIDDEN, NUM_KV_HEADS * HEAD_DIM), jnp.float32) * s, 'bk': jax.random.normal(ks[4], (NUM_KV_HEADS * HEAD_DIM,), jnp.float32) * 0.01, 'Wv': jax.random.normal(ks[5], (HIDDEN, NUM_KV_HEADS * HEAD_DIM), jnp.float32) * s, 'bv': jax.random.normal(ks[6], (NUM_KV_HEADS * HEAD_DIM,), jnp.float32) * 0.01, 'Wo': jax.random.normal(ks[7], (NUM_HEADS * HEAD_DIM, HIDDEN), jnp.float32) * s, 'bo': jax.random.normal(ks[8], (HIDDEN,), jnp.float32) * 0.01, 'Wr': jax.random.normal(ks[9], (HIDDEN, NUM_HEADS), jnp.float32) * s, 'br': jax.random.normal(ks[10], (NUM_HEADS,), jnp.float32) * 0.01}
    _L0_attn_all = _L0_attn_setup()
    _L0_attn_in = {k: v for k, v in _L0_attn_all.items() if k in ('Wq', 'bq', 'Wk', 'bk', 'Wv', 'bv', 'Wo', 'bo', 'Wr', 'br')}
    del _L0_attn_all

    def _L0_ffn_setup():
        import jax, jax.numpy as jnp
        import numpy as np
        L, N, E, H, K = (512, 8, 512, 2048, 8)
        key = jax.random.key(seed)
        ks = jax.random.split(key, 6)
        return {'x': jax.random.normal(ks[0], (L, N, E), dtype=jnp.float32), 'proj1': jax.random.normal(ks[1], (H, E), dtype=jnp.float32) * 0.02, 'proj1_bias': jax.random.normal(ks[2], (H,), dtype=jnp.float32) * 0.02, 'proj2': jax.random.normal(ks[3], (E, H), dtype=jnp.float32) * 0.02, 'proj2_bias': jax.random.normal(ks[4], (E,), dtype=jnp.float32) * 0.02, 'gate_w': jax.random.normal(ks[5], (E, K), dtype=jnp.float32)}
    _L0_ffn_all = _L0_ffn_setup()
    _L0_ffn_in = {k: v for k, v in _L0_ffn_all.items() if k in ('proj1', 'proj1_bias', 'proj2', 'proj2_bias', 'gate_w')}
    del _L0_ffn_all
    return {'x': x, 'L0_tok_W': _L0_tok_in['W'], 'L0_tok_delta_values': _L0_tok_in['delta_values'], 'L0_tok_token_indices': _L0_tok_in['token_indices'], 'L0_attn_Wq': _L0_attn_in['Wq'], 'L0_attn_bq': _L0_attn_in['bq'], 'L0_attn_Wk': _L0_attn_in['Wk'], 'L0_attn_bk': _L0_attn_in['bk'], 'L0_attn_Wv': _L0_attn_in['Wv'], 'L0_attn_bv': _L0_attn_in['bv'], 'L0_attn_Wo': _L0_attn_in['Wo'], 'L0_attn_bo': _L0_attn_in['bo'], 'L0_attn_Wr': _L0_attn_in['Wr'], 'L0_attn_br': _L0_attn_in['br'], 'L0_ffn_proj1': _L0_ffn_in['proj1'], 'L0_ffn_proj1_bias': _L0_ffn_in['proj1_bias'], 'L0_ffn_proj2': _L0_ffn_in['proj2'], 'L0_ffn_proj2_bias': _L0_ffn_in['proj2_bias'], 'L0_ffn_gate_w': _L0_ffn_in['gate_w']}

def reference(x, L0_tok_W, L0_tok_delta_values, L0_tok_token_indices, L0_attn_Wq, L0_attn_bq, L0_attn_Wk, L0_attn_bk, L0_attn_Wv, L0_attn_bv, L0_attn_Wo, L0_attn_bo, L0_attn_Wr, L0_attn_br, L0_ffn_proj1, L0_ffn_proj1_bias, L0_ffn_proj2, L0_ffn_proj2_bias, L0_ffn_gate_w):
    import jax
    import jax.numpy as jnp

    def _L0_tok_ref(x, W, delta_values, token_indices):
        import jax, jax.numpy as jnp
        import numpy as np
        VOCAB = 32000
        EMBED = 512
        N_TRAIN = 64
        BATCH, SEQ = (4, 1024)
        delta = delta_values.reshape(EMBED, N_TRAIN).T
        W_eff = W.at[token_indices].add(delta)
        return W_eff[x]

    def _L0_attn_ref(hidden_states, Wq, bq, Wk, bk, Wv, bv, Wo, bo, Wr, br):
        import jax, jax.numpy as jnp
        import numpy as np
        import math
        HIDDEN = 512
        NUM_HEADS = 16
        NUM_KV_HEADS = 8
        HEAD_DIM = HIDDEN // NUM_HEADS
        ROPE_THETA = 1000000.0
        SPARSITY_RATIO = 0.5
        VISION_SPARSITY_RATIO = 0.4
        BATCH = 2
        SEQ = 512

        def rotate_half(x):
            h = x.shape[-1] // 2
            return jnp.concatenate([-x[..., h:], x[..., :h]], axis=-1)
        bsz, q_len, _ = hidden_states.shape
        q = (hidden_states @ Wq + bq).reshape(bsz, q_len, NUM_HEADS, HEAD_DIM).transpose(0, 2, 1, 3)
        k = (hidden_states @ Wk + bk).reshape(bsz, q_len, NUM_KV_HEADS, HEAD_DIM).transpose(0, 2, 1, 3)
        v = (hidden_states @ Wv + bv).reshape(bsz, q_len, NUM_KV_HEADS, HEAD_DIM).transpose(0, 2, 1, 3)
        pos = jnp.arange(q_len, dtype=jnp.float32)
        inv_freq = 1.0 / ROPE_THETA ** (jnp.arange(0, HEAD_DIM, 2, dtype=jnp.float32) / HEAD_DIM)
        freqs = pos[:, None] * inv_freq[None, :]
        emb = jnp.concatenate([freqs, freqs], axis=-1)
        cos = jnp.cos(emb)[None, None, :, :]
        sin = jnp.sin(emb)[None, None, :, :]
        q = q * cos + rotate_half(q) * sin
        k = k * cos + rotate_half(k) * sin
        n_rep = NUM_HEADS // NUM_KV_HEADS
        k = jnp.repeat(k, n_rep, axis=1)
        v = jnp.repeat(v, n_rep, axis=1)
        routing = jax.nn.sigmoid(hidden_states @ Wr + br).transpose(0, 2, 1)
        ratio = VISION_SPARSITY_RATIO if q_len > 128 else SPARSITY_RATIO
        topk = max(1, min(int(q_len * ratio), q_len))
        _, idx = jax.lax.top_k(routing, topk)
        mask = jax.vmap(jax.vmap(lambda i: jnp.zeros((q_len,), bool).at[i].set(True)))(idx)
        scores = jnp.einsum('bhqd,bhkd->bhqk', q, k) / math.sqrt(HEAD_DIM)
        sparse = jnp.where(mask[:, :, None, :], scores, -jnp.inf)
        probs = jax.nn.softmax(sparse.astype(jnp.float32), axis=-1).astype(q.dtype)
        out = jnp.einsum('bhqk,bhkd->bhqd', probs, v)
        out = out.transpose(0, 2, 1, 3).reshape(bsz, q_len, NUM_HEADS * HEAD_DIM)
        return out @ Wo + bo

    def _L0_ffn_ref(x, proj1, proj1_bias, proj2, proj2_bias, gate_w):
        import jax, jax.numpy as jnp
        import numpy as np
        L, N, E, H, K = (512, 8, 512, 2048, 8)
        dst = jnp.argmax(jnp.einsum('lne,ek->lnk', x, gate_w), axis=-1)
        h = jax.nn.gelu(jnp.einsum('lne,he->lnh', x, proj1) + proj1_bias, approximate=False)
        out = jnp.einsum('lnh,eh->lne', h, proj2) + proj2_bias
        del dst
        return out
    h = _L0_tok_ref(x, L0_tok_W, L0_tok_delta_values, L0_tok_token_indices)
    h = h + _L0_attn_ref(_layernorm(h, axis=-1), L0_attn_Wq, L0_attn_bq, L0_attn_Wk, L0_attn_bk, L0_attn_Wv, L0_attn_bv, L0_attn_Wo, L0_attn_bo, L0_attn_Wr, L0_attn_br)
    h = h + _L0_ffn_ref(_layernorm(h, axis=-1), L0_ffn_proj1, L0_ffn_proj1_bias, L0_ffn_proj2, L0_ffn_proj2_bias, L0_ffn_gate_w)
    return h

_drawn_inputs = setup_inputs


def setup_inputs(seed=0):
    import zlib

    import numpy as np

    out = dict(_drawn_inputs(seed))
    spreads = {}
    factors = {'L0_tok_delta_values': 3.21,
     'L0_attn_bq': 32.691,
     'L0_attn_bk': 64.0,
     'L0_attn_bv': 5.715,
     'L0_attn_bo': 6.513,
     'L0_ffn_proj1_bias': 5.832,
     'L0_ffn_proj2_bias': 3.252}
    for name, (base, spread) in spreads.items():
        noise = np.random.default_rng([zlib.crc32(name.encode()), seed]).standard_normal(out[name].shape)
        drawn = base * np.exp(spread * noise) if base else spread * noise
        out[name] = jnp.asarray(drawn.astype(out[name].dtype))
    for name, factor in factors.items():
        out[name] = (out[name] * factor).astype(out[name].dtype)
    return out
```

```python
from contextlib import ExitStack

import numpy as np

import concourse.bass as bass
from concourse import mybir

F32 = mybir.dt.float32
F32R = mybir.dt.float32r
I32 = mybir.dt.int32
ALU = mybir.AluOpType
ACT = mybir.ActivationFunctionType
AX = mybir.AxisListType

P = 128
B, S, D = 16, 512, 512
V = 32000
NTRAIN = 64
T = S // P
C = D // P
NH, NKV, HD = 16, 8, 32
KEEP = int(S * 0.4)
HALF = KEEP // 2
QKV = (NH + 2 * NKV) * HD
ROPE = (NH + NKV) * HD
SCALE = float(HD) ** -0.5
H = 2048
HC = H // P
EPS = 1e-5
GROUP = P // NH
NG = B // GROUP


class Event:

    def __init__(self, ctx, nc, name, per, base=0):
        self.sem, self.per, self.base = ctx.enter_context(nc.semaphore(name)), per, base

    def start(self, eng):
        if self.base:
            eng.sem_inc(self.sem, self.base)

    def wait(self, eng, i, n):
        assert n + self.base >= 1, "a wait that might be against zero"
        eng.wait_ge(self.sem, i * self.per + (n + self.base))


def product(pe, out, lhs, rhs, first, last):
    pe.matmul(out, lhs[0], rhs[0], start=first, stop=False, skip_group_check=True)
    pe.matmul(out, lhs[0], rhs[1], start=False, stop=False, skip_group_check=True)
    return pe.matmul(out, lhs[1], rhs[0], start=False, stop=last, skip_group_check=True)


def identity(pool, ident, set_ready):
    pool.memset(ident[:], 0.0).then_inc(set_ready.sem, 1)
    pool.wait_ge(set_ready.sem, 1)
    pool.affine_select(out=ident[:], in_=ident[:], compare_op=ALU.not_equal, fill=1.0,
                       base=0, pattern=[[-1, P]], channel_multiplier=1).then_inc(set_ready.sem, 1)


def embed_phase(nc, keep, a, scr):
    with ExitStack() as ctx:
        sb = lambda name, shape, dt=F32: ctx.enter_context(nc.sbuf_tensor(name, shape, dt))
        ev = lambda name, per=1, base=0: Event(ctx, nc, name, per, base)
        ids_i = sb("ids_i", [B * T, P], I32)
        ids_f = sb("ids_f", [B * T, P])
        ids_neg = sb("ids_neg", [B * T, P])
        id_col = sb("id_col", [P, B * T], I32)
        ids_now = sb("ids_now", [P, T], I32)
        trained_i = sb("trained_i", [P, 1], I32)
        trained = sb("trained", [P, 1])
        trained_neg = sb("trained_neg", [P, 1])
        delta_raw = sb("delta_raw", [P, D])
        delta_hi = sb("delta_hi", [P, D])
        delta = sb("delta", [P, D], F32R)
        id_row = sb("id_row", [P, S])
        onehot = sb("onehot", [P, S], F32R)
        rows = sb("rows", [P, T, D])
        h = sb("h0", [P, T, D])
        stats = sb("stats", [P, T, 6])
        mean_var = sb("mean_var", [P, T, 2])
        exponent = sb("exponent", [P, T])
        rstd = sb("rstd_now", [P, T])
        xn = sb("xn0", [P, 2, D])
        xT_hi = sb("xT_hi0", [P, C, S], F32R)
        xT_lo = sb("xT_lo0", [P, C, S], F32R)
        route = sb("route", [NH, S])
        br = sb("br", [NH, 1])
        wqkv_raw = sb("wqkv_raw", [P, C, QKV])
        wo_raw = sb("wo_raw", [P, C, D])
        wr_raw = sb("wr_raw", [P, C, NH])
        wr = [sb("wr_hi", [P, C, NH], F32R), sb("wr_lo", [P, C, NH], F32R)]
        ps_delta = [ctx.enter_context(nc.psum_tensor(f"ps_delta{n}", [P, D], F32)) for n in range(2)]
        ps_xT = [ctx.enter_context(nc.psum_tensor(f"ps_xT0{n}", [P, C, P], F32)) for n in range(2)]
        ps_route = ctx.enter_context(nc.psum_tensor("ps_route", [NH, S], F32))
        ps_ids = ctx.enter_context(nc.psum_tensor("ps_ids", [P, B * T], F32))

        passed = ev("passed")
        small_in = ev("small_in")
        weights_in = ev("weights_in")
        cols_in = ev("cols_in")
        made = ev("made")
        ids_ready = ev("ids_ready")
        ids_turned = ev("ids_turned")
        ids_stored = ev("ids_stored")
        id_col_ready = ev("id_col_ready")
        const_ready = ev("const_ready")
        w_hi_ready = ev("w_hi_ready")
        w_lo_ready = ev("w_lo_ready")
        row_in = ev("row_in", 16)
        onehot_ready = ev("onehot_ready", 1, 1)
        delta_ready = ev("delta_ready", T)
        ids_now_ready = ev("ids_now_ready", 1)
        gathered = [ev(f"gathered{t}", 16) for t in range(T)]
        h_ready = ev("h_ready", T, T)
        stats_ready = ev("stats_ready", T)
        var_ready = ev("var_ready", T)
        rstd_ready = ev("rstd_ready", 1)
        stats_kept = ev("stats_kept", 1, 1)
        h_stored = ev("h_stored", 16, 16)
        xn_ready = ev("xn_ready", T)
        xT_ready = ev("xT_ready", T, 2)
        hi_ready = ev("hi_ready", T)
        lo_ready = ev("lo_ready", T, 2)
        route_ready = ev("route_ready", 1, 1)
        score_ready = ev("score_ready", 1, 1)
        score_stored = ev("score_stored", 16, 16)

        with nc.Block() as block:
            @block.sync
            def _(sp):
                h_stored.start(sp)
                score_stored.start(sp)
                sp.dma_start(ids_i[:], a["x"]).then_inc(small_in.sem, 16)
                for half in range(2):
                    at = slice(NTRAIN * half, NTRAIN * (half + 1))
                    sp.dma_start(trained_i[at, :], a["token_indices"]).then_inc(small_in.sem, 16)
                    sp.dma_start(delta_raw[at, :], a["delta"]).then_inc(small_in.sem, 16)
                sp.dma_start(br[:], a["br"]).then_inc(small_in.sem, 16)
                sp.dma_start(wr_raw[:], a["Wr"].rearrange("(c p) n -> p c n", p=P)).then_inc(small_in.sem, 16)
                ids_ready.wait(sp, 0, 1)
                sp.dma_start(scr["ids"].rearrange("(t p) -> t p", p=P), ids_f[:]).then_inc(ids_stored.sem, 16)
                for n, (w, k) in enumerate((("Wq", NH), ("Wk", NKV), ("Wv", NKV))):
                    at = (0, NH * HD, ROPE)[n]
                    sp.dma_start(wqkv_raw[:, :, at:at + k * HD],
                                 a[w].rearrange("(c p) n -> p c n", p=P)).then_inc(weights_in.sem, 16)
                sp.dma_start(wo_raw[:], a["Wo"].rearrange("(c p) n -> p c n", p=P)).then_inc(weights_in.sem, 16)
                for n, (w, k) in enumerate((("bq", NH), ("bk", NKV), ("bv", NKV))):
                    at = (0, NH * HD, ROPE)[n]
                    sp.dma_start(keep["bqkv"][:, at:at + k * HD],
                                 a[w].to_broadcast([P, k * HD])).then_inc(weights_in.sem, 16)
                sp.dma_start(keep["bo"][:], a["bo"].to_broadcast([P, D])).then_inc(weights_in.sem, 16)
                sp.dma_start(keep["cos"][:], a["cos"].rearrange("(t p) k n -> p t k n", p=P)).then_inc(weights_in.sem, 16)
                sp.dma_start(keep["sin"][:], a["sin"].rearrange("(t p) k n -> p t k n", p=P)).then_inc(weights_in.sem, 16)
                sp.wait_ge(ids_stored.sem, 16)
                with sp.Fori(0, B) as i:
                    onehot_ready.wait(sp, i, 0)
                    sp.dma_start(id_row[:], scr["ids2"][bass.ds(i, 1), :].to_broadcast([P, S])).then_inc(row_in.sem, 16)
                    h_ready.wait(sp, i, T)
                    sp.dma_start(scr["h"][bass.ds(i, 1)].rearrange("o (t p) d -> p (o t) d", p=P),
                                 h[:]).then_inc(h_stored.sem, 16)
                    score_ready.wait(sp, i, 1)
                    sp.dma_start(scr["route"][bass.ds(i, 1)].rearrange("o h s -> (o h) s"),
                                 route[:]).then_inc(score_stored.sem, 16)
                sp.wait_ge(h_stored.sem, 16 * (B + 1))
                sp.wait_ge(score_stored.sem, 16 * (B + 1))
                sp.wait_ge(weights_in.sem, 16 * 10)

            @block.gpsimd
            def _(pool):
                stats_kept.start(pool)
                pool.memset(keep["ident"][:], 0.0).then_inc(const_ready.sem, 1)
                pool.memset(exponent[:], -0.5).then_inc(const_ready.sem, 1)
                pool.iota(keep["iota"][:], [[1, KEEP]], base=0, channel_multiplier=0,
                          allow_small_or_imprecise_dtypes=True).then_inc(const_ready.sem, 1)
                pool.wait_ge(const_ready.sem, 3)
                pool.affine_select(out=keep["ident"][:], in_=keep["ident"][:], compare_op=ALU.not_equal, fill=1.0,
                                   base=0, pattern=[[-1, P]], channel_multiplier=1).then_inc(const_ready.sem, 1)
                id_col_ready.wait(pool, 0, 1)
                with pool.Fori(0, B) as i:
                    for t in range(T):
                        h_ready.wait(pool, i, t + 1 - T)
                    pool.tensor_copy(ids_now[:], id_col[:, bass.ds(i * T, T)]).then_inc(ids_now_ready.sem, 1)
                    ids_now_ready.wait(pool, i, 1)
                    pool.sem_inc(passed.sem)
                    for t in range(T):
                        pool.indirect_dma_start(out=rows[:, t, :], out_offset=None, in_=a["W"],
                                                in_offset=bass.IndirectOffsetOnAxis(ap=ids_now[:, t:t + 1], axis=0)
                                                ).then_inc(gathered[t].sem, 16)
                    var_ready.wait(pool, i, T)
                    pool.tensor_tensor(rstd[:], mean_var[:, :, 1], exponent[:], ALU.pow).then_inc(rstd_ready.sem, 1)
                    rstd_ready.wait(pool, i, 1)
                    pool.tensor_copy(keep["rstd"][:, bass.ds(i * T, T)], rstd[:])
                    pool.tensor_copy(keep["mean"][:, bass.ds(i * T, T)], mean_var[:, :, 0]).then_inc(stats_kept.sem, 1)

            @block.vector
            def _(dve):
                steps = [0]

                def done(instruction):
                    steps[0] += 1
                    instruction.then_inc(made.sem, 1)
                    dve.wait_ge(made.sem, steps[0])

                onehot_ready.start(dve)
                h_ready.start(dve)
                lo_ready.start(dve)
                dve.wait_ge(small_in.sem, 16 * 7)
                for src, neg, out in ((ids_i, ids_neg, ids_f), (trained_i, trained_neg, trained)):
                    done(dve.tensor_copy(out[:], src[:]))
                    done(dve.tensor_scalar(neg[:], out[:], 0.0, float(V), ALU.is_lt, ALU.mult))
                    done(dve.tensor_tensor(out[:], out[:], neg[:], ALU.add))
                dve.tensor_scalar(ids_f[:], ids_f[:], 0.0, float(V - 1), ALU.max, ALU.min).then_inc(ids_ready.sem, 1)
                done(dve.tensor_copy(delta_hi[:].bitcast(F32R), delta_raw[:]))
                dve.tensor_copy(delta[0:NTRAIN, :], delta_hi[0:NTRAIN, :])
                done(dve.tensor_tensor(delta[NTRAIN:P, :], delta_raw[NTRAIN:P, :], delta_hi[NTRAIN:P, :], ALU.subtract))
                done(dve.tensor_copy(wr[0][:], wr_raw[:]))
                done(dve.tensor_tensor(wr[1][:], wr_raw[:], wr[0][:].bitcast(F32), ALU.subtract))
                dve.wait_ge(ids_turned.sem, 1)
                dve.tensor_copy(id_col[:], ps_ids[:]).then_inc(id_col_ready.sem, 1)
                dve.wait_ge(weights_in.sem, 16 * 10)
                for n, (raw, hi, lo) in enumerate(((wqkv_raw, *keep["wqkv"]), (wo_raw, *keep["wo"]))):
                    dve.wait_ge(w_hi_ready.sem, n + 1)
                    dve.tensor_tensor(lo[:], raw[:], hi[:].bitcast(F32), ALU.subtract).then_inc(w_lo_ready.sem, 1)
                with dve.Fori(0, B) as i:
                    row_in.wait(dve, i, 16)
                    dve.tensor_scalar(onehot[:], id_row[:], trained[:, 0:1], None,
                                      ALU.is_equal).then_inc(onehot_ready.sem, 1)
                    h_stored.wait(dve, i, 0)
                    for t in range(T):
                        gathered[t].wait(dve, i, 16)
                        delta_ready.wait(dve, i, t + 1)
                        dve.tensor_tensor(h[:, t, :], rows[:, t, :], ps_delta[t % 2][:], ALU.add).then_inc(h_ready.sem, 1)
                    for t in range(T):
                        h_ready.wait(dve, i, t + 1)
                        dve.bn_stats(stats[:, t, :], h[:, t, :]).then_inc(stats_ready.sem, 1)
                    stats_kept.wait(dve, i, 0)
                    for t in range(T):
                        stats_ready.wait(dve, i, t + 1)
                        dve.sem_inc(passed.sem)
                        dve.bn_aggr(mean_var[:, t, :], stats[:, t, :]).then_inc(var_ready.sem, 1)
                    rstd_ready.wait(dve, i, 1)

                    def low(t):
                        hi_ready.wait(dve, i, t + 1)
                        at = slice(P * t, P * (t + 1))
                        dve.tensor_tensor(xT_lo[:, :, at], ps_xT[t % 2][:], xT_hi[:, :, at].bitcast(F32),
                                          ALU.subtract).then_inc(lo_ready.sem, 1)

                    for t in range(T):
                        xT_ready.wait(dve, i, t + 1 - 2)
                        dve.tensor_scalar(xn[:, t % 2, :], h[:, t, :], mean_var[:, t, 0:1], rstd[:, t:t + 1],
                                          ALU.subtract, ALU.mult).then_inc(xn_ready.sem, 1)
                        if t == 0:
                            route_ready.wait(dve, i, 0)
                        if t:
                            low(t - 1)
                    low(T - 1)

            @block.scalar
            def _(act):
                score_ready.start(act)
                act.wait_ge(weights_in.sem, 16 * 10)
                act.activation(keep["wqkv"][0][:], wqkv_raw[:], ACT.Copy).then_inc(w_hi_ready.sem, 1)
                act.activation(keep["wo"][0][:], wo_raw[:], ACT.Copy).then_inc(w_hi_ready.sem, 1)
                act.wait_ge(small_in.sem, 16 * 7)
                with act.Fori(0, B) as i:
                    route_ready.wait(act, i, 0)
                    for t in range(T):
                        xT_ready.wait(act, i, t + 1)
                        act.activation(xT_hi[:, :, P * t:P * (t + 1)], ps_xT[t % 2][:],
                                       ACT.Copy).then_inc(hi_ready.sem, 1)
                    route_ready.wait(act, i, 1)
                    score_stored.wait(act, i, 0)
                    act.activation(route[:], ps_route[:], ACT.Sigmoid, bias=br[:, 0:1]).then_inc(score_ready.sem, 1)

            @block.tensor
            def _(pe):
                xT_ready.start(pe)
                route_ready.start(pe)
                pe.wait_ge(const_ready.sem, 4)
                ids_ready.wait(pe, 0, 1)
                pe.transpose(ps_ids[:], ids_f[:], keep["ident"][0:B * T, 0:B * T]).then_inc(ids_turned.sem, 1)
                pe.wait_ge(made.sem, 6 + 4)
                with pe.Fori(0, B) as i:
                    onehot_ready.wait(pe, i, 1)
                    for t in range(T):
                        h_ready.wait(pe, i, t + 1 - 2)
                        pe.matmul(ps_delta[t % 2][:], onehot[:, P * t:P * (t + 1)], delta[:],
                                  start=True, stop=True).then_inc(delta_ready.sem, 1)
                    for t in range(T):
                        xn_ready.wait(pe, i, t + 1)
                        lo_ready.wait(pe, i, t + 1 - 2)
                        for c in range(C):
                            last = pe.transpose(ps_xT[t % 2][:, c, :], xn[:, t % 2, P * c:P * (c + 1)],
                                                keep["ident"][:])
                        last.then_inc(xT_ready.sem, 1)
                    lo_ready.wait(pe, i, T)
                    score_ready.wait(pe, i, 0)
                    for c in range(C):
                        last = product(pe, ps_route[:], [w[:, c, :] for w in wr], (xT_hi[:, c, :], xT_lo[:, c, :]),
                                       c == 0, c == C - 1)
                    last.then_inc(route_ready.sem, 1)


def choose_phase(nc, keep, scr):
    with ExitStack() as ctx:
        sb = lambda name, shape, dt=F32: ctx.enter_context(nc.sbuf_tensor(name, shape, dt))
        ev = lambda name, per=1, base=0: Event(ctx, nc, name, per, base)
        ROUNDS = -(-KEEP // 8)
        REST = KEEP - 8 * (ROUNDS - 1)
        TAKEN, BEYOND = -1.0, 2.0
        score = sb("score", [P, NG, S + 8])
        best = sb("best", [P, 8])
        one = sb("one", [P, S])
        chosen = sb("chosen", [P, NG, S])
        count = sb("count", [P, NG, S])
        ps_pos = [ctx.enter_context(nc.psum_tensor(f"ps_pos{g}", [P, T, P], F32)) for g in range(NG)]
        scores_in = ev("scores_in")
        made = ev("made2")
        place_ready = ev("place_ready")
        turned = ev("turned")
        with nc.Block() as block:
            @block.sync
            def _(sp):
                sp.dma_start(score[:, :, 0:S], scr["route"].rearrange("(g b) h s -> (b h) g s", g=NG)
                             ).then_inc(scores_in.sem, 16)

            @block.vector
            def _(dve):
                steps = [0]

                def done(instruction):
                    steps[0] += 1
                    instruction.then_inc(made.sem, 1)
                    dve.wait_ge(made.sem, steps[0])

                dve.memset(score[:, :, S:S + 8], BEYOND)
                done(dve.memset(one[:], 1.0))
                dve.wait_ge(scores_in.sem, 16)
                for g in range(NG):
                    for r in range(ROUNDS):
                        width = S if r < ROUNDS - 1 else S + 8 - REST
                        done(dve.max(best[:], score[:, g, 0:S]))
                        if width > S:
                            done(dve.memset(best[:, REST:8], BEYOND))
                        done(dve.match_replace(score[:, g, 0:width], best[:], score[:, g, 0:width], TAKEN))
                    done(dve.tensor_scalar(chosen[:, g, :], score[:, g, 0:S], 0.0, None, ALU.is_lt))
                    done(dve.tensor_tensor_scan(count[:, g, :], one[:], chosen[:, g, :], 0.0, ALU.mult, ALU.add))
                    dve.tensor_tensor(count[:, g, :], count[:, g, :], chosen[:, g, :],
                                      ALU.mult).then_inc(place_ready.sem, 1)
                for g in range(NG):
                    dve.wait_ge(turned.sem, g + 1)
                    dve.tensor_scalar(keep["pos"][:, :, P * g:P * (g + 1)], ps_pos[g][:], 1.0, None,
                                      ALU.subtract)

            @block.tensor
            def _(pe):
                for g in range(NG):
                    pe.wait_ge(place_ready.sem, g + 1)
                    for t in range(T):
                        last = pe.transpose(ps_pos[g][:, t, :], count[:, g, P * t:P * (t + 1)], keep["ident"][:])
                    last.then_inc(turned.sem, 1)


def attend_phase(nc, keep, scr):
    with ExitStack() as ctx:
        sb = lambda name, shape, dt=F32: ctx.enter_context(nc.sbuf_tensor(name, shape, dt))
        ps = lambda name: ctx.enter_context(nc.psum_tensor(name, [P, 512], F32))
        ev = lambda name, per=1, base=0: Event(ctx, nc, name, per, base)
        ident, wqkv, wo = keep["ident"], keep["wqkv"], keep["wo"]
        NP = NH // 2
        NQ = NH // 4
        h = sb("h_a", [P, T, D])
        hb = sb("hb_a", [P, T, D])
        h2 = sb("h2_a", [P, T, D])
        xn = sb("xn_a", [P, 2, D])
        xT = [sb("xT_hi_a", [P, C, S], F32R), sb("xT_lo_a", [P, C, S], F32R)]
        x = sb("x_a", [P, 2, QKV])
        turn1 = sb("turn1", [P, 2, ROPE])
        turn2 = sb("turn2", [P, 2, ROPE])
        q = sb("q_a", [P, T, NH * HD])
        kv = sb("kv_a", [P, T, NKV, 2, 2, HD], F32R)
        sel = sb("sel", [P, T, 2, KEEP], F32R)
        kT = sb("kT", [P, 2, 2 * KEEP], F32R)
        vT = sb("vT", [P, 2, 2 * KEEP])
        v = [sb(f"v{n}", [HALF, 2, 2, P], F32R) for n in range(4)]
        q4 = sb("q4", [P, 2, T, 4, HD])
        qT = sb("qT", [P, 2, S], F32R)
        prob = sb("prob", [P, 2, T, KEEP])
        pT = [sb("pT_hi", [HALF, 2, S], F32R), sb("pT_lo", [HALF, 2, S], F32R)]
        nmax = sb("nmax", [P, 2, T])
        total = sb("total", [P, NH, T])
        share = sb("share", [P, NH, T])
        oT = sb("oT", [P, S])
        attn = sb("attn", [P, T, P])
        ps_s = [ps("ps_s0"), ps("ps_s1")]
        ps_p = [ps("ps_p0"), ps("ps_p1")]
        ps_o, ps_k, ps_q, ps_m = ps("ps_o"), ps("ps_k"), ps("ps_q"), ps("ps_m")

        passed = ev("passed_a")
        v_zeroed = ev("v_zeroed")
        h_in = ev("h_in", 16)
        hb_ready = ev("hb_ready", T, T)
        xn_ready = ev("xn_ready_a", T, T)
        xt_ready = ev("xt_ready_a", T, 2)
        xhi_ready = ev("xhi_ready_a", T)
        xlo_ready = ev("xlo_ready_a", T, 2)
        qkv_ready = ev("qkv_ready", T)
        bias_ready = ev("bias_ready", 2 * T)
        turn1_ready = ev("turn1_ready", 2 * T)
        turn2_ready = ev("turn2_ready", T)
        q_ready = ev("q_ready", T, 2)
        k_turned = ev("k_turned", T)
        kvhi_ready = ev("kvhi_ready", T)
        kvlo_ready = ev("kvlo_ready", T, 2)
        sel_ready = ev("sel_ready", NP * T)
        picked = ev("picked", NP * T, T)
        kTa_ready = ev("kTa_ready", NP)
        kTb_ready = ev("kTb_ready", NP)
        vT_ready = ev("vT_ready", NP)
        vt_ready = ev("vt_ready", NP)
        v_ready = ev("v_ready", NH)
        q4hi_ready = ev("q4hi_ready", NH)
        q4_ready = ev("q4_ready", NH)
        qt_ready = ev("qt_ready", NH, 2)
        qT_ready = ev("qT_ready", NH)
        s_ready = ev("s_ready", 2 * NH)
        max_ready = ev("max_ready", 2 * NH)
        exp_ready = ev("exp_ready", T * NH)
        pt_ready = ev("pt_ready", 2 * NH)
        phi_ready = ev("phi_ready", 2 * NH)
        plo_ready = ev("plo_ready", 2 * NH, 2)
        pv_ready = ev("pv_ready", NH, 4)
        oT_ready = ev("oT_ready", NQ)
        share_ready = ev("share_ready", NQ)
        ot_ready = ev("ot_ready", NQ)
        attn_ready = ev("attn_ready", NQ)
        at_ready = ev("at_ready", NQ)
        ahi_ready = ev("ahi_ready", NQ)
        alo_ready = ev("alo_ready", NQ, 1)
        proj_ready = ev("proj_ready", T)
        h2_ready = ev("h2_ready", T, T)
        h2_stored = ev("h2_stored", 16, 16)

        tile = lambda t: slice(P * t, P * (t + 1))
        part = lambda s: slice(HALF * s, HALF * (s + 1))

        misc = {}
        before = (alo_ready, 0)
        for n in range(NH + 3):
            if n >= 5 and n % 4 == 1:
                misc["out", n // 4 - 1] = before
                before = (attn_ready, n // 4)
            if n >= 6 and n % 4 == 2:
                misc["back", n // 4 - 1] = before
                before = (alo_ready, n // 4)
            if n < NH and n % 2 == 0:
                misc["v", n // 2] = before
                before = (v_ready, n + 2)

        with nc.Block() as block:
            @block.sync
            def _(sp):
                h2_stored.start(sp)
                with sp.Fori(0, B) as i:
                    xn_ready.wait(sp, i, 0)
                    hb_ready.wait(sp, i, 0)
                    sp.dma_start(h[:], scr["h"][bass.ds(i, 1)].rearrange("o (t p) d -> p (o t) d", p=P)
                                 ).then_inc(h_in.sem, 16)
                    h2_ready.wait(sp, i, T)
                    sp.dma_start(scr["h2"][bass.ds(i, 1)].rearrange("o (t p) d -> p (o t) d", p=P),
                                 h2[:]).then_inc(h2_stored.sem, 16)
                sp.wait_ge(h2_stored.sem, 16 * (B + 1))

            @block.gpsimd
            def _(pool):
                hb_ready.start(pool)
                for n in range(4):
                    pool.memset(v[n][:].bitcast(F32), 0.0).then_inc(v_zeroed.sem, 1)
                pool.memset(vT[0:64, :, :], 0.0).then_inc(v_zeroed.sem, 1)
                with pool.Fori(0, B) as i:
                    h_in.wait(pool, i, 16)
                    h2_ready.wait(pool, i, 0)
                    for t in range(T):
                        pool.tensor_tensor(hb[:, t, :], h[:, t, :], keep["bo"][:], ALU.add).then_inc(hb_ready.sem, 1)
                    for t in range(T):
                        bias_ready.wait(pool, i, 2 * (t + 1))
                        q_ready.wait(pool, i, t + 1 - 2)
                        last = None
                        for n, (lo, k) in enumerate(((0, NH), (NH, NKV))):
                            src = x[:, t % 2, HD * lo:HD * (lo + k)].rearrange("p (h two d) -> p h two d", two=2, d=HD // 2)
                            dst = turn2[:, t % 2, HD * lo:HD * (lo + k)].rearrange("p (h two d) -> p h two d", two=2, d=HD // 2)
                            for half in range(2):
                                sin = keep["sin"][:, t:t + 1, n, HD // 2 * half:HD // 2 * (half + 1)]
                                last = pool.tensor_tensor(dst[:, :, half, :], src[:, :, 1 - half, :],
                                                          sin.to_broadcast([P, k, HD // 2]), ALU.mult)
                        last.then_inc(turn2_ready.sem, 1)
                    q_ready.wait(pool, i, T)
                    for hd in range(NH):
                        qt_ready.wait(pool, i, hd + 1 - 2)
                        src = q[:, :, HD * hd:HD * (hd + 1)].unsqueeze(2).to_broadcast([P, T, 2, HD])
                        pool.sem_inc(passed.sem)
                        pool.tensor_copy(q4[:, hd % 2, :, 0:2, :].bitcast(F32R), src).then_inc(q4hi_ready.sem, 1)
                        q4hi_ready.wait(pool, i, hd + 1)
                        pool.tensor_tensor(q4[:, hd % 2, :, 2:4, :], src, q4[:, hd % 2, :, 0:2, :],
                                           ALU.subtract).then_inc(q4_ready.sem, 1)

            @block.scalar
            def _(act):
                with act.Fori(0, B) as i:
                    def x_hi(t):
                        xt_ready.wait(act, i, t + 1)
                        act.activation(xT[0][:, :, tile(t)], ps_p[t % 2][:].rearrange("p (c s) -> p c s", c=C),
                                       ACT.Copy).then_inc(xhi_ready.sem, 1)

                    def kv_hi(t):
                        k_turned.wait(act, i, t + 1)
                        src = x[:, t % 2, NH * HD:QKV].rearrange("p (s g d) -> p s g d", s=2, d=HD)
                        act.activation(kv[:, t, :, :, 0, :].rearrange("p g s d -> p s g d"), src,
                                       ACT.Copy).then_inc(kvhi_ready.sem, 1)

                    def k_rows(g):
                        picked.wait(act, i, T * (g + 1))
                        act.activation(kT[0:64, g % 2, :], ps_k[0:64, 0:2 * KEEP], ACT.Copy).then_inc(kTa_ready.sem, 1)

                    def q_rows(hd):
                        qt_ready.wait(act, i, hd + 1)
                        act.activation(qT[:, hd % 2, :], ps_q[:], ACT.Copy).then_inc(qT_ready.sem, 1)

                    def exps(hd, s):
                        max_ready.wait(act, i, 2 * hd + s + 1)
                        for t in (2 * s, 2 * s + 1):
                            act.activation(prob[:, hd % 2, t, :], ps_s[s][:, KEEP * (t % 2):KEEP * (t % 2 + 1)],
                                           ACT.Exp, bias=nmax[:, hd % 2, t:t + 1],
                                           accum_out=total[:, hd, t:t + 1]).then_inc(exp_ready.sem, 1)

                    def p_hi(hd, s):
                        pt_ready.wait(act, i, 2 * hd + s + 1)
                        act.activation(pT[0][:, s, :], ps_p[s][0:HALF, :], ACT.Copy).then_inc(phi_ready.sem, 1)

                    def out_rows(c):
                        pv_ready.wait(act, i, 4 * (c + 1))
                        act.activation(oT[:], ps_o[:], ACT.Copy).then_inc(oT_ready.sem, 1)

                    def a_hi(c):
                        at_ready.wait(act, i, c + 1)
                        act.activation(xT[0][:, c, :], ps_m[:], ACT.Copy).then_inc(ahi_ready.sem, 1)

                    x_hi(0)
                    x_hi(1)
                    x_hi(2)
                    x_hi(3)
                    for t in range(T):
                        kv_hi(t)
                    k_rows(0)
                    q_rows(0)
                    exps(0, 0)
                    exps(0, 1)
                    for n in range(NH):
                        if n % 2 and n + 1 < NH:
                            k_rows((n + 1) // 2)
                        if n + 1 < NH:
                            q_rows(n + 1)
                        if n >= 4 and n % 4 == 0:
                            out_rows(n // 4 - 1)
                        if n >= 6 and n % 4 == 2:
                            a_hi(n // 4 - 1)
                        for s in range(2):
                            if n + 1 < NH:
                                exps(n + 1, s)
                            p_hi(n, s)
                    out_rows(NQ - 1)
                    a_hi(NQ - 1)

            @block.vector
            def _(dve):
                xn_ready.start(dve)
                xlo_ready.start(dve)
                q_ready.start(dve)
                plo_ready.start(dve)
                kvlo_ready.start(dve)
                alo_ready.start(dve)
                h2_ready.start(dve)
                dve.wait_ge(v_zeroed.sem, 5)
                with dve.Fori(0, B) as i:
                    def norm(t):
                        xt_ready.wait(dve, i, t + 1 - 2)
                        dve.tensor_scalar(xn[:, t % 2, :], h[:, t, :], keep["mean"][:, bass.ds(i * T + t, 1)],
                                          keep["rstd"][:, bass.ds(i * T + t, 1)], ALU.subtract,
                                          ALU.mult).then_inc(xn_ready.sem, 1)

                    def x_lo(t):
                        xhi_ready.wait(dve, i, t + 1)
                        dve.tensor_tensor(xT[1][:, :, tile(t)], ps_p[t % 2][:].rearrange("p (c s) -> p c s", c=C),
                                          xT[0][:, :, tile(t)].bitcast(F32), ALU.subtract).then_inc(xlo_ready.sem, 1)

                    def biases(t):
                        kvlo_ready.wait(dve, i, t + 1 - 2)
                        qkv_ready.wait(dve, i, t + 1)
                        for n, (bank, at) in enumerate(((ps_s[t % 2], slice(0, 512)), ((ps_k, ps_q)[t % 2], slice(512, 1024)))):
                            dve.tensor_tensor(x[:, t % 2, at], bank[:], keep["bqkv"][:, at], ALU.add).then_inc(bias_ready.sem, 1)
                        for n, (lo, k) in enumerate(((0, NH), (NH, NKV))):
                            at = slice(HD * lo, HD * (lo + k))
                            bias_ready.wait(dve, i, 2 * t + n + 1)
                            dve.tensor_tensor(turn1[:, t % 2, at].rearrange("p (h d) -> p h d", d=HD),
                                              x[:, t % 2, at].rearrange("p (h d) -> p h d", d=HD),
                                              keep["cos"][:, t:t + 1, n, :].to_broadcast([P, k, HD]),
                                              ALU.mult).then_inc(turn1_ready.sem, 1)

                    def rotated(t):
                        turn2_ready.wait(dve, i, t + 1)
                        turn1_ready.wait(dve, i, 2 * (t + 1))
                        at = slice(NH * HD, ROPE)
                        dve.tensor_tensor(x[:, t % 2, at], turn1[:, t % 2, at], turn2[:, t % 2, at],
                                          ALU.add).then_inc(k_turned.sem, 1)
                        at = slice(0, NH * HD)
                        dve.tensor_tensor(q[:, t, :], turn1[:, t % 2, at], turn2[:, t % 2, at],
                                          ALU.add).then_inc(q_ready.sem, 1)
                        kvhi_ready.wait(dve, i, t + 1)
                        k_turned.wait(dve, i, t + 1)
                        view = lambda z: kv[:, t, :, :, z, :].rearrange("p g s d -> p s g d")
                        dve.tensor_tensor(view(1), x[:, t % 2, NH * HD:QKV].rearrange("p (s g d) -> p s g d", s=2, d=HD),
                                          view(0).bitcast(F32), ALU.subtract).then_inc(kvlo_ready.sem, 1)

                    def select(g):
                        for t in range(T):
                            picked.wait(dve, i, T * g + t + 1 - T)
                            for n in range(2):
                                last = dve.tensor_scalar(sel[:, t, n, :], keep["iota"][:],
                                                         keep["pos"][:, t, bass.ds(i * NH + 2 * g + n, 1)], None,
                                                         ALU.is_equal)
                            last.then_inc(sel_ready.sem, 1)

                    def kv_rows(g):
                        picked.wait(dve, i, T * (g + 1))
                        dve.tensor_copy(vT[64:128, g % 2, :], ps_k[64:128, 0:2 * KEEP]).then_inc(vT_ready.sem, 1)
                        kTa_ready.wait(dve, i, g + 1)
                        dve.tensor_copy(kT[64:128, g % 2, :], kT[0:64, g % 2, :]).then_inc(kTb_ready.sem, 1)

                    def v_cols(g):
                        vt_ready.wait(dve, i, g + 1)
                        for hd in (2 * g, 2 * g + 1):
                            n = hd % 4
                            pv_ready.wait(dve, i, hd + 1 - 4)
                            src = ps_m[0:HALF, 256 * (hd % 2):256 * (hd % 2) + 256].rearrange("p (s x) -> p s x", s=2)
                            dve.tensor_copy(v[n][:, :, :, HD * n:HD * (n + 1)],
                                            src[:, :, 64:128].rearrange("p s (l d) -> p s l d", l=2)
                                            ).then_inc(v_ready.sem, 1)

                    def maxima(hd, s):
                        s_ready.wait(dve, i, 2 * hd + s + 1)
                        dve.tensor_reduce(nmax[:, hd % 2, 2 * s:2 * s + 2],
                                          ps_s[s][:, 0:2 * KEEP].rearrange("p (t k) -> p t k", t=2), AX.X,
                                          ALU.max, negate=True).then_inc(max_ready.sem, 1)

                    def p_lo(hd, s):
                        phi_ready.wait(dve, i, 2 * hd + s + 1)
                        dve.tensor_tensor(pT[1][:, s, :], ps_p[s][0:HALF, :], pT[0][:, s, :].bitcast(F32),
                                          ALU.subtract).then_inc(plo_ready.sem, 1)

                    def shares(c):
                        exp_ready.wait(dve, i, 16 * (c + 1))
                        dve.reciprocal(share[:, 4 * c:4 * c + 4, :], total[:, 4 * c:4 * c + 4, :]).then_inc(share_ready.sem, 1)

                    def normalised(c):
                        share_ready.wait(dve, i, c + 1)
                        ot_ready.wait(dve, i, c + 1)
                        dve.tensor_tensor(attn[:].rearrange("p t (n d) -> p t n d", n=4),
                                          ps_m[:].rearrange("p (t n d) -> p t n d", t=T, n=4),
                                          share[:, 4 * c:4 * c + 4, :].rearrange("p n t -> p t n").unsqueeze(3)
                                          .to_broadcast([P, T, 4, HD]), ALU.mult).then_inc(attn_ready.sem, 1)

                    def a_lo(c):
                        ahi_ready.wait(dve, i, c + 1)
                        dve.tensor_tensor(xT[1][:, c, :], ps_m[:], xT[0][:, c, :].bitcast(F32),
                                          ALU.subtract).then_inc(alo_ready.sem, 1)

                    h_in.wait(dve, i, 16)
                    norm(0)
                    norm(1)
                    x_lo(0)
                    norm(2)
                    x_lo(1)
                    norm(3)
                    biases(0)
                    x_lo(2)
                    x_lo(3)
                    biases(1)
                    rotated(0)
                    select(0)
                    biases(2)
                    rotated(1)
                    biases(3)
                    rotated(2)
                    rotated(3)
                    kv_rows(0)
                    maxima(0, 0)
                    maxima(0, 1)
                    for n in range(NH):
                        if n % 2 == 0 and n + 2 < NH:
                            select(n // 2 + 1)
                        if n % 2 and n + 1 < NH:
                            kv_rows((n + 1) // 2)
                        if n >= 4 and n % 4 == 0:
                            shares(n // 4 - 1)
                        if n >= 5 and n % 4 == 1:
                            normalised(n // 4 - 1)
                        if n >= 6 and n % 4 == 2:
                            a_lo(n // 4 - 1)
                        if n % 2 == 0:
                            v_cols(n // 2)
                        for s in range(2):
                            if n + 1 < NH:
                                maxima(n + 1, s)
                        for s in range(2):
                            p_lo(n, s)
                    shares(NQ - 1)
                    normalised(NQ - 1)
                    a_lo(NQ - 1)
                    h2_stored.wait(dve, i, 0)
                    hb_ready.wait(dve, i, T)
                    for t in range(T):
                        proj_ready.wait(dve, i, t + 1)
                        dve.tensor_tensor(h2[:, t, :], ps_s[t % 2][:], hb[:, t, :], ALU.add).then_inc(h2_ready.sem, 1)

            @block.tensor
            def _(pe):
                xt_ready.start(pe)
                picked.start(pe)
                qt_ready.start(pe)
                pv_ready.start(pe)
                with pe.Fori(0, B) as i:
                    def turn_x(t):
                        xn_ready.wait(pe, i, t + 1)
                        xlo_ready.wait(pe, i, t + 1 - 2)
                        for c in range(C):
                            last = pe.transpose(ps_p[t % 2][:, tile(c)], xn[:, t % 2, tile(c)], ident[:])
                        last.then_inc(xt_ready.sem, 1)

                    def project(t):
                        xlo_ready.wait(pe, i, t + 1)
                        if t >= 2:
                            bias_ready.wait(pe, i, 2 * (t - 1))
                        for bank, at in ((ps_s[t % 2], slice(0, 512)), ((ps_k, ps_q)[t % 2], slice(512, 1024))):
                            for c in range(C):
                                last = product(pe, bank[:], [m[:, c, tile(t)] for m in xT],
                                               [m[:, c, at] for m in wqkv], c == 0, c == C - 1)
                        last.then_inc(qkv_ready.sem, 1)

                    def pick(g):
                        if g:
                            kTa_ready.wait(pe, i, g)
                            vT_ready.wait(pe, i, g)
                        else:
                            kvlo_ready.wait(pe, i, T)
                        for t in range(T):
                            sel_ready.wait(pe, i, T * g + t + 1)
                            mm = pe.matmul(ps_k[:, 0:2 * KEEP], kv[:, t, g, :, :, :].rearrange("p s l d -> p (s l d)"),
                                           sel[:, t, :, :].rearrange("p n k -> p (n k)"), start=(t == 0), stop=(t == T - 1))
                            mm.then_inc(picked.sem, 1)

                    def turn_v(g):
                        e, n = misc["v", g]
                        e.wait(pe, i, n)
                        vT_ready.wait(pe, i, g + 1)
                        for n in range(2):
                            for s in range(2):
                                at = 256 * n + 128 * s
                                last = pe.transpose(ps_m[0:HALF, at:at + P],
                                                    vT[:, g % 2, KEEP * n + HALF * s:KEEP * n + HALF * (s + 1)],
                                                    ident[:])
                        last.then_inc(vt_ready.sem, 1)

                    def turn_q(hd):
                        if hd:
                            qT_ready.wait(pe, i, hd)
                        q4_ready.wait(pe, i, hd + 1)
                        for t in range(T):
                            last = pe.transpose(ps_q[:, tile(t)], q4[:, hd % 2, t, :, :].rearrange("p n d -> p (n d)"), ident[:])
                        last.then_inc(qt_ready.sem, 1)

                    def scores(hd):
                        qT_ready.wait(pe, i, hd + 1)
                        kTa_ready.wait(pe, i, hd // 2 + 1)
                        kTb_ready.wait(pe, i, hd // 2 + 1)
                        for t in range(T):
                            if hd and t % 2 == 0:
                                exp_ready.wait(pe, i, T * (hd - 1) + t + 2)
                            mm = pe.matmul(ps_s[t // 2][:, KEEP * (t % 2):KEEP * (t % 2 + 1)], qT[:, hd % 2, tile(t)],
                                           kT[:, hd // 2 % 2, KEEP * (hd % 2):KEEP * (hd % 2 + 1)], start=True, stop=True)
                            if t % 2:
                                mm.then_inc(s_ready.sem, 1)

                    def turn_p(hd):
                        exp_ready.wait(pe, i, T * (hd + 1))
                        for s in range(2):
                            plo_ready.wait(pe, i, 2 * hd + s + 1 - 2)
                            for t in range(T):
                                last = pe.transpose(ps_p[s][0:HALF, tile(t)], prob[:, hd % 2, t, part(s)], ident[:])
                            last.then_inc(pt_ready.sem, 1)

                    def values(hd):
                        n = hd % 4
                        v_ready.wait(pe, i, hd + 1)
                        if n == 0 and hd:
                            oT_ready.wait(pe, i, hd // 4)
                        for s in range(2):
                            plo_ready.wait(pe, i, 2 * hd + s + 1)
                            last = product(pe, ps_o[:], [v[n][:, s, l, :] for l in range(2)], [m[:, s, :] for m in pT],
                                           n == 0 and s == 0, n == 3 and s == 1)
                        last.then_inc(pv_ready.sem, 1)

                    def turn_out(c):
                        e, n = misc["out", c]
                        e.wait(pe, i, n)
                        oT_ready.wait(pe, i, c + 1)
                        for t in range(T):
                            last = pe.transpose(ps_m[:, tile(t)], oT[:, tile(t)], ident[:])
                        last.then_inc(ot_ready.sem, 1)

                    def turn_back(c):
                        attn_ready.wait(pe, i, c + 1)
                        for t in range(T):
                            last = pe.transpose(ps_m[:, tile(t)], attn[:, t, :], ident[:])
                        last.then_inc(at_ready.sem, 1)

                    turn_x(0)
                    turn_x(1)
                    project(0)
                    turn_x(2)
                    project(1)
                    turn_x(3)
                    project(2)
                    project(3)
                    pick(0)
                    turn_q(0)
                    scores(0)
                    for n in range(NH):
                        if n % 2 and n + 1 < NH:
                            pick((n + 1) // 2)
                        if n + 1 < NH:
                            turn_q(n + 1)
                        if n >= 5 and n % 4 == 1:
                            turn_out(n // 4 - 1)
                        if n >= 6 and n % 4 == 2:
                            turn_back(n // 4 - 1)
                        if n:
                            values(n - 1)
                        if n % 2 == 0:
                            turn_v(n // 2)
                        if n + 1 < NH:
                            scores(n + 1)
                        turn_p(n)
                    values(NH - 1)
                    turn_out(NQ - 1)
                    turn_back(NQ - 1)
                    alo_ready.wait(pe, i, NQ)
                    for t in range(T):
                        if t >= 2:
                            h2_ready.wait(pe, i, t - 1)
                        for c in range(C):
                            last = product(pe, ps_s[t % 2][:], [m[:, c, tile(t)] for m in xT],
                                           [m[:, c, :] for m in wo], c == 0, c == C - 1)
                        last.then_inc(proj_ready.sem, 1)


def ffn_phase(nc, ident, a, scr, out):
    with ExitStack() as ctx:
        sb = lambda name, shape, dt=F32: ctx.enter_context(nc.sbuf_tensor(name, shape, dt))
        ps = lambda name: ctx.enter_context(nc.psum_tensor(name, [P, 512], F32))
        ev = lambda name, per=1, base=0: Event(ctx, nc, name, per, base)
        RING, LAG = 4, 3
        w1 = [sb("w1_hi", [P, C, H], F32R), sb("w1_lo", [P, C, H], F32R)]
        w2 = [sb("w2_hi", [P, HC, D], F32R), sb("w2_lo", [P, HC, D], F32R)]
        b1 = sb("b1", [P, HC])
        b2 = sb("b2", [P, D])
        h = sb("h_f", [P, T, D])
        hb = sb("hb_f", [P, T, D])
        res = sb("res", [P, T, D])
        stats = sb("stats_f", [P, T, 6])
        mean_var = sb("mean_var_f", [P, T, 2])
        exponent = sb("exponent_f", [P, T])
        rstd = sb("rstd_f", [P, T])
        xn = sb("xn_f", [P, 2, D])
        xT = [sb("xT_hi_f", [P, C, S], F32R), sb("xT_lo_f", [P, C, S], F32R)]
        g = sb("g", [P, 2, S])
        gs = [sb("g_hi", [P, RING, S], F32R), sb("g_lo", [P, RING, S], F32R)]
        ps_x = [ps("ps_x0"), ps("ps_x1")]
        ps_h = [ps("ps_h0"), ps("ps_h1")]
        ps_y = [ps(f"ps_y{t}") for t in range(T)]

        PIECES = 8
        piece_in = [ev("piece_in0", 16), ev("piece_in1", 16)]
        small_in = ev("small_in_f")
        piece_hi = ev("piece_hi")
        piece_lo = ev("piece_lo")
        set_ready = ev("set_ready")
        passed = ev("passed_f")
        h_in = ev("h_in_f", 16)
        stats_ready = ev("stats_ready_f", T)
        var_ready = ev("var_ready_f", T, T)
        rstd_ready = ev("rstd_ready_f", 1)
        hb_ready = ev("hb_ready_f", T, T)
        xn_ready = ev("xn_ready_f", T, T)
        xt_ready = ev("xt_ready_f", T, 2)
        xhi_ready = ev("xhi_ready_f", T)
        xlo_ready = ev("xlo_ready_f", T, 2)
        up_ready = ev("up_ready", HC, HC)
        gelu_ready = ev("gelu_ready", HC, 2)
        ghi_ready = ev("ghi_ready", HC)
        glo_ready = ev("glo_ready", HC, 2)
        down_ready = ev("down_ready", HC, RING)
        res_ready = ev("res_ready", T, T)
        res_stored = ev("res_stored", 16, 16)
        tile = lambda t: slice(P * t, P * (t + 1))

        def piece(n):
            if n < 4:
                return a["w1"][P * n:P * (n + 1), :], [w[:, n, :] for w in w1]
            at = slice(4 * (n - 4), 4 * (n - 3))
            return (a["w2"].rearrange("(c p) n -> p c n", p=P)[:, at, :],
                    [w[:, at, :].rearrange("p c n -> p (c n)") for w in w2])

        stage = (hb, res)
        flat = lambda m: m[:].rearrange("p t d -> p (t d)")

        def batches(eng, body, front):
            front(0)
            with eng.Fori(0, B - 1) as i:
                body(i, lambda: front(i + 1))
            body(B - 1, None)

        with nc.Block() as block:
            @block.sync
            def _(sp):
                res_stored.start(sp)
                sp.dma_start(b1[:], a["b1"]).then_inc(small_in.sem, 16)
                sp.dma_start(b2[:], a["b2"].to_broadcast([P, D])).then_inc(small_in.sem, 16)
                for n in range(PIECES):
                    if n >= 2:
                        sp.wait_ge(piece_lo.sem, n - 1)
                    src, _ = piece(n)
                    dst = flat(stage[n % 2]) if n < 4 else stage[n % 2][:]
                    sp.dma_start(dst, src).then_inc(piece_in[n % 2].sem, 16)

                def front(i):
                    xn_ready.wait(sp, i, 0)
                    hb_ready.wait(sp, i, 0)
                    sp.dma_start(h[:], scr["h2"][bass.ds(i, 1)].rearrange("o (t p) d -> p (o t) d", p=P)
                                 ).then_inc(h_in.sem, 16)

                def body(i, more):
                    if more:
                        more()
                    res_ready.wait(sp, i, T)
                    sp.dma_start(out[bass.ds(i, 1)].rearrange("o (t p) d -> p (o t) d", p=P),
                                 res[:]).then_inc(res_stored.sem, 16)

                batches(sp, body, front)
                sp.wait_ge(res_stored.sem, 16 * (B + 1))

            @block.gpsimd
            def _(pool):
                hb_ready.start(pool)
                pool.memset(exponent[:], -0.5).then_inc(set_ready.sem, 1)
                pool.wait_ge(set_ready.sem, 1)
                pool.wait_ge(small_in.sem, 32)
                pool.wait_ge(piece_lo.sem, PIECES)

                def front(i):
                    var_ready.wait(pool, i, T)
                    pool.tensor_tensor(rstd[:], mean_var[:, :, 1], exponent[:], ALU.pow).then_inc(rstd_ready.sem, 1)

                def sums(i):
                    h_in.wait(pool, i, 16)
                    res_ready.wait(pool, i, 0)
                    for t in range(T):
                        pool.tensor_tensor(hb[:, t, :], h[:, t, :], b2[:], ALU.add).then_inc(hb_ready.sem, 1)

                def body(i, more):
                    sums(i)
                    if more:
                        more()

                batches(pool, body, front)

            @block.scalar
            def _(act):
                gelu_ready.start(act)
                for n in range(PIECES):
                    act.wait_ge(piece_in[n % 2].sem, 16 * (n // 2 + 1))
                    act.activation(piece(n)[1][0], flat(stage[n % 2]), ACT.Copy).then_inc(piece_hi.sem, 1)
                act.wait_ge(small_in.sem, 32)

                def front(i):
                    for t in range(T):
                        xt_ready.wait(act, i, t + 1)
                        act.activation(xT[0][:, :, tile(t)], ps_x[t % 2][:].rearrange("p (c s) -> p c s", c=C),
                                       ACT.Copy).then_inc(xhi_ready.sem, 1)

                def body(i, more):
                    for c in range(HC):
                        up_ready.wait(act, i, c + 1)
                        glo_ready.wait(act, i, c + 1 - 2)
                        act.activation(g[:, c % 2, :], ps_h[c % 2][:], ACT.Gelu, bias=b1[:, c:c + 1]
                                       ).then_inc(gelu_ready.sem, 1)
                    if more:
                        more()

                batches(act, body, front)

            @block.vector
            def _(dve):
                var_ready.start(dve)
                xn_ready.start(dve)
                xlo_ready.start(dve)
                glo_ready.start(dve)
                res_ready.start(dve)
                for n in range(PIECES):
                    dve.wait_ge(piece_hi.sem, n + 1)
                    hi, lo = piece(n)[1]
                    dve.tensor_tensor(lo, flat(stage[n % 2]), hi.bitcast(F32), ALU.subtract).then_inc(piece_lo.sem, 1)

                def moments(i):
                    h_in.wait(dve, i, 16)
                    for t in range(T):
                        dve.bn_stats(stats[:, t, :], h[:, t, :]).then_inc(stats_ready.sem, 1)
                    stats_ready.wait(dve, i, T)
                    dve.sem_inc(passed.sem)
                    for t in range(T):
                        dve.bn_aggr(mean_var[:, t, :], stats[:, t, :]).then_inc(var_ready.sem, 1)

                def norms(i):
                    rstd_ready.wait(dve, i, 1)

                    def norm(t):
                        xt_ready.wait(dve, i, t + 1 - 2)
                        dve.tensor_scalar(xn[:, t % 2, :], h[:, t, :], mean_var[:, t, 0:1], rstd[:, t:t + 1],
                                          ALU.subtract, ALU.mult).then_inc(xn_ready.sem, 1)

                    def x_lo(t):
                        xhi_ready.wait(dve, i, t + 1)
                        dve.tensor_tensor(xT[1][:, :, tile(t)], ps_x[t % 2][:].rearrange("p (c s) -> p c s", c=C),
                                          xT[0][:, :, tile(t)].bitcast(F32), ALU.subtract).then_inc(xlo_ready.sem, 1)

                    norm(0)
                    norm(1)
                    x_lo(0)
                    norm(2)
                    x_lo(1)
                    norm(3)
                    x_lo(2)
                    x_lo(3)

                def front(i):
                    moments(i)
                    norms(i)

                def body(i, more):
                    for c in range(HC):
                        gelu_ready.wait(dve, i, c + 1)
                        down_ready.wait(dve, i, c + 1 - RING)
                        at = c % RING
                        dve.tensor_copy(gs[0][:, at, :], g[:, c % 2, :]).then_inc(ghi_ready.sem, 1)
                        ghi_ready.wait(dve, i, c + 1)
                        dve.tensor_tensor(gs[1][:, at, :], g[:, c % 2, :], gs[0][:, at, :].bitcast(F32),
                                          ALU.subtract).then_inc(glo_ready.sem, 1)
                    if more:
                        more()
                    res_stored.wait(dve, i, 0)
                    hb_ready.wait(dve, i, T)
                    down_ready.wait(dve, i, HC)
                    for t in range(T):
                        dve.tensor_tensor(res[:, t, :], ps_y[t][:], hb[:, t, :], ALU.add).then_inc(res_ready.sem, 1)

                batches(dve, body, front)

            @block.tensor
            def _(pe):
                xt_ready.start(pe)
                up_ready.start(pe)
                down_ready.start(pe)
                pe.wait_ge(piece_lo.sem, PIECES)

                def turn(i, t):
                    xn_ready.wait(pe, i, t + 1)
                    xlo_ready.wait(pe, i, t + 1 - 2)
                    for c in range(C):
                        last = pe.transpose(ps_x[t % 2][:, tile(c)], xn[:, t % 2, tile(c)], ident[:])
                    last.then_inc(xt_ready.sem, 1)

                def front(i):
                    for t in range(T):
                        turn(i, t)

                def up(i, c):
                    gelu_ready.wait(pe, i, c + 1 - 2)
                    for k in range(C):
                        last = product(pe, ps_h[c % 2][:], [w[:, k, tile(c)] for w in w1], [m[:, k, :] for m in xT],
                                       k == 0, k == C - 1)
                    last.then_inc(up_ready.sem, 1)

                def down(i, c):
                    glo_ready.wait(pe, i, c + 1)
                    for t in range(T):
                        if c == 0:
                            res_ready.wait(pe, i, t + 1 - T)
                        last = product(pe, ps_y[t][:], [m[:, c % RING, tile(t)] for m in gs], [w[:, c, :] for w in w2],
                                       c == 0, c == HC - 1)
                    last.then_inc(down_ready.sem, 1)

                def body(i, more):
                    xlo_ready.wait(pe, i, T)
                    for c in range(HC + LAG):
                        if c < HC:
                            up(i, c)
                        if c == HC and more:
                            down(i, c - LAG)
                            turn(i + 1, 0)
                            turn(i + 1, 1)
                        elif c == HC + 1 and more:
                            down(i, c - LAG)
                            turn(i + 1, 2)
                            turn(i + 1, 3)
                        elif c >= LAG:
                            down(i, c - LAG)

                batches(pe, body, front)


def program(nc, a, out):
    scr_of = lambda name, shape: nc.dram_tensor(name, shape, F32, kind="Internal").ap()
    scr = {"ids": scr_of("scr_ids", [B * S]), "h": scr_of("scr_h", [B, S, D]), "route": scr_of("scr_route", [B, NH, S]),
           "h2": scr_of("scr_h2", [B, S, D])}
    scr["ids2"] = scr["ids"].rearrange("(b s) -> b s", s=S)
    with ExitStack() as ctx:
        sb = lambda name, shape, dt=F32: ctx.enter_context(nc.sbuf_tensor(name, shape, dt))
        keep = {"ident": sb("ident", [P, P]), "iota": sb("iota", [P, KEEP]),
                "bqkv": sb("bqkv", [P, QKV]), "bo": sb("bo", [P, D]),
                "cos": sb("cos", [P, T, 2, HD]), "sin": sb("sin", [P, T, 2, HD]),
                "mean": sb("mean", [P, B * T]), "rstd": sb("rstd", [P, B * T]),
                "pos": sb("pos", [P, T, B * NH]),
                "wqkv": [sb("wqkv_hi", [P, C, QKV], F32R), sb("wqkv_lo", [P, C, QKV], F32R)],
                "wo": [sb("wo_hi", [P, C, D], F32R), sb("wo_lo", [P, C, D], F32R)]}
        embed_phase(nc, keep, a, scr)
        choose_phase(nc, keep, scr)
        attend_phase(nc, keep, scr)
    with ExitStack() as ctx:
        ident = ctx.enter_context(nc.sbuf_tensor("ident_f", [P, P], F32))
        set_ready = Event(ctx, nc, "ident_ready", 1)
        with nc.Block() as block:
            @block.gpsimd
            def _(pool):
                identity(pool, ident, set_ready)
        ffn_phase(nc, ident, a, scr, out)


def layout(inputs):
    get = lambda name: np.ascontiguousarray(np.asarray(inputs[name]))
    row = lambda name: get(name).reshape(1, -1)
    inv_freq = 1.0 / np.float32(1000000.0) ** (np.arange(0, HD, 2, dtype=np.float32) / np.float32(HD))
    angle = (np.arange(S, dtype=np.float32)[:, None] * inv_freq[None, :].astype(np.float32)).astype(np.float32)
    cos, sin = np.cos(angle), np.sin(angle)
    table = lambda halves: np.stack([np.concatenate(halves, -1) * k for k in (SCALE, 1.0)], 1).astype(np.float32)
    return {
        "x": get("x").reshape(B * T, P),
        "W": get("L0_tok_W"),
        "delta": np.ascontiguousarray(get("L0_tok_delta_values").reshape(D, NTRAIN).T),
        "token_indices": get("L0_tok_token_indices").reshape(NTRAIN, 1),
        "Wq": get("L0_attn_Wq"), "bq": row("L0_attn_bq"), "Wk": get("L0_attn_Wk"), "bk": row("L0_attn_bk"),
        "Wv": get("L0_attn_Wv"), "bv": row("L0_attn_bv"), "Wo": get("L0_attn_Wo"), "bo": row("L0_attn_bo"),
        "Wr": get("L0_attn_Wr"), "br": get("L0_attn_br").reshape(NH, 1),
        "w1": np.ascontiguousarray(get("L0_ffn_proj1").T), "b1": np.ascontiguousarray(get("L0_ffn_proj1_bias").reshape(HC, P).T),
        "w2": np.ascontiguousarray(get("L0_ffn_proj2").T), "b2": row("L0_ffn_proj2_bias"),
        "cos": table([cos, cos]), "sin": table([-sin, sin]),
    }


def kernel(**inputs):
    import concourse.bacc as bacc
    from concourse.bass_utils import run_bass_kernel_spmd

    nc = bacc.Bacc("TRN2", target_bir_lowering=False, num_devices=1)
    arrays = {f"in_{name}": array for name, array in layout(inputs).items()}
    a = {name[3:]: nc.dram_tensor(name, list(array.shape), mybir.dt.from_np(array.dtype), kind="ExternalInput").ap()
         for name, array in arrays.items()}
    out = nc.dram_tensor("out", [B, S, D], F32, kind="ExternalOutput").ap()
    program(nc, a, out)
    return run_bass_kernel_spmd(nc, [arrays], core_ids=[0]).results[0]["out"]
```

```python
from contextlib import ExitStack

import numpy as np

import concourse.bass as bass
from concourse import mybir

F32 = mybir.dt.float32
F32R = mybir.dt.float32r
I32 = mybir.dt.int32
ALU = mybir.AluOpType
ACT = mybir.ActivationFunctionType
AX = mybir.AxisListType

P = 128
B, S, D = 16, 512, 512
V = 32000
NTRAIN = 64
T = S // P
C = D // P
NH, NKV, HD = 16, 8, 32
KEEP = int(S * 0.4)
HALF = KEEP // 2
QKV = (NH + 2 * NKV) * HD
ROPE = (NH + NKV) * HD
SCALE = float(HD) ** -0.5
H = 2048
HC = H // P
EPS = 1e-5
GROUP = P // NH
NG = B // GROUP


class Event:

    def __init__(self, ctx, nc, name, per, base=0):
        self.sem, self.per, self.base = ctx.enter_context(nc.semaphore(name)), per, base

    def start(self, eng):
        if self.base:
            eng.sem_inc(self.sem, self.base)

    def wait(self, eng, i, n):
        assert n + self.base >= 1, "a wait that might be against zero"
        eng.wait_ge(self.sem, i * self.per + (n + self.base))


def product(pe, out, lhs, rhs, first, last):
    pe.matmul(out, lhs[0], rhs[0], start=first, stop=False, skip_group_check=True)
    pe.matmul(out, lhs[0], rhs[1], start=False, stop=False, skip_group_check=True)
    return pe.matmul(out, lhs[1], rhs[0], start=False, stop=last, skip_group_check=True)


def identity(pool, ident, set_ready):
    pool.memset(ident[:], 0.0).then_inc(set_ready.sem, 1)
    pool.wait_ge(set_ready.sem, 1)
    pool.affine_select(out=ident[:], in_=ident[:], compare_op=ALU.not_equal, fill=1.0,
                       base=0, pattern=[[-1, P]], channel_multiplier=1).then_inc(set_ready.sem, 1)


def embed_phase(nc, keep, a, scr):
    with ExitStack() as ctx:
        sb = lambda name, shape, dt=F32: ctx.enter_context(nc.sbuf_tensor(name, shape, dt))
        ev = lambda name, per=1, base=0: Event(ctx, nc, name, per, base)
        ids_i = sb("ids_i", [B * T, P], I32)
        ids_f = sb("ids_f", [B * T, P])
        ids_neg = sb("ids_neg", [B * T, P])
        id_col = sb("id_col", [P, B * T], I32)
        ids_now = sb("ids_now", [P, 2, T], I32)
        trained_i = sb("trained_i", [P, 1], I32)
        trained = sb("trained", [P, 1])
        trained_neg = sb("trained_neg", [P, 1])
        delta_raw = sb("delta_raw", [P, D])
        delta_hi = sb("delta_hi", [P, D])
        delta = sb("delta", [P, D], F32R)
        id_row = sb("id_row", [P, 2, S])
        onehot = sb("onehot", [P, 2, S], F32R)
        rows = sb("rows", [P, 2, T, D])
        h = sb("h0", [P, 2, T, D])
        stats = sb("stats", [P, T, 6])
        mean_var = sb("mean_var", [P, 2, T, 2])
        exponent = sb("exponent", [P, T])
        rstd = sb("rstd_now", [P, 2, T])
        shift = sb("shift_now", [P, 2, T])
        xn = sb("xn0", [P, 2, D])
        xT = sb("xT0", [P, C, S])
        logit = sb("logit", [NH, 2, S])
        br = sb("br", [NH, 1])
        wr = sb("wr", [P, C, NH])
        ps_delta = [ctx.enter_context(nc.psum_tensor(f"ps_delta{t}", [P, D], F32)) for t in range(T)]
        ps_xT = [ctx.enter_context(nc.psum_tensor(f"ps_xT0{n}", [P, C, P], F32)) for n in range(2)]
        ps_route = ctx.enter_context(nc.psum_tensor("ps_route", [NH, S], F32))
        ps_ids = ctx.enter_context(nc.psum_tensor("ps_ids", [P, B * T], F32))

        passed = ev("passed")
        ids_in = ev("ids_in")
        small_in = ev("small_in")
        biases_in = ev("biases_in")
        made = ev("made")
        ids_ready = ev("ids_ready")
        ids_turned = ev("ids_turned")
        ids_stored = ev("ids_stored")
        id_col_ready = ev("id_col_ready")
        const_ready = ev("const_ready")
        row_in = [ev(f"row_in{m}", 8) for m in range(2)]
        onehot_ready = ev("onehot_ready", 1, 2)
        delta_ready = ev("delta_ready", T, T + 1)
        ids_now_ready = ev("ids_now_ready", 1)
        gathered = [[ev(f"gathered{m}{t}", 8) for t in range(T)] for m in range(2)]
        h_ready = ev("h_ready", T, T + 1)
        stats_ready = ev("stats_ready", T)
        var_ready = ev("var_ready", T, T)
        rstd_ready = ev("rstd_ready", 1)
        product_ready = ev("product_ready", 1)
        shift_ready = ev("shift_ready", 1)
        stats_kept = ev("stats_kept", 1, 2)
        h_stored = [ev(f"h_stored{m}", 8, 16) for m in range(2)]
        xn_ready = ev("xn_ready", T, T + 1)
        xT_ready = ev("xT_ready", T, 2)
        copied = ev("copied", T, 2)
        route_ready = ev("route_ready", 1, 1)
        logit_ready = ev("logit_ready", 1, 1)
        logit_stored = [ev(f"logit_stored{m}", 8, 16) for m in range(2)]

        def slot_before(stored, eng, i, m):
            stored[m].wait(eng, i, -8 * m)

        def batches(eng, front, body):
            front(0, 0)
            with eng.Fori(0, B // 2 - 1) as pair:
                body(pair * 2, 0, True)
                body(pair * 2 + 1, 1, True)
            body(B - 2, 0, True)
            body(B - 1, 1, False)

        with nc.Block() as block:
            @block.sync
            def _(sp):
                for m in range(2):
                    h_stored[m].start(sp)
                sp.dma_start(ids_i[:], a["x"]).then_inc(ids_in.sem, 16)
                for half in range(2):
                    at = slice(NTRAIN * half, NTRAIN * (half + 1))
                    sp.dma_start(trained_i[at, :], a["token_indices"]).then_inc(small_in.sem, 16)
                    sp.dma_start(delta_raw[at, :], a["delta"]).then_inc(small_in.sem, 16)
                sp.dma_start(br[:], a["br"]).then_inc(small_in.sem, 16)
                sp.dma_start(wr[:], a["Wr"].rearrange("(c p) n -> p c n", p=P)).then_inc(small_in.sem, 16)
                ids_ready.wait(sp, 0, 1)
                sp.dma_start(scr["ids"].rearrange("(t p) -> t p", p=P), ids_f[:]).then_inc(ids_stored.sem, 16)
                sp.wait_ge(ids_stored.sem, 16)

                def front(i, m):
                    onehot_ready.wait(sp, i, -1)
                    sp.dma_start(id_row[:, m, :], scr["ids2"][bass.ds(i, 1), :].to_broadcast([P, S])).then_inc(row_in[m].sem, 16)

                def body(i, m, more):
                    if more:
                        front(i + 1, 1 - m)
                    h_ready.wait(sp, i, T)
                    sp.dma_start(scr["h"][bass.ds(i, 1)].rearrange("o (t p) d -> p (o t) d", p=P),
                                 h[:, m]).then_inc(h_stored[m].sem, 16)

                batches(sp, front, body)
                for n, (w, k) in enumerate((("bq", NH), ("bk", NKV), ("bv", NKV))):
                    at = (0, NH * HD, ROPE)[n]
                    sp.dma_start(keep["bqkv"][:, at:at + k * HD],
                                 a[w].to_broadcast([P, k * HD])).then_inc(biases_in.sem, 16)
                sp.dma_start(keep["bo"][:], a["bo"].to_broadcast([P, D])).then_inc(biases_in.sem, 16)
                sp.dma_start(keep["cos"][:], a["cos"].rearrange("(t p) k n -> p t k n", p=P)).then_inc(biases_in.sem, 16)
                sp.dma_start(keep["sin"][:], a["sin"].rearrange("(t p) k n -> p t k n", p=P)).then_inc(biases_in.sem, 16)
                sp.wait_ge(biases_in.sem, 16 * 6)
                for m in range(2):
                    sp.wait_ge(h_stored[m].sem, 16 * (B // 2 + 1))
                    sp.wait_ge(logit_stored[m].sem, 16 * (B // 2 + 1))

            @block.gpsimd
            def _(pool):
                stats_kept.start(pool)
                pool.memset(keep["ident"][:], 0.0).then_inc(const_ready.sem, 1)
                pool.memset(exponent[:], -0.5).then_inc(const_ready.sem, 1)
                pool.iota(keep["iota"][:], [[1, KEEP]], base=0, channel_multiplier=0,
                          allow_small_or_imprecise_dtypes=True).then_inc(const_ready.sem, 1)
                pool.wait_ge(const_ready.sem, 3)
                pool.affine_select(out=keep["ident"][:], in_=keep["ident"][:], compare_op=ALU.not_equal, fill=1.0,
                                   base=0, pattern=[[-1, P]], channel_multiplier=1).then_inc(const_ready.sem, 1)
                id_col_ready.wait(pool, 0, 1)

                def front(i, m):
                    h_ready.wait(pool, i, -T)
                    pool.tensor_copy(ids_now[:, m, :], id_col[:, bass.ds(i * T, T)]).then_inc(ids_now_ready.sem, 1)
                    ids_now_ready.wait(pool, i, 1)
                    pool.sem_inc(passed.sem)
                    for t in range(T):
                        pool.indirect_dma_start(out=rows[:, m, t, :], out_offset=None, in_=a["W"],
                                                in_offset=bass.IndirectOffsetOnAxis(ap=ids_now[:, m, t:t + 1], axis=0)
                                                ).then_inc(gathered[m][t].sem, 16)

                def body(i, m, more):
                    if more:
                        front(i + 1, 1 - m)
                    var_ready.wait(pool, i, T)
                    xn_ready.wait(pool, i, -T)
                    pool.tensor_tensor(rstd[:, m], mean_var[:, m, :, 1], exponent[:], ALU.pow).then_inc(rstd_ready.sem, 1)
                    rstd_ready.wait(pool, i, 1)
                    pool.tensor_tensor(shift[:, m], mean_var[:, m, :, 0], rstd[:, m], ALU.mult).then_inc(product_ready.sem, 1)
                    product_ready.wait(pool, i, 1)
                    pool.sem_inc(passed.sem)
                    pool.tensor_scalar(shift[:, m], shift[:, m], -1.0, None, ALU.mult).then_inc(shift_ready.sem, 1)
                    pool.tensor_copy(keep["rstd"][:, bass.ds(i * T, T)], rstd[:, m])
                    pool.tensor_copy(keep["mean"][:, bass.ds(i * T, T)], mean_var[:, m, :, 0]).then_inc(stats_kept.sem, 1)

                batches(pool, front, body)

            @block.vector
            def _(dve):
                steps = [0]

                def done(instruction):
                    steps[0] += 1
                    instruction.then_inc(made.sem, 1)
                    dve.wait_ge(made.sem, steps[0])

                onehot_ready.start(dve)
                h_ready.start(dve)
                var_ready.start(dve)
                for src, neg, out in ((ids_i, ids_neg, ids_f), (trained_i, trained_neg, trained)):
                    if src is ids_i:
                        dve.wait_ge(ids_in.sem, 16)
                    else:
                        dve.wait_ge(small_in.sem, 16 * 6)
                    done(dve.tensor_copy(out[:], src[:]))
                    done(dve.tensor_scalar(neg[:], out[:], 0.0, float(V), ALU.is_lt, ALU.mult))
                    done(dve.tensor_tensor(out[:], out[:], neg[:], ALU.add))
                    if src is ids_i:
                        dve.tensor_scalar(ids_f[:], ids_f[:], 0.0, float(V - 1), ALU.max, ALU.min).then_inc(ids_ready.sem, 1)
                        dve.wait_ge(ids_turned.sem, 1)
                        dve.tensor_copy(id_col[:], ps_ids[:]).then_inc(id_col_ready.sem, 1)
                done(dve.tensor_copy(delta_hi[:].bitcast(F32R), delta_raw[:]))
                dve.tensor_copy(delta[0:NTRAIN, :], delta_hi[0:NTRAIN, :])
                done(dve.tensor_tensor(delta[NTRAIN:P, :], delta_raw[NTRAIN:P, :], delta_hi[NTRAIN:P, :], ALU.subtract))

                def front(i, m):
                    row_in[m].wait(dve, i, 16 - 8 * m)
                    delta_ready.wait(dve, i, -T)
                    dve.tensor_scalar(onehot[:, m, :], id_row[:, m, :], trained[:, 0:1], None,
                                      ALU.is_equal).then_inc(onehot_ready.sem, 1)

                def body(i, m, more):
                    if more:
                        front(i + 1, 1 - m)
                    slot_before(h_stored, dve, i, m)
                    xn_ready.wait(dve, i, -T)
                    for t in range(T):
                        gathered[m][t].wait(dve, i, 16 - 8 * m)
                        delta_ready.wait(dve, i, t + 1)
                        dve.tensor_tensor(h[:, m, t, :], rows[:, m, t, :], ps_delta[t][:], ALU.add).then_inc(h_ready.sem, 1)
                    var_ready.wait(dve, i, 0)
                    for t in range(T):
                        h_ready.wait(dve, i, t + 1)
                        dve.bn_stats(stats[:, t, :], h[:, m, t, :]).then_inc(stats_ready.sem, 1)
                    stats_kept.wait(dve, i, -1)
                    stats_ready.wait(dve, i, T)
                    dve.sem_inc(passed.sem)
                    for t in range(T):
                        dve.bn_aggr(mean_var[:, m, t, :], stats[:, t, :]).then_inc(var_ready.sem, 1)

                batches(dve, front, body)

            @block.scalar
            def _(act):
                logit_ready.start(act)
                xn_ready.start(act)
                copied.start(act)
                for m in range(2):
                    logit_stored[m].start(act)
                act.wait_ge(small_in.sem, 16 * 6)

                def norm(i, m, t):
                    xT_ready.wait(act, i, t + 1 - 2)
                    act.activation(xn[:, t % 2, :], h[:, m, t, :], ACT.Identity, bias=shift[:, m, t:t + 1],
                                   scale=rstd[:, m, t:t + 1]).then_inc(xn_ready.sem, 1)

                def copy(i, t):
                    xT_ready.wait(act, i, t + 1)
                    act.activation(xT[:, :, P * t:P * (t + 1)], ps_xT[t % 2][:], ACT.Copy).then_inc(copied.sem, 1)

                def front(i, m):
                    shift_ready.wait(act, i, 1)
                    norm(i, m, 0)
                    norm(i, m, 1)

                def body(i, m, more):
                    route_ready.wait(act, i, 0)
                    copy(i, 0)
                    norm(i, m, 2)
                    copy(i, 1)
                    norm(i, m, 3)
                    copy(i, 2)
                    copy(i, 3)
                    if more:
                        front(i + 1, 1 - m)
                    route_ready.wait(act, i, 1)
                    slot_before(logit_stored, act, i, m)
                    act.activation(logit[:, m, :], ps_route[:], ACT.Identity, bias=br[:, 0:1]).then_inc(logit_ready.sem, 1)
                    logit_ready.wait(act, i, 1)
                    act.dma_start(scr["route"][bass.ds(i, 1)].rearrange("o h s -> (o h) s"),
                                  logit[:, m, :]).then_inc(logit_stored[m].sem, 16)

                batches(act, front, body)

            @block.tensor
            def _(pe):
                xT_ready.start(pe)
                route_ready.start(pe)
                delta_ready.start(pe)
                pe.wait_ge(const_ready.sem, 4)
                ids_ready.wait(pe, 0, 1)
                pe.transpose(ps_ids[:], ids_f[:], keep["ident"][0:B * T, 0:B * T]).then_inc(ids_turned.sem, 1)
                pe.wait_ge(small_in.sem, 16 * 6)
                pe.wait_ge(made.sem, 6 + 2)

                def front(i, m):
                    onehot_ready.wait(pe, i, 1)
                    for t in range(T):
                        h_ready.wait(pe, i, t + 1 - T)
                        pe.matmul(ps_delta[t][:], onehot[:, m, P * t:P * (t + 1)], delta[:],
                                  start=True, stop=True).then_inc(delta_ready.sem, 1)

                def body(i, m, more):
                    if more:
                        front(i + 1, 1 - m)
                    for t in range(T):
                        xn_ready.wait(pe, i, t + 1)
                        copied.wait(pe, i, t + 1 - 2)
                        for c in range(C):
                            last = pe.transpose(ps_xT[t % 2][:, c, :], xn[:, t % 2, P * c:P * (c + 1)],
                                                keep["ident"][:])
                        last.then_inc(xT_ready.sem, 1)
                    copied.wait(pe, i, T)
                    logit_ready.wait(pe, i, 0)
                    for c in range(C):
                        last = pe.matmul(ps_route[:], wr[:, c, :], xT[:, c, :], start=(c == 0), stop=(c == C - 1))
                    last.then_inc(route_ready.sem, 1)

                batches(pe, front, body)


def choose_phase(nc, keep, a, scr):
    with ExitStack() as ctx:
        sb = lambda name, shape, dt=F32: ctx.enter_context(nc.sbuf_tensor(name, shape, dt))
        ev = lambda name, per=1, base=0: Event(ctx, nc, name, per, base)
        ROUNDS = -(-KEEP // 8)
        REST = KEEP - 8 * (ROUNDS - 1)
        TAKEN, BEYOND = -1.0, 2.0
        logit = sb("logits", [P, NG, S])
        score = sb("score", [P, NG, S + 8])
        best = sb("best", [P, 8])
        one = sb("one", [P, S])
        chosen = sb("chosen", [P, NG, S])
        count = sb("count", [P, NG, S])
        wqkv_raw = sb("wqkv_raw", [P, C, QKV])
        wo_raw = sb("wo_raw", [P, C, D])
        ps_pos = [ctx.enter_context(nc.psum_tensor(f"ps_pos{g}", [P, T, P], F32)) for g in range(NG)]
        logits_in = ev("logits_in")
        scored = ev("scored")
        made = ev("made2")
        place_ready = ev("place_ready")
        turned = ev("turned")
        weights_in = ev("weights_in")
        w_hi_ready = ev("w_hi_ready")
        w_lo_ready = ev("w_lo_ready")
        weights = ((wqkv_raw, *keep["wqkv"]), (wo_raw, *keep["wo"]))
        with nc.Block() as block:
            @block.sync
            def _(sp):
                sp.dma_start(logit[:], scr["route"].rearrange("(g b) h s -> (b h) g s", g=NG)
                             ).then_inc(logits_in.sem, 16)
                for n, (w, k) in enumerate((("Wq", NH), ("Wk", NKV), ("Wv", NKV))):
                    at = (0, NH * HD, ROPE)[n]
                    sp.dma_start(wqkv_raw[:, :, at:at + k * HD],
                                 a[w].rearrange("(c p) n -> p c n", p=P)).then_inc(weights_in.sem, 16)
                sp.dma_start(wo_raw[:], a["Wo"].rearrange("(c p) n -> p c n", p=P)).then_inc(weights_in.sem, 16)

            @block.scalar
            def _(act):
                act.wait_ge(logits_in.sem, 16)
                for g in range(NG):
                    act.activation(score[:, g, 0:S], logit[:, g, :], ACT.Sigmoid).then_inc(scored.sem, 1)
                act.wait_ge(weights_in.sem, 16 * 4)
                for raw, hi, lo in weights:
                    act.activation(hi[:], raw[:], ACT.Copy).then_inc(w_hi_ready.sem, 1)

            @block.gpsimd
            def _(pool):
                for n, (raw, hi, lo) in enumerate(weights):
                    pool.wait_ge(w_hi_ready.sem, n + 1)
                    pool.tensor_tensor(lo[:], raw[:], hi[:].bitcast(F32), ALU.subtract).then_inc(w_lo_ready.sem, 1)

            @block.vector
            def _(dve):
                steps = [0]

                def done(instruction):
                    steps[0] += 1
                    instruction.then_inc(made.sem, 1)
                    dve.wait_ge(made.sem, steps[0])

                dve.memset(score[:, :, S:S + 8], BEYOND)
                done(dve.memset(one[:], 1.0))
                dve.wait_ge(scored.sem, NG)
                for g in range(NG):
                    for r in range(ROUNDS):
                        width = S if r < ROUNDS - 1 else S + 8 - REST
                        done(dve.max(best[:], score[:, g, 0:S]))
                        if width > S:
                            done(dve.memset(best[:, REST:8], BEYOND))
                        done(dve.match_replace(score[:, g, 0:width], best[:], score[:, g, 0:width], TAKEN))
                    done(dve.tensor_scalar(chosen[:, g, :], score[:, g, 0:S], 0.0, None, ALU.is_lt))
                    done(dve.tensor_tensor_scan(count[:, g, :], one[:], chosen[:, g, :], 0.0, ALU.mult, ALU.add))
                    dve.tensor_tensor(count[:, g, :], count[:, g, :], chosen[:, g, :],
                                      ALU.mult).then_inc(place_ready.sem, 1)
                for g in range(NG):
                    dve.wait_ge(turned.sem, g + 1)
                    dve.tensor_scalar(keep["pos"][:, :, P * g:P * (g + 1)], ps_pos[g][:], 1.0, None,
                                      ALU.subtract)

            @block.tensor
            def _(pe):
                for g in range(NG):
                    pe.wait_ge(place_ready.sem, g + 1)
                    for t in range(T):
                        last = pe.transpose(ps_pos[g][:, t, :], count[:, g, P * t:P * (t + 1)], keep["ident"][:])
                    last.then_inc(turned.sem, 1)


def attend_phase(nc, keep, scr):
    with ExitStack() as ctx:
        sb = lambda name, shape, dt=F32: ctx.enter_context(nc.sbuf_tensor(name, shape, dt))
        ps = lambda name: ctx.enter_context(nc.psum_tensor(name, [P, 512], F32))
        ev = lambda name, per=1, base=0: Event(ctx, nc, name, per, base)
        ident, wqkv, wo = keep["ident"], keep["wqkv"], keep["wo"]
        NP = NH // 2
        NQ = NH // 4
        h = sb("h_a", [P, T, D])
        h2 = sb("h2_a", [P, T, D])
        xT = [sb("xT_hi_a", [P, C, S], F32R), sb("xT_lo_a", [P, C, S], F32R)]
        aT = [sb("aT_hi", [P, C, S], F32R), sb("aT_lo", [P, C, S], F32R)]
        x = sb("x_a", [P, 2, QKV])
        turn1 = sb("turn1", [P, 2, ROPE])
        turn2 = sb("turn2", [P, 2, ROPE])
        xn = turn1[:, :, 0:D]
        q = sb("q_a", [P, T, NH * HD])
        kv = sb("kv_a", [P, T, NKV, 2, 2, HD], F32R)
        sel = sb("sel", [P, T, 2, KEEP], F32R)
        kT = sb("kT", [P, 2, 2 * KEEP], F32R)
        vT = sb("vT", [P, 2, 2 * KEEP])
        v = [sb(f"v{n}", [HALF, 2, 2, P], F32R) for n in range(4)]
        q4 = sb("q4", [P, 2, T, 4, HD])
        qT = sb("qT", [P, 2, S], F32R)
        prob = sb("prob", [P, 2, T, KEEP])
        pT = [sb("pT_hi", [HALF, 2, 2, S], F32R), sb("pT_lo", [HALF, 2, 2, S], F32R)]
        nmax = sb("nmax", [P, 2, T])
        total = sb("total", [P, NH, T])
        share = sb("share", [P, NH, T])
        oT = sb("oT", [P, S])
        attn = sb("attn", [P, T, P])
        ps_s = [ps("ps_s0"), ps("ps_s1")]
        ps_p = [ps("ps_p0"), ps("ps_p1")]
        ps_o, ps_k, ps_q, ps_m = ps("ps_o"), ps("ps_k"), ps("ps_q"), ps("ps_m")

        passed = ev("passed_a")
        v_zeroed = ev("v_zeroed")
        h_in = ev("h_in", 16)
        sum_ready = ev("sum_ready", T, T)
        xn_ready = ev("xn_ready_a", T, T)
        xt_ready = ev("xt_ready_a", T, 2)
        xhi_ready = ev("xhi_ready_a", T)
        xlo_ready = ev("xlo_ready_a", T, 2)
        qkv_ready = ev("qkv_ready", 2 * T)
        bias_ready = ev("bias_ready", 2 * T)
        turn1_ready = ev("turn1_ready", 2 * T)
        turn2_ready = ev("turn2_ready", T)
        q_ready = ev("q_ready", T, 2)
        k_turned = ev("k_turned", T)
        kvhi_ready = ev("kvhi_ready", T)
        kvlo_ready = ev("kvlo_ready", T, 2)
        sel_ready = ev("sel_ready", NP * T)
        picked = ev("picked", NP * T, T)
        kTa_ready = ev("kTa_ready", NP, 1)
        kTb_ready = ev("kTb_ready", NP)
        vT_ready = ev("vT_ready", NP, 1)
        vt_ready = ev("vt_ready", NP)
        v_ready = ev("v_ready", NH)
        q4hi_ready = ev("q4hi_ready", NH)
        q4_ready = ev("q4_ready", NH, 2)
        qt_ready = ev("qt_ready", NH, 2)
        qT_ready = ev("qT_ready", NH, 1)
        s_ready = ev("s_ready", 2 * NH)
        max_ready = ev("max_ready", 2 * NH)
        exp_ready = ev("exp_ready", T * NH, 1)
        pt_ready = ev("pt_ready", 2 * NH)
        phi_ready = ev("phi_ready", 2 * NH)
        plo_ready = ev("plo_ready", 2 * NH, 2)
        pv_ready = ev("pv_ready", NH, 4)
        oT_ready = ev("oT_ready", NQ)
        share_ready = ev("share_ready", NQ)
        ot_ready = ev("ot_ready", NQ)
        attn_ready = ev("attn_ready", NQ)
        at_ready = ev("at_ready", NQ)
        ahi_ready = ev("ahi_ready", NQ)
        alo_ready = ev("alo_ready", NQ, 1)
        proj_ready = ev("proj_ready", T)
        h2_ready = ev("h2_ready", T, T)
        h2_stored = ev("h2_stored", 16 * T, 16)

        tile = lambda t: slice(P * t, P * (t + 1))
        part = lambda s: slice(HALF * s, HALF * (s + 1))

        kv_bank = [ps_k, ps_k, ps_s[0], ps_k]
        q_bank = [ps_q, ps_q, ps_s[1], ps_q]
        out_bank = [*ps_s, *ps_p]

        misc = {("v", 0): (alo_ready, 0)}
        before = (v_ready, 2)
        for n in range(NH + 4):
            if n % 2 and n + 1 < NH:
                misc["v", (n + 1) // 2] = before
                before = (v_ready, n + 3)
            if n >= 6 and n % 4 == 2:
                misc["back", n // 4 - 1] = before
                before = (alo_ready, n // 4)
            if n >= 5 and n % 4 == 1:
                misc["out", n // 4 - 1] = before
                before = (attn_ready, n // 4)

        def batches(eng, body, front):
            front(0)
            with eng.Fori(0, B - 1) as i:
                body(i, i + 1)
            body(B - 1, None)

        with nc.Block() as block:
            @block.sync
            def _(sp):
                h2_stored.start(sp)

                def front(j):
                    xn_ready.wait(sp, j, 0)
                    sum_ready.wait(sp, j, 0)
                    sp.dma_start(h[:], scr["h"][bass.ds(j, 1)].rearrange("o (t p) d -> p (o t) d", p=P)
                                 ).then_inc(h_in.sem, 16)

                def body(i, j):
                    if j is not None:
                        front(j)
                    for t in range(T):
                        h2_ready.wait(sp, i, t + 1)
                        sp.dma_start(scr["h2"][bass.ds(i, 1), tile(t), :].rearrange("o p d -> p (o d)"),
                                     h2[:, t, :]).then_inc(h2_stored.sem, 16)

                batches(sp, body, front)
                sp.wait_ge(h2_stored.sem, 16 * (B * T + 1))

            @block.gpsimd
            def _(pool):
                sum_ready.start(pool)
                for n in range(4):
                    pool.memset(v[n][:].bitcast(F32), 0.0).then_inc(v_zeroed.sem, 1)
                pool.memset(vT[0:64, :, :], 0.0).then_inc(v_zeroed.sem, 1)
                q4_ready.start(pool)

                def front(j):
                    for t in range(T):
                        bias_ready.wait(pool, j, 2 * (t + 1))
                        q_ready.wait(pool, j, t + 1 - 2)
                        for n, (lo, k) in enumerate(((0, NH), (NH, NKV))):
                            view = lambda m: (m[:, t % 2, HD * lo:HD * (lo + k)]
                                              .rearrange("p (h two d) -> p h two d", two=2, d=HD // 2))
                            for half in range(2):
                                sin = keep["sin"][:, t:t + 1, n, HD // 2 * half:HD // 2 * (half + 1)]
                                last = pool.tensor_tensor(view(turn2)[:, :, half, :], view(x)[:, :, 1 - half, :],
                                                          sin.to_broadcast([P, k, HD // 2]), ALU.mult)
                        last.then_inc(turn2_ready.sem, 1)

                def body(i, j):
                    q_ready.wait(pool, i, T)
                    for hd in range(NH):
                        qt_ready.wait(pool, i, hd + 1 - 2)
                        q4_ready.wait(pool, i, hd + 1 - 2)
                        src = q[:, :, HD * hd:HD * (hd + 1)].unsqueeze(2).to_broadcast([P, T, 2, HD])
                        pool.sem_inc(passed.sem)
                        pool.tensor_copy(q4[:, hd % 2, :, 0:2, :].bitcast(F32R), src).then_inc(q4hi_ready.sem, 1)
                        q4hi_ready.wait(pool, i, hd + 1)
                        pool.tensor_tensor(q4[:, hd % 2, :, 2:4, :], src, q4[:, hd % 2, :, 0:2, :],
                                           ALU.subtract).then_inc(q4_ready.sem, 1)
                        if hd == 2:
                            h_in.wait(pool, i, 16)
                            h2_stored.wait(pool, i, 0)
                            for t in range(T):
                                pool.tensor_tensor(h2[:, t, :], h[:, t, :], keep["bo"][:],
                                                   ALU.add).then_inc(sum_ready.sem, 1)
                    if j is not None:
                        front(j)

                batches(pool, body, front)

            @block.scalar
            def _(act):
                exp_ready.start(act)
                kTa_ready.start(act)
                qT_ready.start(act)

                def x_hi(j, t):
                    xt_ready.wait(act, j, t + 1)
                    act.activation(xT[0][:, :, tile(t)], ps_k[:].rearrange("p (c s) -> p c s", c=C),
                                   ACT.Copy).then_inc(xhi_ready.sem, 1)

                def kv_hi(j, t):
                    k_turned.wait(act, j, t + 1)
                    src = x[:, t % 2, NH * HD:QKV].rearrange("p (s g d) -> p s g d", s=2, d=HD)
                    act.activation(kv[:, t, :, :, 0, :].rearrange("p g s d -> p s g d"), src,
                                   ACT.Copy).then_inc(kvhi_ready.sem, 1)

                def k_rows(i, g):
                    picked.wait(act, i, T * (g + 1))
                    act.activation(kT[0:64, g % 2, :], ps_k[0:64, 0:2 * KEEP], ACT.Copy).then_inc(kTa_ready.sem, 1)

                def q_rows(i, hd):
                    qt_ready.wait(act, i, hd + 1)
                    act.activation(qT[:, hd % 2, :], ps_q[:], ACT.Copy).then_inc(qT_ready.sem, 1)

                def exps(i, hd):
                    for s in range(2):
                        max_ready.wait(act, i, 2 * hd + s + 1)
                        for t in (2 * s, 2 * s + 1):
                            act.activation(prob[:, hd % 2, t, :], ps_s[s][:, KEEP * (t % 2):KEEP * (t % 2 + 1)],
                                           ACT.Exp, bias=nmax[:, hd % 2, t:t + 1],
                                           accum_out=total[:, hd, t:t + 1]).then_inc(exp_ready.sem, 1)

                def p_hi(i, hd):
                    pv_ready.wait(act, i, hd + 1 - 2)
                    for s in range(2):
                        pt_ready.wait(act, i, 2 * hd + s + 1)
                        act.activation(pT[0][:, hd % 2, s, :], ps_p[s][0:HALF, :], ACT.Copy).then_inc(phi_ready.sem, 1)

                def out_rows(i, c):
                    pv_ready.wait(act, i, 4 * (c + 1))
                    act.activation(oT[:], ps_o[:], ACT.Copy).then_inc(oT_ready.sem, 1)

                def a_hi(i, c):
                    at_ready.wait(act, i, c + 1)
                    act.activation(aT[0][:, c, :], ps_m[:], ACT.Copy).then_inc(ahi_ready.sem, 1)

                def front(j):
                    for t in range(T):
                        x_hi(j, t)
                    for t in range(T):
                        kv_hi(j, t)

                def body(i, j):
                    q_rows(i, 0)
                    k_rows(i, 0)
                    q_rows(i, 1)
                    exps(i, 0)
                    for n in range(NH):
                        p_hi(i, n)
                        if n % 2 == 0 and n + 2 < NH:
                            q_rows(i, n + 2)
                        if n + 1 < NH:
                            exps(i, n + 1)
                        if n % 2 and n + 2 < NH:
                            q_rows(i, n + 2)
                        if n % 2 == 0 and n + 2 < NH:
                            k_rows(i, n // 2 + 1)
                        if n >= 4 and n % 4 == 0:
                            out_rows(i, n // 4 - 1)
                        if n >= 6 and n % 4 == 2:
                            a_hi(i, n // 4 - 1)
                        if j is not None and n >= 7 and n % 2:
                            if n < 15:
                                x_hi(j, (n - 7) // 2)
                            else:
                                kv_hi(j, 0)
                    out_rows(i, NQ - 1)
                    if j is not None:
                        kv_hi(j, 1)
                    a_hi(i, NQ - 1)
                    if j is not None:
                        kv_hi(j, 2)
                        kv_hi(j, 3)

                batches(act, body, front)

            @block.vector
            def _(dve):
                xn_ready.start(dve)
                xlo_ready.start(dve)
                q_ready.start(dve)
                plo_ready.start(dve)
                kvlo_ready.start(dve)
                alo_ready.start(dve)
                h2_ready.start(dve)
                dve.wait_ge(v_zeroed.sem, 5)
                vT_ready.start(dve)

                def norm(j, t):
                    if t < 2:
                        q_ready.wait(dve, j, 0)
                    xt_ready.wait(dve, j, t + 1 - 2)
                    dve.tensor_scalar(xn[:, t % 2, :], h[:, t, :], keep["mean"][:, bass.ds(j * T + t, 1)],
                                      keep["rstd"][:, bass.ds(j * T + t, 1)], ALU.subtract,
                                      ALU.mult).then_inc(xn_ready.sem, 1)

                def x_lo(j, t):
                    xhi_ready.wait(dve, j, t + 1)
                    dve.tensor_tensor(xT[1][:, :, tile(t)], ps_k[:].rearrange("p (c s) -> p c s", c=C),
                                      xT[0][:, :, tile(t)].bitcast(F32), ALU.subtract).then_inc(xlo_ready.sem, 1)

                def biases(j, t, n):
                    kvlo_ready.wait(dve, j, t + 1 - 2)
                    qkv_ready.wait(dve, j, 2 * t + n + 1)
                    bank = (kv_bank, q_bank)[n][t]
                    lo, k = ((NH, NKV), (0, NH))[n]
                    at = slice(HD * lo, HD * lo + 512)
                    dve.tensor_tensor(x[:, t % 2, at], bank[:], keep["bqkv"][:, at], ALU.add).then_inc(bias_ready.sem, 1)
                    at = slice(HD * lo, HD * (lo + k))
                    bias_ready.wait(dve, j, 2 * t + n + 1)
                    dve.tensor_tensor(turn1[:, t % 2, at].rearrange("p (h d) -> p h d", d=HD),
                                      x[:, t % 2, at].rearrange("p (h d) -> p h d", d=HD),
                                      keep["cos"][:, t:t + 1, 1 - n, :].to_broadcast([P, k, HD]),
                                      ALU.mult).then_inc(turn1_ready.sem, 1)

                def rotated(j, t):
                    turn2_ready.wait(dve, j, t + 1)
                    turn1_ready.wait(dve, j, 2 * (t + 1))
                    q4_ready.wait(dve, j, 0)
                    at = slice(NH * HD, ROPE)
                    dve.tensor_tensor(x[:, t % 2, at], turn1[:, t % 2, at], turn2[:, t % 2, at],
                                      ALU.add).then_inc(k_turned.sem, 1)
                    at = slice(0, NH * HD)
                    dve.tensor_tensor(q[:, t, :], turn1[:, t % 2, at], turn2[:, t % 2, at],
                                      ALU.add).then_inc(q_ready.sem, 1)
                    kvhi_ready.wait(dve, j, t + 1)
                    k_turned.wait(dve, j, t + 1)
                    view = lambda z: kv[:, t, :, :, z, :].rearrange("p g s d -> p s g d")
                    dve.tensor_tensor(view(1), x[:, t % 2, NH * HD:QKV].rearrange("p (s g d) -> p s g d", s=2, d=HD),
                                      view(0).bitcast(F32), ALU.subtract).then_inc(kvlo_ready.sem, 1)

                def select(i, g, tiles):
                    for t in tiles:
                        picked.wait(dve, i, T * g + t + 1 - T)
                        for n in range(2):
                            last = dve.tensor_scalar(sel[:, t, n, :], keep["iota"][:],
                                                     keep["pos"][:, t, bass.ds(i * NH + 2 * g + n, 1)], None,
                                                     ALU.is_equal)
                        last.then_inc(sel_ready.sem, 1)

                def kv_rows(i, g):
                    picked.wait(dve, i, T * (g + 1))
                    dve.tensor_copy(vT[64:128, g % 2, :], ps_k[64:128, 0:2 * KEEP]).then_inc(vT_ready.sem, 1)
                    kTa_ready.wait(dve, i, g + 1)
                    dve.tensor_copy(kT[64:128, g % 2, :], kT[0:64, g % 2, :]).then_inc(kTb_ready.sem, 1)

                def v_cols(i, g):
                    vt_ready.wait(dve, i, g + 1)
                    for hd in (2 * g, 2 * g + 1):
                        n = hd % 4
                        pv_ready.wait(dve, i, hd + 1 - 4)
                        src = ps_m[0:HALF, 256 * (hd % 2):256 * (hd % 2) + 256].rearrange("p (s x) -> p s x", s=2)
                        dve.tensor_copy(v[n][:, :, :, HD * n:HD * (n + 1)],
                                        src[:, :, 64:128].rearrange("p s (l d) -> p s l d", l=2)
                                        ).then_inc(v_ready.sem, 1)

                def maxima(i, hd):
                    for s in range(2):
                        s_ready.wait(dve, i, 2 * hd + s + 1)
                        dve.tensor_reduce(nmax[:, hd % 2, 2 * s:2 * s + 2],
                                          ps_s[s][:, 0:2 * KEEP].rearrange("p (t k) -> p t k", t=2), AX.X,
                                          ALU.max, negate=True).then_inc(max_ready.sem, 1)

                def p_lo(i, hd):
                    for s in range(2):
                        phi_ready.wait(dve, i, 2 * hd + s + 1)
                        dve.tensor_tensor(pT[1][:, hd % 2, s, :], ps_p[s][0:HALF, :], pT[0][:, hd % 2, s, :].bitcast(F32),
                                          ALU.subtract).then_inc(plo_ready.sem, 1)

                def shares(i, c):
                    exp_ready.wait(dve, i, 16 * (c + 1))
                    dve.reciprocal(share[:, 4 * c:4 * c + 4, :], total[:, 4 * c:4 * c + 4, :]).then_inc(share_ready.sem, 1)

                def normalised(i, c):
                    share_ready.wait(dve, i, c + 1)
                    ot_ready.wait(dve, i, c + 1)
                    dve.tensor_tensor(attn[:].rearrange("p t (n d) -> p t n d", n=4),
                                      ps_m[:].rearrange("p (t n d) -> p t n d", t=T, n=4),
                                      share[:, 4 * c:4 * c + 4, :].rearrange("p n t -> p t n").unsqueeze(3)
                                      .to_broadcast([P, T, 4, HD]), ALU.mult).then_inc(attn_ready.sem, 1)

                def a_lo(i, c):
                    ahi_ready.wait(dve, i, c + 1)
                    dve.tensor_tensor(aT[1][:, c, :], ps_m[:], aT[0][:, c, :].bitcast(F32),
                                      ALU.subtract).then_inc(alo_ready.sem, 1)

                def front(j):
                    h_in.wait(dve, j, 16)
                    norm(j, 0)
                    norm(j, 1)
                    x_lo(j, 0)
                    norm(j, 2)
                    x_lo(j, 1)
                    norm(j, 3)
                    x_lo(j, 2)
                    x_lo(j, 3)
                    for t in range(T):
                        biases(j, t, 0)
                        biases(j, t, 1)
                        if t:
                            rotated(j, t - 1)
                    rotated(j, T - 1)
                    select(j, 0, range(T))

                def body(i, j):
                    kv_rows(i, 0)
                    v_cols(i, 0)
                    maxima(i, 0)
                    select(i, 1, range(T))
                    for n in range(NH):
                        if n + 1 < NH:
                            maxima(i, n + 1)
                        p_lo(i, n)
                        if n >= 4 and n % 4 == 0:
                            shares(i, n // 4 - 1)
                        if n % 2 and n + 1 < NH:
                            v_cols(i, (n + 1) // 2)
                        if n % 2 == 0 and n + 2 < NH:
                            kv_rows(i, n // 2 + 1)
                        if n >= 6 and n % 4 == 2:
                            a_lo(i, n // 4 - 1)
                        if n >= 5 and n % 4 == 1:
                            normalised(i, n // 4 - 1)
                        if n + 3 < NH:
                            if n % 2 == 0 and n + 4 < NH:
                                select(i, n // 2 + 2, (0, 1))
                            elif n % 2:
                                select(i, (n + 3) // 2, (2, 3))
                        if j is not None:
                            if 6 <= n <= 12 and n % 2 == 0:
                                if n == 6:
                                    h_in.wait(dve, j, 16)
                                norm(j, (n - 6) // 2)
                            if 7 <= n <= 13 and n % 2:
                                x_lo(j, (n - 7) // 2)
                            if n >= 14:
                                biases(j, n - 14, 0)
                                biases(j, n - 14, 1)
                    shares(i, NQ - 1)
                    if j is not None:
                        rotated(j, 0)
                        biases(j, 2, 0)
                    normalised(i, NQ - 1)
                    if j is not None:
                        biases(j, 2, 1)
                        rotated(j, 1)
                    a_lo(i, NQ - 1)
                    if j is not None:
                        biases(j, 3, 0)
                        biases(j, 3, 1)
                        rotated(j, 2)
                        rotated(j, 3)
                        select(j, 0, range(T))
                    sum_ready.wait(dve, i, T)
                    for t in range(T):
                        proj_ready.wait(dve, i, t + 1)
                        dve.tensor_tensor(h2[:, t, :], out_bank[t][:], h2[:, t, :], ALU.add).then_inc(h2_ready.sem, 1)

                batches(dve, body, front)

            @block.tensor
            def _(pe):
                xt_ready.start(pe)
                picked.start(pe)
                qt_ready.start(pe)
                pv_ready.start(pe)
                def turn_x(j, t):
                    xn_ready.wait(pe, j, t + 1)
                    xlo_ready.wait(pe, j, t)
                    for c in range(C):
                        last = pe.transpose(ps_k[:, tile(c)], xn[:, t % 2, tile(c)], ident[:])
                    last.then_inc(xt_ready.sem, 1)

                def project(j, t, n):
                    xlo_ready.wait(pe, j, t + 1)
                    if t == 2:
                        exp_ready.wait(pe, j, 0)
                    elif t == 0:
                        (kTa_ready, qT_ready)[n].wait(pe, j, 0)
                        xlo_ready.wait(pe, j, T)
                    else:
                        bias_ready.wait(pe, j, 2 * (t // 2) + n + 1)
                    at = (slice(512, 1024), slice(0, 512))[n]
                    for c in range(C):
                        last = product(pe, (kv_bank, q_bank)[n][t][:], [m[:, c, tile(t)] for m in xT],
                                       [m[:, c, at] for m in wqkv], c == 0, c == C - 1)
                    last.then_inc(qkv_ready.sem, 1)

                def pick(i, j, g):
                    if g == 0:
                        kvlo_ready.wait(pe, i, T)
                    elif g >= 5 and j is not None:
                        xlo_ready.wait(pe, j, g - 4)
                    else:
                        kTa_ready.wait(pe, i, g)
                        vT_ready.wait(pe, i, g)
                    for t in range(T):
                        sel_ready.wait(pe, i, T * g + t + 1)
                        pe.matmul(ps_k[:, 0:2 * KEEP], kv[:, t, g, :, :, :].rearrange("p s l d -> p (s l d)"),
                                  sel[:, t, :, :].rearrange("p n k -> p (n k)"), start=(t == 0),
                                  stop=(t == T - 1)).then_inc(picked.sem, 1)

                def turn_v(i, g):
                    e, n = misc["v", g]
                    e.wait(pe, i, n)
                    vT_ready.wait(pe, i, g + 1)
                    for n in range(2):
                        for s in range(2):
                            at = 256 * n + 128 * s
                            last = pe.transpose(ps_m[0:HALF, at:at + P],
                                                vT[:, g % 2, KEEP * n + HALF * s:KEEP * n + HALF * (s + 1)], ident[:])
                    last.then_inc(vt_ready.sem, 1)

                def turn_q(i, hd):
                    if hd:
                        qT_ready.wait(pe, i, hd)
                    else:
                        bias_ready.wait(pe, i, 2 * T)
                    q4_ready.wait(pe, i, hd + 1)
                    for t in range(T):
                        last = pe.transpose(ps_q[:, tile(t)], q4[:, hd % 2, t, :, :].rearrange("p n d -> p (n d)"), ident[:])
                    last.then_inc(qt_ready.sem, 1)

                def scores(i, hd):
                    qT_ready.wait(pe, i, hd + 1)
                    kTa_ready.wait(pe, i, hd // 2 + 1)
                    kTb_ready.wait(pe, i, hd // 2 + 1)
                    for t in range(T):
                        if t % 2 == 0:
                            if hd:
                                exp_ready.wait(pe, i, T * (hd - 1) + t + 2)
                            else:
                                h2_ready.wait(pe, i, 0)
                        mm = pe.matmul(ps_s[t // 2][:, KEEP * (t % 2):KEEP * (t % 2 + 1)], qT[:, hd % 2, tile(t)],
                                       kT[:, hd // 2 % 2, KEEP * (hd % 2):KEEP * (hd % 2 + 1)], start=True, stop=True)
                        if t % 2:
                            mm.then_inc(s_ready.sem, 1)

                def turn_p(i, hd):
                    exp_ready.wait(pe, i, T * (hd + 1))
                    for s in range(2):
                        plo_ready.wait(pe, i, 2 * hd + s + 1 - 2)
                        for t in range(T):
                            last = pe.transpose(ps_p[s][0:HALF, tile(t)], prob[:, hd % 2, t, part(s)], ident[:])
                        last.then_inc(pt_ready.sem, 1)

                def values(i, hd):
                    n = hd % 4
                    v_ready.wait(pe, i, hd + 1)
                    if n == 0 and hd:
                        oT_ready.wait(pe, i, hd // 4)
                    for s in range(2):
                        plo_ready.wait(pe, i, 2 * hd + s + 1)
                        last = product(pe, ps_o[:], [v[n][:, s, l, :] for l in range(2)], [m[:, hd % 2, s, :] for m in pT],
                                       n == 0 and s == 0, n == 3 and s == 1)
                    last.then_inc(pv_ready.sem, 1)

                def turn_out(i, c):
                    e, n = misc["out", c]
                    e.wait(pe, i, n)
                    oT_ready.wait(pe, i, c + 1)
                    for t in range(T):
                        last = pe.transpose(ps_m[:, tile(t)], oT[:, tile(t)], ident[:])
                    last.then_inc(ot_ready.sem, 1)

                def turn_back(i, c):
                    e, n = misc["back", c]
                    e.wait(pe, i, n)
                    for t in range(T):
                        last = pe.transpose(ps_m[:, tile(t)], attn[:, t, :], ident[:])
                    last.then_inc(at_ready.sem, 1)

                def project_out(i, t):
                    for c in range(C):
                        last = product(pe, out_bank[t][:], [m[:, c, tile(t)] for m in aT],
                                       [m[:, c, :] for m in wo], c == 0, c == C - 1)
                    last.then_inc(proj_ready.sem, 1)

                def front(j):
                    for t in range(T):
                        turn_x(j, t)
                    for t in range(T):
                        project(j, t, 0)
                        project(j, t, 1)

                def body(i, j):
                    turn_q(i, 0)
                    pick(i, j, 0)
                    turn_q(i, 1)
                    turn_v(i, 0)
                    scores(i, 0)
                    for n in range(NH):
                        turn_p(i, n)
                        if n + 1 < NH:
                            scores(i, n + 1)
                        if n + 2 < NH:
                            turn_q(i, n + 2)
                        if n % 2 and n + 1 < NH:
                            turn_v(i, (n + 1) // 2)
                        if n % 2 == 0 and n + 2 < NH:
                            pick(i, j, n // 2 + 1)
                        if n:
                            values(i, n - 1)
                        if n >= 6 and n % 4 == 2:
                            turn_back(i, n // 4 - 1)
                        if n >= 5 and n % 4 == 1:
                            turn_out(i, n // 4 - 1)
                        if j is not None:
                            if 7 <= n <= 13 and n % 2:
                                kTa_ready.wait(pe, i, (n + 1) // 2 + 1)
                                vT_ready.wait(pe, i, (n + 1) // 2 + 1)
                                turn_x(j, (n - 7) // 2)
                            if n >= 14:
                                project(j, n - 14, 0)
                                project(j, n - 14, 1)
                    values(i, NH - 1)
                    if j is not None:
                        project(j, 2, 0)
                    turn_out(i, NQ - 1)
                    if j is not None:
                        project(j, 2, 1)
                    turn_back(i, NQ - 1)
                    if j is not None:
                        project(j, 3, 0)
                        project(j, 3, 1)
                    alo_ready.wait(pe, i, NQ)
                    bias_ready.wait(pe, j if j is not None else i, 2 * T - 2 if j is not None else 2 * T)
                    for t in range(T):
                        project_out(i, t)

                batches(pe, body, front)


def ffn_phase(nc, ident, a, scr, out):
    with ExitStack() as ctx:
        sb = lambda name, shape, dt=F32: ctx.enter_context(nc.sbuf_tensor(name, shape, dt))
        ps = lambda name: ctx.enter_context(nc.psum_tensor(name, [P, 512], F32))
        ev = lambda name, per=1, base=0: Event(ctx, nc, name, per, base)
        RING, LAG = 4, 3
        w1 = [sb("w1_hi", [P, C, H], F32R), sb("w1_lo", [P, C, H], F32R)]
        w2 = [sb("w2_hi", [P, HC, D], F32R), sb("w2_lo", [P, HC, D], F32R)]
        b1 = sb("b1", [P, HC])
        b2 = sb("b2", [P, D])
        h = sb("h_f", [P, T, D])
        hb = sb("hb_f", [P, T, D])
        res = sb("res", [P, T, D])
        stats = sb("stats_f", [P, T, 6])
        mean_var = sb("mean_var_f", [P, T, 2])
        exponent = sb("exponent_f", [P, T])
        rstd = sb("rstd_f", [P, T])
        xn = sb("xn_f", [P, 2, D])
        xT = [sb("xT_hi_f", [P, C, S], F32R), sb("xT_lo_f", [P, C, S], F32R)]
        g = sb("g", [P, 2, S])
        gs = [sb("g_hi", [P, RING, S], F32R), sb("g_lo", [P, RING, S], F32R)]
        ps_x = [ps("ps_x0"), ps("ps_x1")]
        ps_h = [ps("ps_h0"), ps("ps_h1")]
        ps_y = [ps(f"ps_y{t}") for t in range(T)]

        PIECES = 8
        piece_in = [ev("piece_in0", 16), ev("piece_in1", 16)]
        small_in = ev("small_in_f")
        piece_hi = ev("piece_hi")
        piece_lo = ev("piece_lo")
        set_ready = ev("set_ready")
        passed = ev("passed_f")
        h_in = ev("h_in_f", 16)
        stats_ready = ev("stats_ready_f", T)
        var_ready = ev("var_ready_f", T, T)
        rstd_ready = ev("rstd_ready_f", 1)
        hb_ready = ev("hb_ready_f", T, T)
        xn_ready = ev("xn_ready_f", T, T)
        xt_ready = ev("xt_ready_f", T, 2)
        xhi_ready = ev("xhi_ready_f", T)
        xlo_ready = ev("xlo_ready_f", T, 2)
        up_ready = ev("up_ready", HC, HC)
        gelu_ready = ev("gelu_ready", HC, 2)
        ghi_ready = ev("ghi_ready", HC)
        glo_ready = ev("glo_ready", HC, 2)
        down_ready = ev("down_ready", HC, RING)
        res_ready = ev("res_ready", T, T)
        res_stored = ev("res_stored", 16, 16)
        tile = lambda t: slice(P * t, P * (t + 1))

        def piece(n):
            if n < 4:
                return a["w1"][P * n:P * (n + 1), :], [w[:, n, :] for w in w1]
            at = slice(4 * (n - 4), 4 * (n - 3))
            return (a["w2"].rearrange("(c p) n -> p c n", p=P)[:, at, :],
                    [w[:, at, :].rearrange("p c n -> p (c n)") for w in w2])

        stage = (hb, res)
        flat = lambda m: m[:].rearrange("p t d -> p (t d)")

        def batches(eng, body, front):
            front(0)
            with eng.Fori(0, B - 1) as i:
                body(i, lambda: front(i + 1))
            body(B - 1, None)

        with nc.Block() as block:
            @block.sync
            def _(sp):
                res_stored.start(sp)
                sp.dma_start(b1[:], a["b1"]).then_inc(small_in.sem, 16)
                sp.dma_start(b2[:], a["b2"].to_broadcast([P, D])).then_inc(small_in.sem, 16)
                for n in range(PIECES):
                    if n >= 2:
                        sp.wait_ge(piece_lo.sem, n - 1)
                    src, _ = piece(n)
                    dst = flat(stage[n % 2]) if n < 4 else stage[n % 2][:]
                    sp.dma_start(dst, src).then_inc(piece_in[n % 2].sem, 16)

                def front(i):
                    xn_ready.wait(sp, i, 0)
                    hb_ready.wait(sp, i, 0)
                    sp.dma_start(h[:], scr["h2"][bass.ds(i, 1)].rearrange("o (t p) d -> p (o t) d", p=P)
                                 ).then_inc(h_in.sem, 16)

                def body(i, more):
                    if more:
                        more()
                    res_ready.wait(sp, i, T)
                    sp.dma_start(out[bass.ds(i, 1)].rearrange("o (t p) d -> p (o t) d", p=P),
                                 res[:]).then_inc(res_stored.sem, 16)

                batches(sp, body, front)
                sp.wait_ge(res_stored.sem, 16 * (B + 1))

            @block.gpsimd
            def _(pool):
                hb_ready.start(pool)
                pool.memset(exponent[:], -0.5).then_inc(set_ready.sem, 1)
                pool.wait_ge(set_ready.sem, 1)
                pool.wait_ge(small_in.sem, 32)
                pool.wait_ge(piece_lo.sem, PIECES)

                def front(i):
                    var_ready.wait(pool, i, T)
                    pool.tensor_tensor(rstd[:], mean_var[:, :, 1], exponent[:], ALU.pow).then_inc(rstd_ready.sem, 1)

                def sums(i):
                    h_in.wait(pool, i, 16)
                    res_ready.wait(pool, i, 0)
                    for t in range(T):
                        pool.tensor_tensor(hb[:, t, :], h[:, t, :], b2[:], ALU.add).then_inc(hb_ready.sem, 1)

                def body(i, more):
                    sums(i)
                    if more:
                        more()

                batches(pool, body, front)

            @block.scalar
            def _(act):
                gelu_ready.start(act)
                for n in range(PIECES):
                    act.wait_ge(piece_in[n % 2].sem, 16 * (n // 2 + 1))
                    act.activation(piece(n)[1][0], flat(stage[n % 2]), ACT.Copy).then_inc(piece_hi.sem, 1)
                act.wait_ge(small_in.sem, 32)

                def front(i):
                    for t in range(T):
                        xt_ready.wait(act, i, t + 1)
                        act.activation(xT[0][:, :, tile(t)], ps_x[t % 2][:].rearrange("p (c s) -> p c s", c=C),
                                       ACT.Copy).then_inc(xhi_ready.sem, 1)

                def body(i, more):
                    for c in range(HC):
                        up_ready.wait(act, i, c + 1)
                        glo_ready.wait(act, i, c + 1 - 2)
                        act.activation(g[:, c % 2, :], ps_h[c % 2][:], ACT.Gelu, bias=b1[:, c:c + 1]
                                       ).then_inc(gelu_ready.sem, 1)
                    if more:
                        more()

                batches(act, body, front)

            @block.vector
            def _(dve):
                var_ready.start(dve)
                xn_ready.start(dve)
                xlo_ready.start(dve)
                glo_ready.start(dve)
                res_ready.start(dve)
                for n in range(PIECES):
                    dve.wait_ge(piece_hi.sem, n + 1)
                    hi, lo = piece(n)[1]
                    dve.tensor_tensor(lo, flat(stage[n % 2]), hi.bitcast(F32), ALU.subtract).then_inc(piece_lo.sem, 1)

                def moments(i):
                    h_in.wait(dve, i, 16)
                    for t in range(T):
                        dve.bn_stats(stats[:, t, :], h[:, t, :]).then_inc(stats_ready.sem, 1)
                    stats_ready.wait(dve, i, T)
                    dve.sem_inc(passed.sem)
                    for t in range(T):
                        dve.bn_aggr(mean_var[:, t, :], stats[:, t, :]).then_inc(var_ready.sem, 1)

                def norms(i):
                    rstd_ready.wait(dve, i, 1)

                    def norm(t):
                        xt_ready.wait(dve, i, t + 1 - 2)
                        dve.tensor_scalar(xn[:, t % 2, :], h[:, t, :], mean_var[:, t, 0:1], rstd[:, t:t + 1],
                                          ALU.subtract, ALU.mult).then_inc(xn_ready.sem, 1)

                    def x_lo(t):
                        xhi_ready.wait(dve, i, t + 1)
                        dve.tensor_tensor(xT[1][:, :, tile(t)], ps_x[t % 2][:].rearrange("p (c s) -> p c s", c=C),
                                          xT[0][:, :, tile(t)].bitcast(F32), ALU.subtract).then_inc(xlo_ready.sem, 1)

                    norm(0)
                    norm(1)
                    x_lo(0)
                    norm(2)
                    x_lo(1)
                    norm(3)
                    x_lo(2)
                    x_lo(3)

                def front(i):
                    moments(i)
                    norms(i)

                def body(i, more):
                    for c in range(HC):
                        gelu_ready.wait(dve, i, c + 1)
                        down_ready.wait(dve, i, c + 1 - RING)
                        at = c % RING
                        dve.tensor_copy(gs[0][:, at, :], g[:, c % 2, :]).then_inc(ghi_ready.sem, 1)
                        ghi_ready.wait(dve, i, c + 1)
                        dve.tensor_tensor(gs[1][:, at, :], g[:, c % 2, :], gs[0][:, at, :].bitcast(F32),
                                          ALU.subtract).then_inc(glo_ready.sem, 1)
                    if more:
                        more()
                    res_stored.wait(dve, i, 0)
                    hb_ready.wait(dve, i, T)
                    down_ready.wait(dve, i, HC)
                    for t in range(T):
                        dve.tensor_tensor(res[:, t, :], ps_y[t][:], hb[:, t, :], ALU.add).then_inc(res_ready.sem, 1)

                batches(dve, body, front)

            @block.tensor
            def _(pe):
                xt_ready.start(pe)
                up_ready.start(pe)
                down_ready.start(pe)
                pe.wait_ge(piece_lo.sem, PIECES)

                def turn(i, t):
                    xn_ready.wait(pe, i, t + 1)
                    xlo_ready.wait(pe, i, t + 1 - 2)
                    for c in range(C):
                        last = pe.transpose(ps_x[t % 2][:, tile(c)], xn[:, t % 2, tile(c)], ident[:])
                    last.then_inc(xt_ready.sem, 1)

                def front(i):
                    for t in range(T):
                        turn(i, t)

                def up(i, c):
                    gelu_ready.wait(pe, i, c + 1 - 2)
                    for k in range(C):
                        last = product(pe, ps_h[c % 2][:], [w[:, k, tile(c)] for w in w1], [m[:, k, :] for m in xT],
                                       k == 0, k == C - 1)
                    last.then_inc(up_ready.sem, 1)

                def down(i, c):
                    glo_ready.wait(pe, i, c + 1)
                    for t in range(T):
                        if c == 0:
                            res_ready.wait(pe, i, t + 1 - T)
                        last = product(pe, ps_y[t][:], [m[:, c % RING, tile(t)] for m in gs], [w[:, c, :] for w in w2],
                                       c == 0, c == HC - 1)
                    last.then_inc(down_ready.sem, 1)

                def body(i, more):
                    xlo_ready.wait(pe, i, T)
                    for c in range(HC + LAG):
                        if c < HC:
                            up(i, c)
                        if c == HC and more:
                            down(i, c - LAG)
                            turn(i + 1, 0)
                            turn(i + 1, 1)
                        elif c == HC + 1 and more:
                            down(i, c - LAG)
                            turn(i + 1, 2)
                            turn(i + 1, 3)
                        elif c >= LAG:
                            down(i, c - LAG)

                batches(pe, body, front)


def program(nc, a, out):
    scr_of = lambda name, shape: nc.dram_tensor(name, shape, F32, kind="Internal").ap()
    scr = {"ids": scr_of("scr_ids", [B * S]), "h": scr_of("scr_h", [B, S, D]), "route": scr_of("scr_route", [B, NH, S]),
           "h2": scr_of("scr_h2", [B, S, D])}
    scr["ids2"] = scr["ids"].rearrange("(b s) -> b s", s=S)
    with ExitStack() as ctx:
        sb = lambda name, shape, dt=F32: ctx.enter_context(nc.sbuf_tensor(name, shape, dt))
        keep = {"ident": sb("ident", [P, P]), "iota": sb("iota", [P, KEEP]),
                "bqkv": sb("bqkv", [P, QKV]), "bo": sb("bo", [P, D]),
                "cos": sb("cos", [P, T, 2, HD]), "sin": sb("sin", [P, T, 2, HD]),
                "mean": sb("mean", [P, B * T]), "rstd": sb("rstd", [P, B * T]),
                "pos": sb("pos", [P, T, B * NH], mybir.dt.bfloat16),
                "wqkv": [sb("wqkv_hi", [P, C, QKV], F32R), sb("wqkv_lo", [P, C, QKV], F32R)],
                "wo": [sb("wo_hi", [P, C, D], F32R), sb("wo_lo", [P, C, D], F32R)]}
        embed_phase(nc, keep, a, scr)
        choose_phase(nc, keep, a, scr)
        attend_phase(nc, keep, scr)
    with ExitStack() as ctx:
        ident = ctx.enter_context(nc.sbuf_tensor("ident_f", [P, P], F32))
        set_ready = Event(ctx, nc, "ident_ready", 1)
        with nc.Block() as block:
            @block.gpsimd
            def _(pool):
                identity(pool, ident, set_ready)
        ffn_phase(nc, ident, a, scr, out)


def layout(inputs):
    get = lambda name: np.ascontiguousarray(np.asarray(inputs[name]))
    row = lambda name: get(name).reshape(1, -1)
    inv_freq = 1.0 / np.float32(1000000.0) ** (np.arange(0, HD, 2, dtype=np.float32) / np.float32(HD))
    angle = (np.arange(S, dtype=np.float32)[:, None] * inv_freq[None, :].astype(np.float32)).astype(np.float32)
    cos, sin = np.cos(angle), np.sin(angle)
    table = lambda halves: np.stack([np.concatenate(halves, -1) * k for k in (SCALE, 1.0)], 1).astype(np.float32)
    return {
        "x": get("x").reshape(B * T, P),
        "W": get("L0_tok_W"),
        "delta": np.ascontiguousarray(get("L0_tok_delta_values").reshape(D, NTRAIN).T),
        "token_indices": get("L0_tok_token_indices").reshape(NTRAIN, 1),
        "Wq": get("L0_attn_Wq"), "bq": row("L0_attn_bq"), "Wk": get("L0_attn_Wk"), "bk": row("L0_attn_bk"),
        "Wv": get("L0_attn_Wv"), "bv": row("L0_attn_bv"), "Wo": get("L0_attn_Wo"), "bo": row("L0_attn_bo"),
        "Wr": get("L0_attn_Wr"), "br": get("L0_attn_br").reshape(NH, 1),
        "w1": np.ascontiguousarray(get("L0_ffn_proj1").T), "b1": np.ascontiguousarray(get("L0_ffn_proj1_bias").reshape(HC, P).T),
        "w2": np.ascontiguousarray(get("L0_ffn_proj2").T), "b2": row("L0_ffn_proj2_bias"),
        "cos": table([cos, cos]), "sin": table([-sin, sin]),
    }


def kernel(**inputs):
    import concourse.bacc as bacc
    from concourse.bass_utils import run_bass_kernel_spmd

    nc = bacc.Bacc("TRN2", target_bir_lowering=False, num_devices=1)
    arrays = {f"in_{name}": array for name, array in layout(inputs).items()}
    a = {name[3:]: nc.dram_tensor(name, list(array.shape), mybir.dt.from_np(array.dtype), kind="ExternalInput").ap()
         for name, array in arrays.items()}
    out = nc.dram_tensor("out", [B, S, D], F32, kind="ExternalOutput").ap()
    program(nc, a, out)
    return run_bass_kernel_spmd(nc, [arrays], core_ids=[0]).results[0]["out"]
```

```python
from contextlib import ExitStack

import numpy as np

import concourse.bass as bass
from concourse import mybir

F32 = mybir.dt.float32
F32R = mybir.dt.float32r
I32 = mybir.dt.int32
ALU = mybir.AluOpType
ACT = mybir.ActivationFunctionType
AX = mybir.AxisListType

P = 128
B, S, D = 16, 512, 512
V = 32000
NTRAIN = 64
T = S // P
C = D // P
NH, NKV, HD = 16, 8, 32
KEEP = int(S * 0.4)
HALF = KEEP // 2
QKV = (NH + 2 * NKV) * HD
ROPE = (NH + NKV) * HD
SCALE = float(HD) ** -0.5
H = 2048
HC = H // P
EPS = 1e-5
GROUP = P // NH
NG = B // GROUP


class Event:

    def __init__(self, ctx, nc, name, per, base=0):
        self.sem, self.per, self.base = ctx.enter_context(nc.semaphore(name)), per, base

    def start(self, eng):
        if self.base:
            eng.sem_inc(self.sem, self.base)

    def wait(self, eng, i, n):
        assert n + self.base >= 1, "a wait that might be against zero"
        eng.wait_ge(self.sem, i * self.per + (n + self.base))


def product(pe, out, lhs, rhs, first, last):
    pe.matmul(out, lhs[0], rhs[0], start=first, stop=False, skip_group_check=True)
    pe.matmul(out, lhs[0], rhs[1], start=False, stop=False, skip_group_check=True)
    return pe.matmul(out, lhs[1], rhs[0], start=False, stop=last, skip_group_check=True)


def identity(pool, ident, set_ready):
    pool.memset(ident[:], 0.0).then_inc(set_ready.sem, 1)
    pool.wait_ge(set_ready.sem, 1)
    pool.affine_select(out=ident[:], in_=ident[:], compare_op=ALU.not_equal, fill=1.0,
                       base=0, pattern=[[-1, P]], channel_multiplier=1).then_inc(set_ready.sem, 1)


def embed_phase(nc, keep, a, scr):
    with ExitStack() as ctx:
        sb = lambda name, shape, dt=F32: ctx.enter_context(nc.sbuf_tensor(name, shape, dt))
        ev = lambda name, per=1, base=0: Event(ctx, nc, name, per, base)
        ids_i = sb("ids_i", [B * T, P], I32)
        ids_f = sb("ids_f", [B * T, P])
        ids_neg = sb("ids_neg", [B * T, P])
        id_col = sb("id_col", [P, B * T], I32)
        ids_now = sb("ids_now", [P, 2, T], I32)
        trained_i = sb("trained_i", [P, 1], I32)
        trained = sb("trained", [P, 1])
        trained_neg = sb("trained_neg", [P, 1])
        delta_raw = sb("delta_raw", [P, D])
        delta_hi = sb("delta_hi", [P, D])
        delta = sb("delta", [P, D], F32R)
        id_row = sb("id_row", [P, 2, S])
        onehot = sb("onehot", [P, 2, S], F32R)
        rows = sb("rows", [P, 2, T, D])
        h = sb("h0", [P, 2, T, D])
        stats = sb("stats", [P, T, 6])
        mean_var = sb("mean_var", [P, 2, T, 2])
        exponent = sb("exponent", [P, T])
        rstd = sb("rstd_now", [P, 2, T])
        shift = sb("shift_now", [P, 2, T])
        xn = sb("xn0", [P, T, D])
        xT = sb("xT0", [P, C, S])
        logit = sb("logit", [NH, B, S])
        br = sb("br", [NH, 1])
        wr = sb("wr", [P, C, NH])
        ps_delta = [ctx.enter_context(nc.psum_tensor(f"ps_delta{t}", [P, D], F32)) for t in range(T)]
        ps_xT = [ctx.enter_context(nc.psum_tensor(f"ps_xT0{n}", [P, C, P], F32)) for n in range(2)]
        ps_route = ctx.enter_context(nc.psum_tensor("ps_route", [NH, S], F32))
        ps_ids = ctx.enter_context(nc.psum_tensor("ps_ids", [P, B * T], F32))

        passed = ev("passed")
        ids_in = ev("ids_in")
        small_in = ev("small_in")
        biases_in = ev("biases_in")
        logits_moved = ev("logits_moved")
        made = ev("made")
        ids_ready = ev("ids_ready")
        ids_turned = ev("ids_turned")
        ids_stored = ev("ids_stored")
        id_col_ready = ev("id_col_ready")
        const_ready = ev("const_ready")
        row_in = [ev(f"row_in{m}", 8) for m in range(2)]
        onehot_ready = ev("onehot_ready", 1, 2)
        delta_ready = ev("delta_ready", T, T + 1)
        ids_now_ready = ev("ids_now_ready", 1)
        gathered = [[ev(f"gathered{m}{t}", 8) for t in range(T)] for m in range(2)]
        h_ready = ev("h_ready", T, T + 1)
        stats_ready = ev("stats_ready", T)
        var_ready = ev("var_ready", T, T)
        rstd_ready = ev("rstd_ready", 1)
        product_ready = ev("product_ready", 1)
        shift_ready = ev("shift_ready", 1)
        stats_kept = ev("stats_kept", 1, 2)
        h_stored = [ev(f"h_stored{m}", 8, 16) for m in range(2)]
        xn_ready = ev("xn_ready", T, T + 1)
        xT_ready = ev("xT_ready", T, T)
        copied = ev("copied", T, 2)
        route_ready = ev("route_ready", 1, 1)
        logit_ready = ev("logit_ready", 1, 1)

        def slot_before(stored, eng, i, m):
            stored[m].wait(eng, i, -8 * m)

        def batches(eng, front, body):
            front(0, 0)
            with eng.Fori(0, B // 2 - 1) as pair:
                body(pair * 2, 0, 2)
                body(pair * 2 + 1, 1, 2)
            body(B - 2, 0, 1)
            body(B - 1, 1, 0)

        with nc.Block() as block:
            @block.sync
            def _(sp):
                for m in range(2):
                    h_stored[m].start(sp)
                sp.dma_start(ids_i[:], a["x"]).then_inc(ids_in.sem, 16)
                for half in range(2):
                    at = slice(NTRAIN * half, NTRAIN * (half + 1))
                    sp.dma_start(trained_i[at, :], a["token_indices"]).then_inc(small_in.sem, 16)
                    sp.dma_start(delta_raw[at, :], a["delta"]).then_inc(small_in.sem, 16)
                sp.dma_start(br[:], a["br"]).then_inc(small_in.sem, 16)
                sp.dma_start(wr[:], a["Wr"].rearrange("(c p) n -> p c n", p=P)).then_inc(small_in.sem, 16)
                ids_ready.wait(sp, 0, 1)
                sp.dma_start(scr["ids"].rearrange("(t p) -> t p", p=P), ids_f[:]).then_inc(ids_stored.sem, 16)
                sp.wait_ge(ids_stored.sem, 16)

                def row(i, m):
                    onehot_ready.wait(sp, i, -1)
                    sp.dma_start(id_row[:, m, :], scr["ids2"][bass.ds(i, 1), :].to_broadcast([P, S])).then_inc(row_in[m].sem, 16)

                def front(i, m):
                    row(i, m)
                    row(i + 1, 1 - m)

                def body(i, m, more):
                    if more == 2:
                        row(i + 2, m)
                    h_ready.wait(sp, i, T)
                    sp.dma_start(scr["h"][bass.ds(i, 1)].rearrange("o (t p) d -> p (o t) d", p=P),
                                 h[:, m]).then_inc(h_stored[m].sem, 16)

                batches(sp, front, body)
                for n, (w, k) in enumerate((("bq", NH), ("bk", NKV), ("bv", NKV))):
                    at = (0, NH * HD, ROPE)[n]
                    sp.dma_start(keep["bqkv"][:, at:at + k * HD],
                                 a[w].to_broadcast([P, k * HD])).then_inc(biases_in.sem, 16)
                sp.dma_start(keep["bo"][:], a["bo"].to_broadcast([P, D])).then_inc(biases_in.sem, 16)
                sp.dma_start(keep["cos"][:], a["cos"].rearrange("(t p) k n -> p t k n", p=P)).then_inc(biases_in.sem, 16)
                sp.dma_start(keep["sin"][:], a["sin"].rearrange("(t p) k n -> p t k n", p=P)).then_inc(biases_in.sem, 16)
                logit_ready.wait(sp, B, 0)
                sp.dma_start(scr["route"].rearrange("b h s -> h b s"), logit[:]).then_inc(logits_moved.sem, 16)
                sp.wait_ge(logits_moved.sem, 16)
                sp.dma_start(keep["logit"][:], scr["route"].rearrange("(g b) h s -> (b h) g s", g=NG)
                             ).then_inc(logits_moved.sem, 16)
                sp.wait_ge(logits_moved.sem, 32)
                sp.wait_ge(biases_in.sem, 16 * 6)
                for m in range(2):
                    sp.wait_ge(h_stored[m].sem, 16 * (B // 2 + 1))

            @block.gpsimd
            def _(pool):
                stats_kept.start(pool)
                pool.memset(keep["ident"][:], 0.0).then_inc(const_ready.sem, 1)
                pool.memset(exponent[:], -0.5).then_inc(const_ready.sem, 1)
                pool.iota(keep["iota"][:], [[1, KEEP]], base=0, channel_multiplier=0,
                          allow_small_or_imprecise_dtypes=True).then_inc(const_ready.sem, 1)
                pool.wait_ge(const_ready.sem, 3)
                pool.affine_select(out=keep["ident"][:], in_=keep["ident"][:], compare_op=ALU.not_equal, fill=1.0,
                                   base=0, pattern=[[-1, P]], channel_multiplier=1).then_inc(const_ready.sem, 1)
                id_col_ready.wait(pool, 0, 1)

                def front(i, m):
                    h_ready.wait(pool, i, -T)
                    pool.tensor_copy(ids_now[:, m, :], id_col[:, bass.ds(i * T, T)]).then_inc(ids_now_ready.sem, 1)
                    ids_now_ready.wait(pool, i, 1)
                    pool.sem_inc(passed.sem)
                    for t in range(T):
                        pool.indirect_dma_start(out=rows[:, m, t, :], out_offset=None, in_=a["W"],
                                                in_offset=bass.IndirectOffsetOnAxis(ap=ids_now[:, m, t:t + 1], axis=0)
                                                ).then_inc(gathered[m][t].sem, 16)

                def body(i, m, more):
                    if more:
                        front(i + 1, 1 - m)
                    var_ready.wait(pool, i, T)
                    xn_ready.wait(pool, i, -T)
                    pool.tensor_tensor(rstd[:, m], mean_var[:, m, :, 1], exponent[:], ALU.pow).then_inc(rstd_ready.sem, 1)
                    rstd_ready.wait(pool, i, 1)
                    pool.tensor_tensor(shift[:, m], mean_var[:, m, :, 0], rstd[:, m], ALU.mult).then_inc(product_ready.sem, 1)
                    product_ready.wait(pool, i, 1)
                    pool.sem_inc(passed.sem)
                    pool.tensor_scalar(shift[:, m], shift[:, m], -1.0, None, ALU.mult).then_inc(shift_ready.sem, 1)
                    pool.tensor_copy(keep["rstd"][:, bass.ds(i * T, T)], rstd[:, m])
                    pool.tensor_copy(keep["mean"][:, bass.ds(i * T, T)], mean_var[:, m, :, 0]).then_inc(stats_kept.sem, 1)

                batches(pool, front, body)

            @block.vector
            def _(dve):
                steps = [0]

                def done(instruction):
                    steps[0] += 1
                    instruction.then_inc(made.sem, 1)
                    dve.wait_ge(made.sem, steps[0])

                onehot_ready.start(dve)
                h_ready.start(dve)
                var_ready.start(dve)
                for src, neg, out in ((ids_i, ids_neg, ids_f), (trained_i, trained_neg, trained)):
                    if src is ids_i:
                        dve.wait_ge(ids_in.sem, 16)
                    else:
                        dve.wait_ge(small_in.sem, 16 * 6)
                    done(dve.tensor_copy(out[:], src[:]))
                    done(dve.tensor_scalar(neg[:], out[:], 0.0, float(V), ALU.is_lt, ALU.mult))
                    done(dve.tensor_tensor(out[:], out[:], neg[:], ALU.add))
                    if src is ids_i:
                        dve.tensor_scalar(ids_f[:], ids_f[:], 0.0, float(V - 1), ALU.max, ALU.min).then_inc(ids_ready.sem, 1)
                        dve.wait_ge(ids_turned.sem, 1)
                        dve.tensor_copy(id_col[:], ps_ids[:]).then_inc(id_col_ready.sem, 1)
                done(dve.tensor_copy(delta_hi[:].bitcast(F32R), delta_raw[:]))
                dve.tensor_copy(delta[0:NTRAIN, :], delta_hi[0:NTRAIN, :])
                done(dve.tensor_tensor(delta[NTRAIN:P, :], delta_raw[NTRAIN:P, :], delta_hi[NTRAIN:P, :], ALU.subtract))

                def front(i, m):
                    row_in[m].wait(dve, i, 16 - 8 * m)
                    delta_ready.wait(dve, i, -T)
                    dve.tensor_scalar(onehot[:, m, :], id_row[:, m, :], trained[:, 0:1], None,
                                      ALU.is_equal).then_inc(onehot_ready.sem, 1)

                def body(i, m, more):
                    if more:
                        front(i + 1, 1 - m)
                    slot_before(h_stored, dve, i, m)
                    xn_ready.wait(dve, i, -T)
                    for t in range(T):
                        gathered[m][t].wait(dve, i, 16 - 8 * m)
                        delta_ready.wait(dve, i, t + 1)
                        dve.tensor_tensor(h[:, m, t, :], rows[:, m, t, :], ps_delta[t][:], ALU.add).then_inc(h_ready.sem, 1)
                    var_ready.wait(dve, i, 0)
                    for t in range(T):
                        h_ready.wait(dve, i, t + 1)
                        dve.bn_stats(stats[:, t, :], h[:, m, t, :]).then_inc(stats_ready.sem, 1)
                    stats_kept.wait(dve, i, -1)
                    stats_ready.wait(dve, i, T)
                    dve.sem_inc(passed.sem)
                    for t in range(T):
                        dve.bn_aggr(mean_var[:, m, t, :], stats[:, t, :]).then_inc(var_ready.sem, 1)

                batches(dve, front, body)

            @block.scalar
            def _(act):
                logit_ready.start(act)
                xn_ready.start(act)
                copied.start(act)
                act.wait_ge(small_in.sem, 16 * 6)

                def norm(i, m, t):
                    xT_ready.wait(act, i, t + 1 - T)
                    act.activation(xn[:, t, :], h[:, m, t, :], ACT.Identity, bias=shift[:, m, t:t + 1],
                                   scale=rstd[:, m, t:t + 1]).then_inc(xn_ready.sem, 1)

                def copy(i, t):
                    xT_ready.wait(act, i, t + 1)
                    act.activation(xT[:, :, P * t:P * (t + 1)], ps_xT[t % 2][:], ACT.Copy).then_inc(copied.sem, 1)

                def front(i, m):
                    shift_ready.wait(act, i, 1)
                    for t in range(T):
                        norm(i, m, t)

                def body(i, m, more):
                    route_ready.wait(act, i, 0)
                    for t in range(T):
                        copy(i, t)
                    if more:
                        front(i + 1, 1 - m)
                    route_ready.wait(act, i, 1)
                    act.activation(logit[:, bass.ds(i, 1), :].rearrange("h o s -> h (o s)"), ps_route[:], ACT.Identity, bias=br[:, 0:1]).then_inc(logit_ready.sem, 1)

                batches(act, front, body)

            @block.tensor
            def _(pe):
                xT_ready.start(pe)
                route_ready.start(pe)
                delta_ready.start(pe)
                pe.wait_ge(const_ready.sem, 4)
                ids_ready.wait(pe, 0, 1)
                pe.transpose(ps_ids[:], ids_f[:], keep["ident"][0:B * T, 0:B * T]).then_inc(ids_turned.sem, 1)
                pe.wait_ge(small_in.sem, 16 * 6)
                pe.wait_ge(made.sem, 6 + 2)

                def add_deltas(i, m):
                    onehot_ready.wait(pe, i, 1)
                    for t in range(T):
                        h_ready.wait(pe, i, t + 1 - T)
                        pe.matmul(ps_delta[t][:], onehot[:, m, P * t:P * (t + 1)], delta[:],
                                  start=True, stop=True).then_inc(delta_ready.sem, 1)

                def front(i, m):
                    add_deltas(i, m)
                    add_deltas(i + 1, 1 - m)

                def body(i, m, more):
                    for t in range(T):
                        xn_ready.wait(pe, i, t + 1)
                        copied.wait(pe, i, t + 1 - 2)
                        for c in range(C):
                            last = pe.transpose(ps_xT[t % 2][:, c, :], xn[:, t, P * c:P * (c + 1)],
                                                keep["ident"][:])
                        last.then_inc(xT_ready.sem, 1)
                    copied.wait(pe, i, T)
                    logit_ready.wait(pe, i, 0)
                    for c in range(C):
                        if c == C // 2 and more == 2:
                            add_deltas(i + 2, m)
                        last = pe.matmul(ps_route[:], wr[:, c, :], xT[:, c, :], start=(c == 0), stop=(c == C - 1))
                    last.then_inc(route_ready.sem, 1)

                batches(pe, front, body)


def choose_phase(nc, keep, a):
    with ExitStack() as ctx:
        sb = lambda name, shape, dt=F32: ctx.enter_context(nc.sbuf_tensor(name, shape, dt))
        ev = lambda name, per=1, base=0: Event(ctx, nc, name, per, base)
        ROUNDS = -(-KEEP // 8)
        REST = KEEP - 8 * (ROUNDS - 1)
        TAKEN, BEYOND = -1.0, 2.0
        logit = keep["logit"]
        score = sb("score", [P, NG, S + 8])
        best = sb("best", [P, NG, 8])
        one = sb("one", [P, S])
        chosen = sb("chosen", [P, NG, S])
        count = sb("count", [P, NG, S])
        wqkv_raw = sb("wqkv_raw", [P, C, QKV])
        wo_raw = sb("wo_raw", [P, C, D])
        ps_pos = [ctx.enter_context(nc.psum_tensor(f"ps_pos{g}", [P, T, P], F32)) for g in range(NG)]
        scored = ev("scored")
        made = ev("made2")
        place_ready = ev("place_ready")
        turned = ev("turned")
        weights_in = ev("weights_in")
        w_hi_ready = ev("w_hi_ready")
        w_lo_ready = ev("w_lo_ready")
        weights = ((wqkv_raw, *keep["wqkv"]), (wo_raw, *keep["wo"]))
        with nc.Block() as block:
            @block.sync
            def _(sp):
                for n, (w, k) in enumerate((("Wq", NH), ("Wk", NKV), ("Wv", NKV))):
                    at = (0, NH * HD, ROPE)[n]
                    sp.dma_start(wqkv_raw[:, :, at:at + k * HD],
                                 a[w].rearrange("(c p) n -> p c n", p=P)).then_inc(weights_in.sem, 16)
                sp.dma_start(wo_raw[:], a["Wo"].rearrange("(c p) n -> p c n", p=P)).then_inc(weights_in.sem, 16)

            @block.scalar
            def _(act):
                for g in range(NG):
                    act.activation(score[:, g, 0:S], logit[:, g, :], ACT.Sigmoid).then_inc(scored.sem, 1)
                act.wait_ge(weights_in.sem, 16 * 4)
                for raw, hi, lo in weights:
                    act.activation(hi[:], raw[:], ACT.Copy).then_inc(w_hi_ready.sem, 1)

            @block.gpsimd
            def _(pool):
                for n, (raw, hi, lo) in enumerate(weights):
                    pool.wait_ge(w_hi_ready.sem, n + 1)
                    pool.tensor_tensor(lo[:], raw[:], hi[:].bitcast(F32), ALU.subtract).then_inc(w_lo_ready.sem, 1)

            @block.vector
            def _(dve):
                steps = [0]

                def both(step):
                    for g in range(NG):
                        if steps[0] >= NG:
                            dve.wait_ge(made.sem, steps[0] - NG + 1)
                        step(g).then_inc(made.sem, 1)
                        steps[0] += 1

                dve.memset(one[:], 1.0)
                both(lambda g: dve.memset(score[:, g, S:S + 8], BEYOND))
                dve.wait_ge(scored.sem, NG)
                for r in range(ROUNDS):
                    width = S if r < ROUNDS - 1 else S + 8 - REST
                    both(lambda g: dve.max(best[:, g, :], score[:, g, 0:S]))
                    if width > S:
                        both(lambda g: dve.memset(best[:, g, REST:8], BEYOND))
                    both(lambda g: dve.match_replace(score[:, g, 0:width], best[:, g, :], score[:, g, 0:width], TAKEN))
                both(lambda g: dve.tensor_scalar(chosen[:, g, :], score[:, g, 0:S], 0.0, None, ALU.is_lt))
                both(lambda g: dve.tensor_tensor_scan(count[:, g, :], one[:], chosen[:, g, :], 0.0, ALU.mult, ALU.add))
                for g in range(NG):
                    dve.wait_ge(made.sem, steps[0] - NG + 1 + g)
                    dve.tensor_tensor(count[:, g, :], count[:, g, :], chosen[:, g, :],
                                      ALU.mult).then_inc(place_ready.sem, 1)
                for g in range(NG):
                    dve.wait_ge(turned.sem, g + 1)
                    dve.tensor_scalar(keep["pos"][:, :, P * g:P * (g + 1)], ps_pos[g][:], 1.0, None,
                                      ALU.subtract)

            @block.tensor
            def _(pe):
                for g in range(NG):
                    pe.wait_ge(place_ready.sem, g + 1)
                    for t in range(T):
                        last = pe.transpose(ps_pos[g][:, t, :], count[:, g, P * t:P * (t + 1)], keep["ident"][:])
                    last.then_inc(turned.sem, 1)


def attend_phase(nc, keep, scr):
    with ExitStack() as ctx:
        sb = lambda name, shape, dt=F32: ctx.enter_context(nc.sbuf_tensor(name, shape, dt))
        ps = lambda name: ctx.enter_context(nc.psum_tensor(name, [P, 512], F32))
        ev = lambda name, per=1, base=0: Event(ctx, nc, name, per, base)
        ident, wqkv, wo = keep["ident"], keep["wqkv"], keep["wo"]
        NP = NH // 2
        NQ = NH // 4
        h = sb("h_a", [P, T, D])
        h2 = sb("h2_a", [P, T, D])
        xT = [sb("xT_hi_a", [P, C, S], F32R), sb("xT_lo_a", [P, C, S], F32R)]
        aT = [sb("aT_hi", [P, C, S], F32R), sb("aT_lo", [P, C, S], F32R)]
        x = sb("x_a", [P, 2, QKV])
        turn1 = sb("turn1", [P, 2, ROPE])
        turn2 = sb("turn2", [P, 2, ROPE])
        xn = turn1[:, :, 0:D]
        q = sb("q_a", [P, T, NH * HD])
        kv = sb("kv_a", [P, T, NKV, 2, 2, HD], F32R)
        sel = sb("sel", [P, T, 2, KEEP], F32R)
        kT = sb("kT", [P, 2, 2 * KEEP], F32R)
        vT = sb("vT", [P, 2, 2 * KEEP])
        v = [sb(f"v{n}", [HALF, 2, 2, P], F32R) for n in range(4)]
        q4 = sb("q4", [P, 2, T, 4, HD])
        qT = sb("qT", [P, 2, S], F32R)
        prob = sb("prob", [P, 2, T, KEEP])
        pT = [sb("pT_hi", [HALF, 2, 2, S], F32R), sb("pT_lo", [HALF, 2, 2, S], F32R)]
        nmax = sb("nmax", [P, 2, T])
        mean_now = sb("mean_now_a", [P, T])
        rstd_now = sb("rstd_now_a", [P, T])
        total = sb("total", [P, NH, T])
        share = sb("share", [P, NH, T])
        oT = sb("oT", [P, S])
        attn = sb("attn", [P, T, P])
        ps_s = [ps("ps_s0"), ps("ps_s1")]
        ps_p = [ps("ps_p0"), ps("ps_p1")]
        ps_o, ps_k, ps_q, ps_m = ps("ps_o"), ps("ps_k"), ps("ps_q"), ps("ps_m")

        passed = ev("passed_a")
        v_zeroed = ev("v_zeroed")
        h_in = ev("h_in", 16)
        sum_ready = ev("sum_ready", T, T)
        xn_ready = ev("xn_ready_a", T, T)
        stats_now = ev("stats_now", 2)
        xt_ready = ev("xt_ready_a", T, 2)
        xhi_ready = ev("xhi_ready_a", T)
        xlo_ready = ev("xlo_ready_a", T, 2)
        qkv_ready = ev("qkv_ready", 2 * T)
        bias_ready = ev("bias_ready", 2 * T)
        turn1_ready = ev("turn1_ready", 2 * T)
        turn2_ready = ev("turn2_ready", T)
        q_ready = ev("q_ready", T, 2)
        k_turned = ev("k_turned", T)
        kvhi_ready = ev("kvhi_ready", T)
        kvlo_ready = ev("kvlo_ready", T, 2)
        sel_ready = ev("sel_ready", NP * T)
        picked = ev("picked", NP * T, T)
        kTa_ready = ev("kTa_ready", NP, 1)
        kTb_ready = ev("kTb_ready", NP)
        vT_ready = ev("vT_ready", NP, 1)
        vt_ready = ev("vt_ready", NP)
        v_ready = ev("v_ready", NH)
        q4hi_ready = ev("q4hi_ready", NH)
        q4_ready = ev("q4_ready", NH, 2)
        qt_ready = ev("qt_ready", NH, 2)
        qT_ready = ev("qT_ready", NH, 1)
        s_ready = ev("s_ready", 2 * NH)
        max_ready = ev("max_ready", 2 * NH)
        exp_ready = ev("exp_ready", T * NH, 1)
        pt_ready = ev("pt_ready", 2 * NH)
        phi_ready = ev("phi_ready", 2 * NH)
        plo_ready = ev("plo_ready", 2 * NH, 2)
        pv_ready = ev("pv_ready", NH, 4)
        oT_ready = ev("oT_ready", NQ)
        share_ready = ev("share_ready", NQ)
        ot_ready = ev("ot_ready", NQ)
        attn_ready = ev("attn_ready", NQ)
        at_ready = ev("at_ready", NQ)
        ahi_ready = ev("ahi_ready", NQ)
        alo_ready = ev("alo_ready", NQ, 1)
        proj_ready = ev("proj_ready", T)
        h2_ready = ev("h2_ready", T, T)
        h2_stored = ev("h2_stored", 16 * T, 16)

        tile = lambda t: slice(P * t, P * (t + 1))
        part = lambda s: slice(HALF * s, HALF * (s + 1))
        p_turned = lambda b: ps_p[b][0:HALF, :].rearrange("p (s q) -> p s q", s=2)

        kv_bank = [ps_k, ps_k, ps_s[0], ps_k]
        q_bank = [ps_q, ps_q, ps_s[1], ps_q]
        out_bank = [*ps_s, *ps_p]

        pair_at = {max(2 * g - 3, 0): g for g in range(1, NP)}
        turn_at = {6 + 2 * t: t for t in range(T)}

        out_at = {6: 0, 10: 1, 14: 2}
        back_at = {8: 0, 12: 1, 15: 2}

        misc = {("v", 0): (alo_ready, 0)}
        before = (v_ready, 2)
        for n in range(NH):
            if n % 2 and n + 1 < NH:
                misc["v", (n + 1) // 2] = before
                before = (v_ready, n + 3)
            if n in out_at:
                misc["out", out_at[n]] = before
                before = (attn_ready, out_at[n] + 1)
            if n in back_at:
                misc["back", back_at[n]] = before
                before = (alo_ready, back_at[n] + 1)
        misc["out", NQ - 1] = before
        misc["back", NQ - 1] = (attn_ready, NQ)

        def batches(eng, body, front):
            front(0)
            with eng.Fori(0, B - 1) as i:
                body(i, i + 1)
            body(B - 1, None)

        with nc.Block() as block:
            @block.sync
            def _(sp):
                h2_stored.start(sp)

                def front(j):
                    xn_ready.wait(sp, j, 0)
                    sum_ready.wait(sp, j, 0)
                    sp.dma_start(h[:], scr["h"][bass.ds(j, 1)].rearrange("o (t p) d -> p (o t) d", p=P)
                                 ).then_inc(h_in.sem, 16)

                def body(i, j):
                    if j is not None:
                        front(j)
                    for t in range(T):
                        h2_ready.wait(sp, i, t + 1)
                        sp.dma_start(scr["h2"][bass.ds(i, 1), tile(t), :].rearrange("o p d -> p (o d)"),
                                     h2[:, t, :]).then_inc(h2_stored.sem, 16)

                batches(sp, body, front)
                sp.wait_ge(h2_stored.sem, 16 * (B * T + 1))

            @block.gpsimd
            def _(pool):
                sum_ready.start(pool)
                xn_ready.start(pool)
                for n in range(4):
                    pool.memset(v[n][:].bitcast(F32), 0.0).then_inc(v_zeroed.sem, 1)
                q4_ready.start(pool)

                def norm(j, t, half):
                    if t == 0 and half == 0:
                        h_in.wait(pool, j, 16)
                        xn_ready.wait(pool, j, 0)
                        pool.sem_inc(passed.sem)
                        pool.tensor_copy(mean_now[:], keep["mean"][:, bass.ds(j * T, T)]).then_inc(stats_now.sem, 1)
                        pool.tensor_copy(rstd_now[:], keep["rstd"][:, bass.ds(j * T, T)]).then_inc(stats_now.sem, 1)
                        stats_now.wait(pool, j, 2)
                    if t < 2 and half == 0:
                        q_ready.wait(pool, j, 0)
                    if half == 0:
                        xt_ready.wait(pool, j, t + 1 - 2)
                        pool.sem_inc(passed.sem)
                    at = slice(D // 2 * half, D // 2 * (half + 1))
                    last = pool.tensor_scalar(xn[:, t % 2, at], h[:, t, at], mean_now[:, t:t + 1], rstd_now[:, t:t + 1],
                                              ALU.subtract, ALU.mult)
                    if half:
                        last.then_inc(xn_ready.sem, 1)

                def front(j):
                    for t in range(T):
                        norm(j, t, 0)
                        norm(j, t, 1)
                    rotations(j)
                    quads(j, 0)
                    quads(j, 1)

                def rotations(j):
                    for t in range(T):
                        bias_ready.wait(pool, j, 2 * (t + 1))
                        q_ready.wait(pool, j, t + 1 - 2)
                        for n, (lo, k) in enumerate(((0, NH), (NH, NKV))):
                            view = lambda m: (m[:, t % 2, HD * lo:HD * (lo + k)]
                                              .rearrange("p (h two d) -> p h two d", two=2, d=HD // 2))
                            for half in range(2):
                                sin = keep["sin"][:, t:t + 1, n, HD // 2 * half:HD // 2 * (half + 1)]
                                last = pool.tensor_tensor(view(turn2)[:, :, half, :], view(x)[:, :, 1 - half, :],
                                                          sin.to_broadcast([P, k, HD // 2]), ALU.mult)
                        last.then_inc(turn2_ready.sem, 1)
                    q_ready.wait(pool, j, T)

                def quads(i, hd):
                    qt_ready.wait(pool, i, hd + 1 - 2)
                    q4_ready.wait(pool, i, hd + 1 - 2)
                    src = q[:, :, HD * hd:HD * (hd + 1)].unsqueeze(2).to_broadcast([P, T, 2, HD])
                    pool.sem_inc(passed.sem)
                    pool.tensor_copy(q4[:, hd % 2, :, 0:2, :].bitcast(F32R), src).then_inc(q4hi_ready.sem, 1)
                    q4hi_ready.wait(pool, i, hd + 1)
                    pool.tensor_tensor(q4[:, hd % 2, :, 2:4, :], src, q4[:, hd % 2, :, 0:2, :],
                                       ALU.subtract).then_inc(q4_ready.sem, 1)

                def body(i, j):
                    for hd in range(2, NH):
                        quads(i, hd)
                        if hd == 3:
                            h_in.wait(pool, i, 16)
                            h2_stored.wait(pool, i, 0)
                        if 3 <= hd < 3 + T:
                            pool.tensor_tensor(h2[:, hd - 3, :], h[:, hd - 3, :], keep["bo"][:],
                                               ALU.add).then_inc(sum_ready.sem, 1)
                        if j is not None and 7 <= hd < 7 + 2 * T:
                            norm(j, (hd - 7) // 2, (hd - 7) % 2)
                    if j is not None:
                        rotations(j)
                        quads(j, 0)
                        quads(j, 1)

                batches(pool, body, front)

            @block.scalar
            def _(act):
                exp_ready.start(act)
                kTa_ready.start(act)
                vT_ready.start(act)
                qT_ready.start(act)

                def x_hi(j, t):
                    xt_ready.wait(act, j, t + 1)
                    act.activation(xT[0][:, :, tile(t)], ps_k[:].rearrange("p (c s) -> p c s", c=C),
                                   ACT.Copy).then_inc(xhi_ready.sem, 1)

                def kv_hi(j, t):
                    k_turned.wait(act, j, t + 1)
                    src = x[:, t % 2, NH * HD:QKV].rearrange("p (s g d) -> p s g d", s=2, d=HD)
                    act.activation(kv[:, t, :, :, 0, :].rearrange("p g s d -> p s g d"), src,
                                   ACT.Copy).then_inc(kvhi_ready.sem, 1)

                def k_rows(i, g):
                    picked.wait(act, i, T * (g + 1))
                    act.activation(vT[:, g % 2, :], ps_k[:, 0:2 * KEEP], ACT.Copy).then_inc(vT_ready.sem, 1)
                    act.activation(kT[0:64, g % 2, :], ps_k[0:64, 0:2 * KEEP], ACT.Copy).then_inc(kTa_ready.sem, 1)

                def q_rows(i, hd):
                    qt_ready.wait(act, i, hd + 1)
                    act.activation(qT[:, hd % 2, :], ps_q[:], ACT.Copy).then_inc(qT_ready.sem, 1)

                def exps(i, hd):
                    for s in range(2):
                        max_ready.wait(act, i, 2 * hd + s + 1)
                        for t in (2 * s, 2 * s + 1):
                            act.activation(prob[:, hd % 2, t, :], ps_s[s][:, KEEP * (t % 2):KEEP * (t % 2 + 1)],
                                           ACT.Exp, bias=nmax[:, hd % 2, t:t + 1],
                                           accum_out=total[:, hd, t:t + 1]).then_inc(exp_ready.sem, 1)

                def p_hi(i, hd):
                    pv_ready.wait(act, i, hd + 1 - 2)
                    for b in range(2):
                        pt_ready.wait(act, i, 2 * hd + b + 1)
                        act.activation(pT[0][:, hd % 2, :, 256 * b:256 * (b + 1)], p_turned(b),
                                       ACT.Copy).then_inc(phi_ready.sem, 1)

                def out_rows(i, c):
                    pv_ready.wait(act, i, 4 * (c + 1))
                    act.activation(oT[:], ps_o[:], ACT.Copy).then_inc(oT_ready.sem, 1)

                def a_hi(i, c):
                    at_ready.wait(act, i, c + 1)
                    act.activation(aT[0][:, c, :], ps_m[:], ACT.Copy).then_inc(ahi_ready.sem, 1)

                def front(j):
                    for t in range(T):
                        x_hi(j, t)
                    for t in range(T):
                        kv_hi(j, t)
                    opening(j)

                def opening(j):
                    q_rows(j, 0)
                    k_rows(j, 0)
                    q_rows(j, 1)
                    exps(j, 0)

                def body(i, j):
                    for n in range(NH):
                        p_hi(i, n)
                        if n % 2 and n + 2 < NH:
                            q_rows(i, n + 2)
                        if n + 1 < NH:
                            exps(i, n + 1)
                        if n % 2 == 0 and n + 2 < NH:
                            q_rows(i, n + 2)
                        if n in pair_at:
                            k_rows(i, pair_at[n])
                        if n >= 4 and n % 4 == 0:
                            out_rows(i, n // 4 - 1)
                        if n in back_at:
                            a_hi(i, back_at[n])
                        if j is not None:
                            if n in turn_at:
                                x_hi(j, turn_at[n])
                            if n == NH - 1:
                                kv_hi(j, 0)
                    out_rows(i, NQ - 1)
                    if j is not None:
                        kv_hi(j, 1)
                    a_hi(i, NQ - 1)
                    if j is not None:
                        kv_hi(j, 2)
                        kv_hi(j, 3)
                        opening(j)

                batches(act, body, front)

            @block.vector
            def _(dve):
                xlo_ready.start(dve)
                q_ready.start(dve)
                plo_ready.start(dve)
                kvlo_ready.start(dve)
                alo_ready.start(dve)
                h2_ready.start(dve)
                dve.wait_ge(v_zeroed.sem, 4)

                def x_lo(j, t):
                    xhi_ready.wait(dve, j, t + 1)
                    dve.tensor_tensor(xT[1][:, :, tile(t)], ps_k[:].rearrange("p (c s) -> p c s", c=C),
                                      xT[0][:, :, tile(t)].bitcast(F32), ALU.subtract).then_inc(xlo_ready.sem, 1)

                def biases(j, t, n):
                    kvlo_ready.wait(dve, j, t + 1 - 2)
                    qkv_ready.wait(dve, j, 2 * t + n + 1)
                    bank = (kv_bank, q_bank)[n][t]
                    lo, k = ((NH, NKV), (0, NH))[n]
                    at = slice(HD * lo, HD * lo + 512)
                    dve.tensor_tensor(x[:, t % 2, at], bank[:], keep["bqkv"][:, at], ALU.add).then_inc(bias_ready.sem, 1)
                    at = slice(HD * lo, HD * (lo + k))
                    bias_ready.wait(dve, j, 2 * t + n + 1)
                    dve.tensor_tensor(turn1[:, t % 2, at].rearrange("p (h d) -> p h d", d=HD),
                                      x[:, t % 2, at].rearrange("p (h d) -> p h d", d=HD),
                                      keep["cos"][:, t:t + 1, 1 - n, :].to_broadcast([P, k, HD]),
                                      ALU.mult).then_inc(turn1_ready.sem, 1)

                def rotated(j, t):
                    turn2_ready.wait(dve, j, t + 1)
                    turn1_ready.wait(dve, j, 2 * (t + 1))
                    q4_ready.wait(dve, j, 0)
                    at = slice(NH * HD, ROPE)
                    dve.tensor_tensor(x[:, t % 2, at], turn1[:, t % 2, at], turn2[:, t % 2, at],
                                      ALU.add).then_inc(k_turned.sem, 1)
                    at = slice(0, NH * HD)
                    dve.tensor_tensor(q[:, t, :], turn1[:, t % 2, at], turn2[:, t % 2, at],
                                      ALU.add).then_inc(q_ready.sem, 1)
                    kvhi_ready.wait(dve, j, t + 1)
                    k_turned.wait(dve, j, t + 1)
                    view = lambda z: kv[:, t, :, :, z, :].rearrange("p g s d -> p s g d")
                    dve.tensor_tensor(view(1), x[:, t % 2, NH * HD:QKV].rearrange("p (s g d) -> p s g d", s=2, d=HD),
                                      view(0).bitcast(F32), ALU.subtract).then_inc(kvlo_ready.sem, 1)

                def select(i, g, tiles):
                    for t in tiles:
                        picked.wait(dve, i, T * g + t + 1 - T)
                        for n in range(2):
                            last = dve.tensor_scalar(sel[:, t, n, :], keep["iota"][:],
                                                     keep["pos"][:, t, bass.ds(i * NH + 2 * g + n, 1)], None,
                                                     ALU.is_equal)
                        last.then_inc(sel_ready.sem, 1)

                def k_again(i, g):
                    vT_ready.wait(dve, i, g + 1)
                    dve.tensor_copy(kT[64:128, g % 2, :], vT[0:64, g % 2, :]).then_inc(kTb_ready.sem, 1)

                def v_cols(i, g):
                    vt_ready.wait(dve, i, g + 1)
                    for hd in (2 * g, 2 * g + 1):
                        n = hd % 4
                        pv_ready.wait(dve, i, hd + 1 - 4)
                        src = ps_m[0:HALF, 256 * (hd % 2):256 * (hd % 2) + 256].rearrange("p (s x) -> p s x", s=2)
                        dve.tensor_copy(v[n][:, :, :, HD * n:HD * (n + 1)],
                                        src[:, :, 64:128].rearrange("p s (l d) -> p s l d", l=2)
                                        ).then_inc(v_ready.sem, 1)

                def maxima(i, hd):
                    for s in range(2):
                        s_ready.wait(dve, i, 2 * hd + s + 1)
                        dve.tensor_reduce(nmax[:, hd % 2, 2 * s:2 * s + 2],
                                          ps_s[s][:, 0:2 * KEEP].rearrange("p (t k) -> p t k", t=2), AX.X,
                                          ALU.max, negate=True).then_inc(max_ready.sem, 1)

                def p_lo(i, hd):
                    for b in range(2):
                        phi_ready.wait(dve, i, 2 * hd + b + 1)
                        at = slice(256 * b, 256 * (b + 1))
                        dve.tensor_tensor(pT[1][:, hd % 2, :, at], p_turned(b), pT[0][:, hd % 2, :, at].bitcast(F32),
                                          ALU.subtract).then_inc(plo_ready.sem, 1)

                def shares(i, c):
                    exp_ready.wait(dve, i, 16 * (c + 1))
                    dve.reciprocal(share[:, 4 * c:4 * c + 4, :], total[:, 4 * c:4 * c + 4, :]).then_inc(share_ready.sem, 1)

                def normalised(i, c):
                    share_ready.wait(dve, i, c + 1)
                    ot_ready.wait(dve, i, c + 1)
                    dve.tensor_tensor(attn[:].rearrange("p t (n d) -> p t n d", n=4),
                                      ps_m[:].rearrange("p (t n d) -> p t n d", t=T, n=4),
                                      share[:, 4 * c:4 * c + 4, :].rearrange("p n t -> p t n").unsqueeze(3)
                                      .to_broadcast([P, T, 4, HD]), ALU.mult).then_inc(attn_ready.sem, 1)

                def a_lo(i, c):
                    ahi_ready.wait(dve, i, c + 1)
                    dve.tensor_tensor(aT[1][:, c, :], ps_m[:], aT[0][:, c, :].bitcast(F32),
                                      ALU.subtract).then_inc(alo_ready.sem, 1)

                def front(j):
                    for t in range(T):
                        x_lo(j, t)
                    for t in range(T):
                        biases(j, t, 0)
                        biases(j, t, 1)
                        if t:
                            rotated(j, t - 1)
                    rotated(j, T - 1)
                    select(j, 0, range(T))
                    k_again(j, 0)
                    v_cols(j, 0)
                    maxima(j, 0)
                    select(j, 1, range(T))

                def rows_out(i, t):
                    if t == 0:
                        sum_ready.wait(dve, i, T)
                    proj_ready.wait(dve, i, t + 1)
                    dve.tensor_tensor(h2[:, t, :], out_bank[t][:], h2[:, t, :], ALU.add).then_inc(h2_ready.sem, 1)

                def body(i, j):
                    for n in range(NH):
                        if n + 1 < NH:
                            maxima(i, n + 1)
                        if n == 1:
                            select(i, 2, (2, 3))
                        p_lo(i, n)
                        if n >= 4 and n % 4 == 0:
                            shares(i, n // 4 - 1)
                        if n % 2 and n + 1 < NH:
                            v_cols(i, (n + 1) // 2)
                        if n % 2 == 0 and n + 2 < NH:
                            k_again(i, n // 2 + 1)
                        if n in back_at:
                            a_lo(i, back_at[n])
                        if n in out_at:
                            normalised(i, out_at[n])
                        if n == 0:
                            select(i, 2, (0, 1))
                        elif n % 2 == 0 and n // 2 + 2 < NP:
                            select(i, n // 2 + 2, (2, 3))
                        elif n % 2 and (n + 5) // 2 < NP:
                            select(i, (n + 5) // 2, (0, 1))
                        if j is not None:
                            if n in turn_at:
                                x_lo(j, turn_at[n])
                            if n >= 14:
                                biases(j, n - 14, 0)
                                biases(j, n - 14, 1)
                    shares(i, NQ - 1)
                    if j is not None:
                        rotated(j, 0)
                        biases(j, 2, 0)
                    normalised(i, NQ - 1)
                    if j is not None:
                        biases(j, 2, 1)
                        rotated(j, 1)
                    a_lo(i, NQ - 1)
                    if j is not None:
                        biases(j, 3, 0)
                        biases(j, 3, 1)
                        rotated(j, 2)
                        rotated(j, 3)
                        select(j, 0, range(T))
                    rows_out(i, 0)
                    rows_out(i, 1)
                    if j is not None:
                        k_again(j, 0)
                        v_cols(j, 0)
                        maxima(j, 0)
                    rows_out(i, 2)
                    if j is not None:
                        select(j, 1, (0, 1))
                    rows_out(i, 3)
                    if j is not None:
                        select(j, 1, (2, 3))

                batches(dve, body, front)

            @block.tensor
            def _(pe):
                xt_ready.start(pe)
                picked.start(pe)
                qt_ready.start(pe)
                pv_ready.start(pe)
                def turn_x(j, t):
                    xn_ready.wait(pe, j, t + 1)
                    xlo_ready.wait(pe, j, t)
                    for c in range(C):
                        last = pe.transpose(ps_k[:, tile(c)], xn[:, t % 2, tile(c)], ident[:])
                    last.then_inc(xt_ready.sem, 1)

                def project(j, t, n):
                    xlo_ready.wait(pe, j, t + 1)
                    if t == 2:
                        exp_ready.wait(pe, j, 0)
                    elif t == 0:
                        (kTa_ready, qT_ready)[n].wait(pe, j, 0)
                        xlo_ready.wait(pe, j, T)
                    else:
                        bias_ready.wait(pe, j, 2 * (t // 2) + n + 1)
                    at = (slice(512, 1024), slice(0, 512))[n]
                    for c in range(C):
                        last = product(pe, (kv_bank, q_bank)[n][t][:], [m[:, c, tile(t)] for m in xT],
                                       [m[:, c, at] for m in wqkv], c == 0, c == C - 1)
                    last.then_inc(qkv_ready.sem, 1)

                def pick(i, j, g):
                    if g == 0:
                        kvlo_ready.wait(pe, i, T)
                    elif g >= 5 and j is not None:
                        xlo_ready.wait(pe, j, g - 4)
                    else:
                        kTa_ready.wait(pe, i, g)
                        vT_ready.wait(pe, i, g)
                    for t in range(T):
                        sel_ready.wait(pe, i, T * g + t + 1)
                        pe.matmul(ps_k[:, 0:2 * KEEP], kv[:, t, g, :, :, :].rearrange("p s l d -> p (s l d)"),
                                  sel[:, t, :, :].rearrange("p n k -> p (n k)"), start=(t == 0),
                                  stop=(t == T - 1)).then_inc(picked.sem, 1)

                def turn_v(i, g):
                    e, n = misc["v", g]
                    e.wait(pe, i, n)
                    vT_ready.wait(pe, i, g + 1)
                    for n in range(2):
                        for s in range(2):
                            at = 256 * n + 128 * s
                            last = pe.transpose(ps_m[0:HALF, at:at + P],
                                                vT[:, g % 2, KEEP * n + HALF * s:KEEP * n + HALF * (s + 1)], ident[:])
                    last.then_inc(vt_ready.sem, 1)

                def turn_q(i, hd):
                    if hd:
                        qT_ready.wait(pe, i, hd)
                    else:
                        bias_ready.wait(pe, i, 2 * T)
                    q4_ready.wait(pe, i, hd + 1)
                    for t in range(T):
                        last = pe.transpose(ps_q[:, tile(t)], q4[:, hd % 2, t, :, :].rearrange("p n d -> p (n d)"), ident[:])
                    last.then_inc(qt_ready.sem, 1)

                def scores(i, hd):
                    qT_ready.wait(pe, i, hd + 1)
                    kTa_ready.wait(pe, i, hd // 2 + 1)
                    kTb_ready.wait(pe, i, hd // 2 + 1)
                    for t in range(T):
                        if t % 2 == 0:
                            if hd:
                                exp_ready.wait(pe, i, T * (hd - 1) + t + 2)
                            else:
                                h2_ready.wait(pe, i, t // 2 + 1 - T)
                        mm = pe.matmul(ps_s[t // 2][:, KEEP * (t % 2):KEEP * (t % 2 + 1)], qT[:, hd % 2, tile(t)],
                                       kT[:, hd // 2 % 2, KEEP * (hd % 2):KEEP * (hd % 2 + 1)], start=True, stop=True)
                        if t % 2:
                            mm.then_inc(s_ready.sem, 1)

                def turn_p(i, hd):
                    for b in range(2):
                        exp_ready.wait(pe, i, T * hd + 2 * b + 2)
                        plo_ready.wait(pe, i, 2 * hd + b + 1 - 2)
                        if hd == 0:
                            h2_ready.wait(pe, i, b + 3 - T)
                        for s in range(2):
                            for t in range(2):
                                last = pe.transpose(p_turned(b)[:, s, tile(t)], prob[:, hd % 2, 2 * b + t, part(s)], ident[:])
                        last.then_inc(pt_ready.sem, 1)

                def values(i, hd):
                    n = hd % 4
                    v_ready.wait(pe, i, hd + 1)
                    plo_ready.wait(pe, i, 2 * hd + 2)
                    if n == 0 and hd:
                        oT_ready.wait(pe, i, hd // 4)
                    for s in range(2):
                        last = product(pe, ps_o[:], [v[n][:, s, l, :] for l in range(2)], [m[:, hd % 2, s, :] for m in pT],
                                       n == 0 and s == 0, n == 3 and s == 1)
                    last.then_inc(pv_ready.sem, 1)

                def turn_out(i, c):
                    e, n = misc["out", c]
                    e.wait(pe, i, n)
                    oT_ready.wait(pe, i, c + 1)
                    for t in range(T):
                        last = pe.transpose(ps_m[:, tile(t)], oT[:, tile(t)], ident[:])
                    last.then_inc(ot_ready.sem, 1)

                def turn_back(i, c):
                    e, n = misc["back", c]
                    e.wait(pe, i, n)
                    for t in range(T):
                        last = pe.transpose(ps_m[:, tile(t)], attn[:, t, :], ident[:])
                    last.then_inc(at_ready.sem, 1)

                def project_out(i, t):
                    for c in range(C):
                        last = product(pe, out_bank[t][:], [m[:, c, tile(t)] for m in aT],
                                       [m[:, c, :] for m in wo], c == 0, c == C - 1)
                    last.then_inc(proj_ready.sem, 1)

                def front(j):
                    for t in range(T):
                        turn_x(j, t)
                    for t in range(T):
                        project(j, t, 0)
                        project(j, t, 1)
                    opening(j)
                    opened(j)

                def opening(j):
                    turn_q(j, 0)
                    pick(j, None, 0)

                def opened(j):
                    turn_q(j, 1)
                    turn_v(j, 0)
                    scores(j, 0)

                def body(i, j):
                    for n in range(NH):
                        turn_p(i, n)
                        if n + 1 < NH:
                            scores(i, n + 1)
                        if n + 2 < NH:
                            turn_q(i, n + 2)
                        if n % 2 and n + 1 < NH:
                            turn_v(i, (n + 1) // 2)
                        if n in out_at:
                            turn_out(i, out_at[n])
                        if n in back_at:
                            turn_back(i, back_at[n])
                        if n:
                            values(i, n - 1)
                        if n in pair_at:
                            pick(i, j, pair_at[n])
                        if j is not None:
                            if n in turn_at:
                                kTa_ready.wait(pe, i, pair_at[n - 1] + 1)
                                vT_ready.wait(pe, i, pair_at[n - 1] + 1)
                                turn_x(j, turn_at[n])
                            if n >= 14:
                                project(j, n - 14, 0)
                                project(j, n - 14, 1)
                    values(i, NH - 1)
                    if j is not None:
                        project(j, 2, 0)
                    turn_out(i, NQ - 1)
                    if j is not None:
                        project(j, 2, 1)
                    turn_back(i, NQ - 1)
                    if j is not None:
                        project(j, 3, 0)
                        project(j, 3, 1)
                    alo_ready.wait(pe, i, NQ)
                    bias_ready.wait(pe, j if j is not None else i, 2 * T - 2 if j is not None else 2 * T)
                    project_out(i, 0)
                    project_out(i, 1)
                    if j is not None:
                        opening(j)
                    project_out(i, 2)
                    if j is not None:
                        opened(j)
                    project_out(i, 3)

                batches(pe, body, front)


def ffn_phase(nc, ident, a, scr, out):
    with ExitStack() as ctx:
        sb = lambda name, shape, dt=F32: ctx.enter_context(nc.sbuf_tensor(name, shape, dt))
        ps = lambda name: ctx.enter_context(nc.psum_tensor(name, [P, 512], F32))
        ev = lambda name, per=1, base=0: Event(ctx, nc, name, per, base)
        RING, LAG = 4, 3
        w1 = [sb("w1_hi", [P, C, H], F32R), sb("w1_lo", [P, C, H], F32R)]
        w2 = [sb("w2_hi", [P, HC, D], F32R), sb("w2_lo", [P, HC, D], F32R)]
        b1 = sb("b1", [P, HC])
        b2 = sb("b2", [P, D])
        h = sb("h_f", [P, T, D])
        hb = sb("hb_f", [P, T, D])
        res = sb("res", [P, T, D])
        stats = sb("stats_f", [P, T, 6])
        mean_var = sb("mean_var_f", [P, T, 2])
        exponent = sb("exponent_f", [P, T])
        unit = sb("unit", [P, 1, 1])
        rstd = sb("rstd_f", [P, T])
        xn = sb("xn_f", [P, 2, D])
        xT = [sb("xT_hi_f", [P, C, S], F32R), sb("xT_lo_f", [P, C, S], F32R)]
        g = sb("g", [P, 2, S])
        gs = [sb("g_hi", [P, RING, S], F32R), sb("g_lo", [P, RING, S], F32R)]
        ps_x = [ps("ps_x0"), ps("ps_x1")]
        ps_h = [ps("ps_h0"), ps("ps_h1")]
        ps_y = [ps(f"ps_y{t}") for t in range(T)]

        PIECES, EARLY = 16, 4
        piece_in = [ev("piece_in0", 16), ev("piece_in1", 16)]
        small_in = ev("small_in_f")
        piece_hi = ev("piece_hi")
        piece_lo = ev("piece_lo")
        late_hi = ev("late_hi")
        late_lo = ev("late_lo")
        set_ready = ev("set_ready")
        passed = ev("passed_f")
        h_in = ev("h_in_f", 16)
        stats_ready = ev("stats_ready_f", T)
        var_ready = ev("var_ready_f", T, T)
        rstd_ready = ev("rstd_ready_f", 1)
        hb_ready = ev("hb_ready_f", T, T)
        xn_ready = ev("xn_ready_f", T, T)
        xt_ready = ev("xt_ready_f", T, 2)
        xhi_ready = ev("xhi_ready_f", T)
        xlo_ready = ev("xlo_ready_f", T, 2)
        up_ready = ev("up_ready", HC, HC)
        gelu_ready = ev("gelu_ready", HC, 2)
        ghi_ready = ev("ghi_ready", HC)
        glo_ready = ev("glo_ready", HC, 2)
        down_ready = ev("down_ready", HC, RING)
        res_ready = ev("res_ready", T, T)
        res_stored = ev("res_stored", 16, 16)
        tile = lambda t: slice(P * t, P * (t + 1))

        def piece(n):
            quarter, kind, half = n // 4, n // 2 % 2, n % 2
            if kind == 0:
                at = (slice(None), slice(2 * half, 2 * half + 2), slice(H // 4 * quarter, H // 4 * (quarter + 1)))
                return a["w1"].rearrange("(c p) n -> p c n", p=P)[at], [w[at] for w in w1]
            at = (slice(None), slice(4 * quarter + 2 * half, 4 * quarter + 2 * half + 2))
            return a["w2"].rearrange("(c p) n -> p c n", p=P)[at], [w[at] for w in w2]

        stage = [res[:, 2 * n:2 * n + 2, :] for n in range(2)]

        def split_wait(eng, n):
            if n < EARLY:
                eng.wait_ge(piece_lo.sem, n + 1)
            else:
                eng.wait_ge(late_lo.sem, n + 1 - EARLY)

        def batches(eng, body, front, meanwhile=lambda: None):
            front(0)
            meanwhile()
            with eng.Fori(0, B - 1) as i:
                body(i, lambda: front(i + 1))
            body(B - 1, None)

        with nc.Block() as block:
            @block.sync
            def _(sp):
                res_stored.start(sp)
                sp.dma_start(b1[:], a["b1"]).then_inc(small_in.sem, 16)
                sp.dma_start(b2[:], a["b2"].to_broadcast([P, D])).then_inc(small_in.sem, 16)

                def front(i):
                    xn_ready.wait(sp, i, 0)
                    hb_ready.wait(sp, i, 0)
                    sp.dma_start(h[:], scr["h2"][bass.ds(i, 1)].rearrange("o (t p) d -> p (o t) d", p=P)
                                 ).then_inc(h_in.sem, 16)

                def weights():
                    for n in range(PIECES):
                        if n >= 2:
                            split_wait(sp, n - 2)
                        sp.dma_start(stage[n % 2], piece(n)[0]).then_inc(piece_in[n % 2].sem, 16)

                def body(i, more):
                    if more:
                        more()
                    res_ready.wait(sp, i, T)
                    sp.dma_start(out[bass.ds(i, 1)].rearrange("o (t p) d -> p (o t) d", p=P),
                                 res[:]).then_inc(res_stored.sem, 16)

                batches(sp, body, front, weights)
                sp.wait_ge(res_stored.sem, 16 * (B + 1))

            @block.gpsimd
            def _(pool):
                hb_ready.start(pool)
                pool.memset(exponent[:], -0.5).then_inc(set_ready.sem, 1)
                pool.memset(unit[:], 1.0).then_inc(set_ready.sem, 1)
                pool.wait_ge(set_ready.sem, 2)
                pool.wait_ge(small_in.sem, 32)

                def front(i):
                    var_ready.wait(pool, i, T)
                    pool.tensor_tensor(rstd[:], mean_var[:, :, 1], exponent[:], ALU.pow).then_inc(rstd_ready.sem, 1)

                def weights():
                    for n in range(EARLY, PIECES):
                        pool.wait_ge(piece_in[n % 2].sem, 16 * (n // 2 + 1))
                        hi, lo = piece(n)[1]
                        pool.tensor_tensor(hi, stage[n % 2], unit[:].to_broadcast([P, 2, D]), ALU.mult
                                           ).then_inc(late_hi.sem, 1)
                        pool.wait_ge(late_hi.sem, n + 1 - EARLY)
                        pool.tensor_tensor(lo, stage[n % 2], hi.bitcast(F32), ALU.subtract).then_inc(late_lo.sem, 1)

                def sums(i):
                    h_in.wait(pool, i, 16)
                    res_ready.wait(pool, i, 0)
                    for t in range(T):
                        pool.tensor_tensor(hb[:, t, :], h[:, t, :], b2[:], ALU.add).then_inc(hb_ready.sem, 1)

                def body(i, more):
                    sums(i)
                    if more:
                        more()

                batches(pool, body, front, weights)

            @block.scalar
            def _(act):
                gelu_ready.start(act)
                act.wait_ge(small_in.sem, 32)

                def front(i):
                    for t in range(T):
                        xt_ready.wait(act, i, t + 1)
                        act.activation(xT[0][:, :, tile(t)], ps_x[t % 2][:].rearrange("p (c s) -> p c s", c=C),
                                       ACT.Copy).then_inc(xhi_ready.sem, 1)

                def body(i, more):
                    for c in range(HC):
                        up_ready.wait(act, i, c + 1)
                        glo_ready.wait(act, i, c + 1 - 2)
                        act.activation(g[:, c % 2, :], ps_h[c % 2][:], ACT.Gelu, bias=b1[:, c:c + 1]
                                       ).then_inc(gelu_ready.sem, 1)
                    if more:
                        more()

                def weights():
                    for n in range(EARLY):
                        act.wait_ge(piece_in[n % 2].sem, 16 * (n // 2 + 1))
                        act.activation(piece(n)[1][0], stage[n % 2], ACT.Copy).then_inc(piece_hi.sem, 1)

                batches(act, body, front, weights)

            @block.vector
            def _(dve):
                var_ready.start(dve)
                xn_ready.start(dve)
                xlo_ready.start(dve)
                glo_ready.start(dve)
                res_ready.start(dve)

                def moments(i):
                    h_in.wait(dve, i, 16)
                    for t in range(T):
                        dve.bn_stats(stats[:, t, :], h[:, t, :]).then_inc(stats_ready.sem, 1)
                    stats_ready.wait(dve, i, T)
                    dve.sem_inc(passed.sem)
                    for t in range(T):
                        dve.bn_aggr(mean_var[:, t, :], stats[:, t, :]).then_inc(var_ready.sem, 1)

                def norms(i):
                    rstd_ready.wait(dve, i, 1)

                    def norm(t):
                        xt_ready.wait(dve, i, t + 1 - 2)
                        dve.tensor_scalar(xn[:, t % 2, :], h[:, t, :], mean_var[:, t, 0:1], rstd[:, t:t + 1],
                                          ALU.subtract, ALU.mult).then_inc(xn_ready.sem, 1)

                    def x_lo(t):
                        xhi_ready.wait(dve, i, t + 1)
                        dve.tensor_tensor(xT[1][:, :, tile(t)], ps_x[t % 2][:].rearrange("p (c s) -> p c s", c=C),
                                          xT[0][:, :, tile(t)].bitcast(F32), ALU.subtract).then_inc(xlo_ready.sem, 1)

                    norm(0)
                    norm(1)
                    x_lo(0)
                    norm(2)
                    x_lo(1)
                    norm(3)
                    x_lo(2)
                    x_lo(3)

                def front(i):
                    moments(i)
                    norms(i)

                def body(i, more):
                    for c in range(HC):
                        gelu_ready.wait(dve, i, c + 1)
                        down_ready.wait(dve, i, c + 1 - RING)
                        at = c % RING
                        dve.tensor_copy(gs[0][:, at, :], g[:, c % 2, :]).then_inc(ghi_ready.sem, 1)
                        ghi_ready.wait(dve, i, c + 1)
                        dve.tensor_tensor(gs[1][:, at, :], g[:, c % 2, :], gs[0][:, at, :].bitcast(F32),
                                          ALU.subtract).then_inc(glo_ready.sem, 1)
                        if c == HC - 5 and more:
                            moments(i + 1)
                    if more:
                        norms(i + 1)
                    res_stored.wait(dve, i, 0)
                    split_wait(dve, PIECES - 1)
                    hb_ready.wait(dve, i, T)
                    down_ready.wait(dve, i, HC)
                    for t in range(T):
                        dve.tensor_tensor(res[:, t, :], ps_y[t][:], hb[:, t, :], ALU.add).then_inc(res_ready.sem, 1)

                def weights():
                    for n in range(EARLY):
                        dve.wait_ge(piece_hi.sem, n + 1)
                        hi, lo = piece(n)[1]
                        dve.tensor_tensor(lo, stage[n % 2], hi.bitcast(F32), ALU.subtract).then_inc(piece_lo.sem, 1)

                batches(dve, body, front, weights)

            @block.tensor
            def _(pe):
                xt_ready.start(pe)
                up_ready.start(pe)
                down_ready.start(pe)

                def turn(i, t):
                    xn_ready.wait(pe, i, t + 1)
                    xlo_ready.wait(pe, i, t + 1 - 2)
                    for c in range(C):
                        last = pe.transpose(ps_x[t % 2][:, tile(c)], xn[:, t % 2, tile(c)], ident[:])
                    last.then_inc(xt_ready.sem, 1)

                def front(i):
                    for t in range(T):
                        turn(i, t)

                def up(i, c):
                    gelu_ready.wait(pe, i, c + 1 - 2)
                    if c % 4 == 0:
                        split_wait(pe, c + 1)
                    for k in range(C):
                        last = product(pe, ps_h[c % 2][:], [w[:, k, tile(c)] for w in w1], [m[:, k, :] for m in xT],
                                       k == 0, k == C - 1)
                    last.then_inc(up_ready.sem, 1)

                def down(i, c):
                    glo_ready.wait(pe, i, c + 1)
                    if c % 4 == 0:
                        split_wait(pe, c + 3)
                    for t in range(T):
                        if c == 0:
                            res_ready.wait(pe, i, t + 1 - T)
                        last = product(pe, ps_y[t][:], [m[:, c % RING, tile(t)] for m in gs], [w[:, c, :] for w in w2],
                                       c == 0, c == HC - 1)
                    last.then_inc(down_ready.sem, 1)

                def body(i, more):
                    xlo_ready.wait(pe, i, T)
                    for c in range(HC + LAG):
                        if c < HC:
                            up(i, c)
                        if c == HC and more:
                            down(i, c - LAG)
                            turn(i + 1, 0)
                            turn(i + 1, 1)
                        elif c == HC + 1 and more:
                            down(i, c - LAG)
                            turn(i + 1, 2)
                            turn(i + 1, 3)
                        elif c >= LAG:
                            down(i, c - LAG)

                batches(pe, body, front)


def program(nc, a, out):
    scr_of = lambda name, shape: nc.dram_tensor(name, shape, F32, kind="Internal").ap()
    scr = {"ids": scr_of("scr_ids", [B * S]), "h": scr_of("scr_h", [B, S, D]), "route": scr_of("scr_route", [B, NH, S]),
           "h2": scr_of("scr_h2", [B, S, D])}
    scr["ids2"] = scr["ids"].rearrange("(b s) -> b s", s=S)
    with ExitStack() as ctx:
        sb = lambda name, shape, dt=F32: ctx.enter_context(nc.sbuf_tensor(name, shape, dt))
        keep = {"ident": sb("ident", [P, P]), "iota": sb("iota", [P, KEEP]),
                "bqkv": sb("bqkv", [P, QKV]), "bo": sb("bo", [P, D]),
                "cos": sb("cos", [P, T, 2, HD]), "sin": sb("sin", [P, T, 2, HD]),
                "mean": sb("mean", [P, B * T]), "rstd": sb("rstd", [P, B * T]),
                "pos": sb("pos", [P, T, B * NH], mybir.dt.bfloat16),
                "wqkv": [sb("wqkv_hi", [P, C, QKV], F32R), sb("wqkv_lo", [P, C, QKV], F32R)],
                "wo": [sb("wo_hi", [P, C, D], F32R), sb("wo_lo", [P, C, D], F32R)]}
        with nc.sbuf_tensor("logits", [P, NG, S], F32) as keep["logit"]:
            embed_phase(nc, keep, a, scr)
            choose_phase(nc, keep, a)
        attend_phase(nc, keep, scr)
    with ExitStack() as ctx:
        ident = ctx.enter_context(nc.sbuf_tensor("ident_f", [P, P], F32))
        set_ready = Event(ctx, nc, "ident_ready", 1)
        with nc.Block() as block:
            @block.gpsimd
            def _(pool):
                identity(pool, ident, set_ready)
        ffn_phase(nc, ident, a, scr, out)


def layout(inputs):
    get = lambda name: np.ascontiguousarray(np.asarray(inputs[name]))
    row = lambda name: get(name).reshape(1, -1)
    inv_freq = 1.0 / np.float32(1000000.0) ** (np.arange(0, HD, 2, dtype=np.float32) / np.float32(HD))
    angle = (np.arange(S, dtype=np.float32)[:, None] * inv_freq[None, :].astype(np.float32)).astype(np.float32)
    cos, sin = np.cos(angle), np.sin(angle)
    table = lambda halves: np.stack([np.concatenate(halves, -1) * k for k in (SCALE, 1.0)], 1).astype(np.float32)
    return {
        "x": get("x").reshape(B * T, P),
        "W": get("L0_tok_W"),
        "delta": np.ascontiguousarray(get("L0_tok_delta_values").reshape(D, NTRAIN).T),
        "token_indices": get("L0_tok_token_indices").reshape(NTRAIN, 1),
        "Wq": get("L0_attn_Wq"), "bq": row("L0_attn_bq"), "Wk": get("L0_attn_Wk"), "bk": row("L0_attn_bk"),
        "Wv": get("L0_attn_Wv"), "bv": row("L0_attn_bv"), "Wo": get("L0_attn_Wo"), "bo": row("L0_attn_bo"),
        "Wr": get("L0_attn_Wr"), "br": get("L0_attn_br").reshape(NH, 1),
        "w1": np.ascontiguousarray(get("L0_ffn_proj1").T), "b1": np.ascontiguousarray(get("L0_ffn_proj1_bias").reshape(HC, P).T),
        "w2": np.ascontiguousarray(get("L0_ffn_proj2").T), "b2": row("L0_ffn_proj2_bias"),
        "cos": table([cos, cos]), "sin": table([-sin, sin]),
    }


def kernel(**inputs):
    import concourse.bacc as bacc
    from concourse.bass_utils import run_bass_kernel_spmd

    nc = bacc.Bacc("TRN2", target_bir_lowering=False, num_devices=1)
    arrays = {f"in_{name}": array for name, array in layout(inputs).items()}
    a = {name[3:]: nc.dram_tensor(name, list(array.shape), mybir.dt.from_np(array.dtype), kind="ExternalInput").ap()
         for name, array in arrays.items()}
    out = nc.dram_tensor("out", [B, S, D], F32, kind="ExternalOutput").ap()
    program(nc, a, out)
    return run_bass_kernel_spmd(nc, [arrays], core_ids=[0]).results[0]["out"]
```
